# Optimizing a Trainium2 kernel written in Bass

```python
import numpy as np
import jax
import jax.numpy as jnp

def _softmax(x, axis=-1):
    return jax.nn.softmax(x, axis=axis)

def _gelu(x):
    return jax.nn.gelu(x, approximate=True)

def _silu(x):
    return jax.nn.silu(x)

def _sigmoid(x):
    return jax.nn.sigmoid(x)

def _layernorm(x, axis=-1, eps=1e-05):
    m = jnp.mean(x, axis=axis, keepdims=True)
    v = jnp.var(x, axis=axis, keepdims=True)
    return (x - m) / jnp.sqrt(v + eps)

def _scatter_add(tgt, idx, src, axis=0):
    return tgt.at[idx].add(src)

def _segment_sum(src, seg, n):
    return jax.ops.segment_sum(src, seg, n)
kernel_name = 'mk_xattn_seq_d2_seqx_r8_c29cec'

def setup_inputs(seed: int=0):
    np.random.seed(seed)
    _w = jnp.asarray

    def _rec_inputs():
        import jax
        import jax.numpy as jnp
        _rk = jax.random.key(seed)
        x = -0.0001548 + 1 * jax.random.normal(jax.random.fold_in(_rk, 1), (8, 256, 160), jnp.float32)
        _lenS = 256 - jax.random.randint(jax.random.fold_in(_rk, 7), (8,), 0, max(1, 256 // 4) + 1, jnp.int32)
        _lenS2 = 512 - jax.random.randint(jax.random.fold_in(_rk, 8), (8,), 0, max(1, 512 // 4) + 1, jnp.int32)
        _ctx_768P = jax.random.normal(jax.random.fold_in(_rk, 11), (8, 16, 96), jnp.float32)
        _ctx_768c = jax.random.dirichlet(jax.random.fold_in(_rk, 511), 0.3 * jnp.ones((16,), jnp.float32), (8, 512))
        _ctx_768t = jnp.einsum('bsk,bkd->bsd', _ctx_768c, _ctx_768P)
        _ctx_768t = _ctx_768t * jax.lax.rsqrt(jnp.mean(jnp.square(_ctx_768t)) + 1e-12) * 0.953939
        ctx_768 = 0.00141353 + 0.998943 * (_ctx_768t + 0.3 * jax.random.normal(jax.random.fold_in(_rk, 611), (8, 512, 96), jnp.float32))
        return (x, ctx_768)
    x, ctx_768 = _rec_inputs()

    def _L0_xattn_setup():
        import jax, jax.numpy as jnp
        import numpy as np
        HEADS = 8
        NUM_TOKENS = 4
        CROSS_ATTENTION_DIM = 96

        def _mha(q, k, v, heads=HEADS):
            B, Sq, H = q.shape
            Sk = k.shape[1]
            d = H // heads
            qh = q.reshape(B, Sq, heads, d).transpose(0, 2, 1, 3)
            kh = k.reshape(B, Sk, heads, d).transpose(0, 2, 1, 3)
            vh = v.reshape(B, Sk, heads, d).transpose(0, 2, 1, 3)
            scores = jnp.einsum('bhqd,bhkd->bhqk', qh, kh) * jnp.asarray(d, q.dtype) ** (-0.5)
            probs = jax.nn.softmax(scores, axis=-1)
            out = jnp.einsum('bhqk,bhkd->bhqd', probs, vh)
            return out.transpose(0, 2, 1, 3).reshape(B, Sq, H)
        key = jax.random.key(seed)
        ks = jax.random.split(key, 10)
        B, S, H, CAD, T = (4, 128, 160, CROSS_ATTENTION_DIM, NUM_TOKENS)
        sc = 0.02
        return {'hidden_states': jax.random.normal(ks[0], (B, S, H), jnp.float32), 'encoder_hidden_states': jax.random.normal(ks[1], (B, 77 + T, CAD), jnp.float32), 'Wq': jax.random.normal(ks[2], (H, H), jnp.float32) * sc, 'Wk': jax.random.normal(ks[3], (CAD, H), jnp.float32) * sc, 'Wv': jax.random.normal(ks[4], (CAD, H), jnp.float32) * sc, 'Wq_ca': jax.random.normal(ks[5], (T, H), jnp.float32) * sc, 'Wk_ca': jax.random.normal(ks[6], (CAD, H), jnp.float32) * sc, 'Wv_ca': jax.random.normal(ks[7], (CAD, H), jnp.float32) * sc, 'Wout': jax.random.normal(ks[8], (H, H), jnp.float32) * sc, 'b_out': jnp.zeros((H,), jnp.float32)}
    _L0_xattn_all = _L0_xattn_setup()
    _L0_xattn_in = {k: v for k, v in _L0_xattn_all.items() if k in ('Wq', 'Wk', 'Wv', 'Wq_ca', 'Wk_ca', 'Wv_ca', 'Wout', 'b_out')}
    del _L0_xattn_all

    def _L1_xattn_setup():
        import jax, jax.numpy as jnp
        import numpy as np
        DIM, HEADS, DHEAD, CTX_DIM, DFF = (160, 20, 64, 96, 640)
        EPS = 1e-05
        SCALE = DHEAD ** (-0.5)

        def layer_norm(x, g, b):
            mu = jnp.mean(x, axis=-1, keepdims=True)
            var = jnp.mean(jnp.square(x - mu), axis=-1, keepdims=True)
            return (x - mu) * jax.lax.rsqrt(var + EPS) * g + b

        def cross_attention(x, ctx, wq, wk, wv, wo, bo):
            B, N, _ = x.shape
            M = ctx.shape[1]
            q = jnp.einsum('bne,ef->bnf', x, wq).reshape(B, N, HEADS, DHEAD).transpose(0, 2, 1, 3)
            k = jnp.einsum('bme,ef->bmf', ctx, wk).reshape(B, M, HEADS, DHEAD).transpose(0, 2, 1, 3)
            v = jnp.einsum('bme,ef->bmf', ctx, wv).reshape(B, M, HEADS, DHEAD).transpose(0, 2, 1, 3)
            scores = jnp.einsum('bhnd,bhmd->bhnm', q, k) * SCALE
            attn = jax.nn.softmax(scores, axis=-1)
            out = jnp.einsum('bhnm,bhmd->bhnd', attn, v)
            out = out.transpose(0, 2, 1, 3).reshape(B, N, HEADS * DHEAD)
            return jnp.einsum('bnf,fe->bne', out, wo) + bo

        def geglu_ff(x, w1, b1, w2, b2):
            h = jnp.einsum('bne,ef->bnf', x, w1) + b1
            a, gate = (h[..., :DFF], h[..., DFF:])
            h = a * jax.nn.gelu(gate)
            return jnp.einsum('bnf,fe->bne', h, w2) + b2

        def block_forward(x, context, g1, be1, wq1, wk1, wv1, wo1, bo1, g2, be2, wq2, wk2, wv2, wo2, bo2, g3, be3, w_ff1, b_ff1, w_ff2, b_ff2):
            x = cross_attention(layer_norm(x, g1, be1), layer_norm(x, g1, be1), wq1, wk1, wv1, wo1, bo1) + x
            x = cross_attention(layer_norm(x, g2, be2), context, wq2, wk2, wv2, wo2, bo2) + x
            return geglu_ff(layer_norm(x, g3, be3), w_ff1, b_ff1, w_ff2, b_ff2) + x
        key = jax.random.key(seed)
        ks = jax.random.split(key, 20)
        s = 0.02
        inner = HEADS * DHEAD
        return {'x': jax.random.normal(ks[0], (4, 128, DIM), jnp.float32), 'context': jax.random.normal(ks[1], (4, 77, CTX_DIM), jnp.float32), 'g1': jnp.ones((DIM,), jnp.float32), 'be1': jnp.zeros((DIM,), jnp.float32), 'wq1': jax.random.normal(ks[2], (DIM, inner), jnp.float32) * s, 'wk1': jax.random.normal(ks[3], (DIM, inner), jnp.float32) * s, 'wv1': jax.random.normal(ks[4], (DIM, inner), jnp.float32) * s, 'wo1': jax.random.normal(ks[5], (inner, DIM), jnp.float32) * s, 'bo1': jnp.zeros((DIM,), jnp.float32), 'g2': jnp.ones((DIM,), jnp.float32), 'be2': jnp.zeros((DIM,), jnp.float32), 'wq2': jax.random.normal(ks[6], (DIM, inner), jnp.float32) * s, 'wk2': jax.random.normal(ks[7], (CTX_DIM, inner), jnp.float32) * s, 'wv2': jax.random.normal(ks[8], (CTX_DIM, inner), jnp.float32) * s, 'wo2': jax.random.normal(ks[9], (inner, DIM), jnp.float32) * s, 'bo2': jnp.zeros((DIM,), jnp.float32), 'g3': jnp.ones((DIM,), jnp.float32), 'be3': jnp.zeros((DIM,), jnp.float32), 'w_ff1': jax.random.normal(ks[10], (DIM, 2 * DFF), jnp.float32) * s, 'b_ff1': jnp.zeros((2 * DFF,), jnp.float32), 'w_ff2': jax.random.normal(ks[11], (DFF, DIM), jnp.float32) * s, 'b_ff2': jnp.zeros((DIM,), jnp.float32)}
    _L1_xattn_all = _L1_xattn_setup()
    _L1_xattn_in = {k: v for k, v in _L1_xattn_all.items() if k in ('g1', 'be1', 'wq1', 'wk1', 'wv1', 'wo1', 'bo1', 'g2', 'be2', 'wq2', 'wk2', 'wv2', 'wo2', 'bo2', 'g3', 'be3', 'w_ff1', 'b_ff1', 'w_ff2', 'b_ff2')}
    del _L1_xattn_all
    return {'x': x, 'ctx_768': ctx_768, 'L0_xattn_Wq': _L0_xattn_in['Wq'], 'L0_xattn_Wk': _L0_xattn_in['Wk'], 'L0_xattn_Wv': _L0_xattn_in['Wv'], 'L0_xattn_Wq_ca': _L0_xattn_in['Wq_ca'], 'L0_xattn_Wk_ca': _L0_xattn_in['Wk_ca'], 'L0_xattn_Wv_ca': _L0_xattn_in['Wv_ca'], 'L0_xattn_Wout': _L0_xattn_in['Wout'], 'L0_xattn_b_out': _L0_xattn_in['b_out'], 'L1_xattn_g1': _L1_xattn_in['g1'], 'L1_xattn_be1': _L1_xattn_in['be1'], 'L1_xattn_wq1': _L1_xattn_in['wq1'], 'L1_xattn_wk1': _L1_xattn_in['wk1'], 'L1_xattn_wv1': _L1_xattn_in['wv1'], 'L1_xattn_wo1': _L1_xattn_in['wo1'], 'L1_xattn_bo1': _L1_xattn_in['bo1'], 'L1_xattn_g2': _L1_xattn_in['g2'], 'L1_xattn_be2': _L1_xattn_in['be2'], 'L1_xattn_wq2': _L1_xattn_in['wq2'], 'L1_xattn_wk2': _L1_xattn_in['wk2'], 'L1_xattn_wv2': _L1_xattn_in['wv2'], 'L1_xattn_wo2': _L1_xattn_in['wo2'], 'L1_xattn_bo2': _L1_xattn_in['bo2'], 'L1_xattn_g3': _L1_xattn_in['g3'], 'L1_xattn_be3': _L1_xattn_in['be3'], 'L1_xattn_w_ff1': _L1_xattn_in['w_ff1'], 'L1_xattn_b_ff1': _L1_xattn_in['b_ff1'], 'L1_xattn_w_ff2': _L1_xattn_in['w_ff2'], 'L1_xattn_b_ff2': _L1_xattn_in['b_ff2']}

def reference(x, ctx_768, L0_xattn_Wq, L0_xattn_Wk, L0_xattn_Wv, L0_xattn_Wq_ca, L0_xattn_Wk_ca, L0_xattn_Wv_ca, L0_xattn_Wout, L0_xattn_b_out, L1_xattn_g1, L1_xattn_be1, L1_xattn_wq1, L1_xattn_wk1, L1_xattn_wv1, L1_xattn_wo1, L1_xattn_bo1, L1_xattn_g2, L1_xattn_be2, L1_xattn_wq2, L1_xattn_wk2, L1_xattn_wv2, L1_xattn_wo2, L1_xattn_bo2, L1_xattn_g3, L1_xattn_be3, L1_xattn_w_ff1, L1_xattn_b_ff1, L1_xattn_w_ff2, L1_xattn_b_ff2):
    import jax
    import jax.numpy as jnp

    def _L0_xattn_ref(hidden_states, encoder_hidden_states, Wq, Wk, Wv, Wq_ca, Wk_ca, Wv_ca, Wout, b_out):
        import jax, jax.numpy as jnp
        import numpy as np
        HEADS = 8
        NUM_TOKENS = 4
        CROSS_ATTENTION_DIM = 96

        def _mha(q, k, v, heads=HEADS):
            B, Sq, H = q.shape
            Sk = k.shape[1]
            d = H // heads
            qh = q.reshape(B, Sq, heads, d).transpose(0, 2, 1, 3)
            kh = k.reshape(B, Sk, heads, d).transpose(0, 2, 1, 3)
            vh = v.reshape(B, Sk, heads, d).transpose(0, 2, 1, 3)
            scores = jnp.einsum('bhqd,bhkd->bhqk', qh, kh) * jnp.asarray(d, q.dtype) ** (-0.5)
            probs = jax.nn.softmax(scores, axis=-1)
            out = jnp.einsum('bhqk,bhkd->bhqd', probs, vh)
            return out.transpose(0, 2, 1, 3).reshape(B, Sq, H)
        residual = hidden_states
        unet_size = residual.shape[1]
        end_pos = encoder_hidden_states.shape[1] - NUM_TOKENS
        enc = encoder_hidden_states[:, :end_pos, :]
        ca = encoder_hidden_states[:, end_pos:, :]
        query = hidden_states @ Wq
        keyt = enc @ Wk
        valt = enc @ Wv
        hs = _mha(query, keyt, valt)
        ca_q1 = jnp.einsum('btc,th->bch', ca, Wq_ca)
        indices = np.linspace(0, CROSS_ATTENTION_DIM - 1, unet_size).astype(np.int64)
        ca_q1 = ca_q1[:, indices, :]
        ca_hs1 = _mha(ca_q1, residual, residual)
        ca_q2 = ca_hs1 @ Wq
        ca_k2 = ca @ Wk_ca
        ca_v2 = ca @ Wv_ca
        ca_hs2 = _mha(ca_q2, ca_k2, ca_v2)
        out = hs + ca_hs2
        out = out @ Wout + b_out
        out = out + residual
        return out

    def _L1_xattn_ref(x, context, g1, be1, wq1, wk1, wv1, wo1, bo1, g2, be2, wq2, wk2, wv2, wo2, bo2, g3, be3, w_ff1, b_ff1, w_ff2, b_ff2):
        import jax, jax.numpy as jnp
        import numpy as np
        DIM, HEADS, DHEAD, CTX_DIM, DFF = (160, 20, 64, 96, 640)
        EPS = 1e-05
        SCALE = DHEAD ** (-0.5)

        def layer_norm(x, g, b):
            mu = jnp.mean(x, axis=-1, keepdims=True)
            var = jnp.mean(jnp.square(x - mu), axis=-1, keepdims=True)
            return (x - mu) * jax.lax.rsqrt(var + EPS) * g + b

        def cross_attention(x, ctx, wq, wk, wv, wo, bo):
            B, N, _ = x.shape
            M = ctx.shape[1]
            q = jnp.einsum('bne,ef->bnf', x, wq).reshape(B, N, HEADS, DHEAD).transpose(0, 2, 1, 3)
            k = jnp.einsum('bme,ef->bmf', ctx, wk).reshape(B, M, HEADS, DHEAD).transpose(0, 2, 1, 3)
            v = jnp.einsum('bme,ef->bmf', ctx, wv).reshape(B, M, HEADS, DHEAD).transpose(0, 2, 1, 3)
            scores = jnp.einsum('bhnd,bhmd->bhnm', q, k) * SCALE
            attn = jax.nn.softmax(scores, axis=-1)
            out = jnp.einsum('bhnm,bhmd->bhnd', attn, v)
            out = out.transpose(0, 2, 1, 3).reshape(B, N, HEADS * DHEAD)
            return jnp.einsum('bnf,fe->bne', out, wo) + bo

        def geglu_ff(x, w1, b1, w2, b2):
            h = jnp.einsum('bne,ef->bnf', x, w1) + b1
            a, gate = (h[..., :DFF], h[..., DFF:])
            h = a * jax.nn.gelu(gate)
            return jnp.einsum('bnf,fe->bne', h, w2) + b2

        def block_forward(x, context, g1, be1, wq1, wk1, wv1, wo1, bo1, g2, be2, wq2, wk2, wv2, wo2, bo2, g3, be3, w_ff1, b_ff1, w_ff2, b_ff2):
            x = cross_attention(layer_norm(x, g1, be1), layer_norm(x, g1, be1), wq1, wk1, wv1, wo1, bo1) + x
            x = cross_attention(layer_norm(x, g2, be2), context, wq2, wk2, wv2, wo2, bo2) + x
            return geglu_ff(layer_norm(x, g3, be3), w_ff1, b_ff1, w_ff2, b_ff2) + x
        return block_forward(x, context, g1, be1, wq1, wk1, wv1, wo1, bo1, g2, be2, wq2, wk2, wv2, wo2, bo2, g3, be3, w_ff1, b_ff1, w_ff2, b_ff2)
    x = _L0_xattn_ref(x, ctx_768, L0_xattn_Wq, L0_xattn_Wk, L0_xattn_Wv, L0_xattn_Wq_ca, L0_xattn_Wk_ca, L0_xattn_Wv_ca, L0_xattn_Wout, L0_xattn_b_out)
    x = _L1_xattn_ref(x, ctx_768, L1_xattn_g1, L1_xattn_be1, L1_xattn_wq1, L1_xattn_wk1, L1_xattn_wv1, L1_xattn_wo1, L1_xattn_bo1, L1_xattn_g2, L1_xattn_be2, L1_xattn_wq2, L1_xattn_wk2, L1_xattn_wv2, L1_xattn_wo2, L1_xattn_bo2, L1_xattn_g3, L1_xattn_be3, L1_xattn_w_ff1, L1_xattn_b_ff1, L1_xattn_w_ff2, L1_xattn_b_ff2)
    return x

_drawn_inputs = setup_inputs


def setup_inputs(seed=0):
    import zlib

    import numpy as np

    out = dict(_drawn_inputs(seed))
    spreads = {'L0_xattn_b_out': (0.0, 0.1),
     'L1_xattn_g1': (1.0, 0.6),
     'L1_xattn_be1': (0.0, 0.376),
     'L1_xattn_bo1': (0.0, 0.1),
     'L1_xattn_g2': (1.0, 0.6),
     'L1_xattn_be2': (0.0, 0.8),
     'L1_xattn_bo2': (0.0, 0.1),
     'L1_xattn_g3': (1.0, 0.6),
     'L1_xattn_be3': (0.0, 0.8),
     'L1_xattn_b_ff1': (0.0, 0.8),
     'L1_xattn_b_ff2': (0.0, 0.1)}
    factors = {'L0_xattn_Wq': 8.0,
     'L0_xattn_Wk': 8.0,
     'L0_xattn_Wq_ca': 64.0,
     'L0_xattn_Wk_ca': 64.0,
     'L1_xattn_wq1': 8.0,
     'L1_xattn_wk1': 8.0,
     'L1_xattn_wq2': 8.0,
     'L1_xattn_wk2': 8.0}
    for name, (base, spread) in spreads.items():
        noise = np.random.default_rng([zlib.crc32(name.encode()), seed]).standard_normal(out[name].shape)
        drawn = base * np.exp(spread * noise) if base else spread * noise
        out[name] = jnp.asarray(drawn.astype(out[name].dtype))
    for name, factor in factors.items():
        out[name] = (out[name] * factor).astype(out[name].dtype)
    return out
```

```python
from contextlib import ExitStack

import numpy as np

import concourse.bass as bass
from concourse import mybir

F32 = mybir.dt.float32
F32R = mybir.dt.float32r
BF16 = mybir.dt.bfloat16
F16 = mybir.dt.float16
ACT = mybir.ActivationFunctionType
ALU = mybir.AluOpType
AX = mybir.AxisListType

P = 128
NB, SEQ, HID = 8, 256, 160
QT = SEQ // P
NT = NB * QT
HA, HB = P, HID - P
REP = P // HB
CTX, CDIM = 512, 96
HEADS, DH = 20, 64
INNER = HEADS * DH
PAIRS = HEADS // 2
NCH = INNER // P
DFF = 640
EPS = 1e-5
DV = DH + 1


def after(engine, semaphore, count):
    if isinstance(count, int) and count <= 0:
        return
    engine.wait_ge(semaphore, count)


class Ring:

    BANKS = 3

    def __init__(self, units, periods=NB):
        self.periods = periods
        self.keys = {kind: units(kind) for kind in ("first", "steady", "last", "tail")}

    def number(self, kind, period, key):
        pos = self.keys[kind].index(key)
        n = len(self.keys["first"])
        if kind == "first":
            return pos
        if kind == "tail":
            return n + (self.periods - 2) * len(self.keys["steady"]) + len(self.keys["last"]) + pos
        return (period - 1) * len(self.keys["steady"]) + n + pos

    def bank(self, kind, key):
        return self.keys[kind].index(key) % self.BANKS

    def back(self, kind, key):
        pos = self.keys[kind].index(key)
        if pos >= self.BANKS:
            return self.BANKS
        before = {"first": [], "steady": ["first", "steady"], "last": ["steady"], "tail": ["last"]}[kind]
        found = []
        for b in before:
            n = len(self.keys[b])
            found += [pos + n - q for q in range(n) if q % self.BANKS == pos % self.BANKS][-1:]
        return min(found) if found else None


def periods(engine, slot):
    for s in range(PAIRS):
        slot("first", s, (0, 0), None, (1, 1))
    with engine.Fori(0, (NB - 2) // 2) as i:
        for j in (1, 2):
            b = i * 2 + j
            for s in range(PAIRS):
                slot("steady", s, (b, j % 2), (b - 1, 1 - j % 2), (b + 1, 1 - j % 2))
    for s in range(PAIRS):
        slot("last", s, (NB - 1, 1), (NB - 2, 0), None)
    for s in range(TAIL):
        slot("tail", s, None, (NB - 1, 1), None)


TAIL = 7


def load_stacked(engine, out, w, semaphore):
    for r in range(REP):
        engine.dma_start(out[r * HB:(r + 1) * HB, :], w[HA:HID, :]).then_inc(semaphore, 16)


def load_vectors(engine, g, be, bo, gain, shift, bo_row, semaphore):
    for out, v in ((gain, g), (shift, be)):
        column = v.rearrange("(p a) -> p a", a=1)
        engine.dma_start(out[:, 0:1], column[0:HA, :]).then_inc(semaphore, 16)
        load_stacked(engine, out[:, 1:2], column, semaphore)
    engine.dma_start(bo_row[:, :], bo.rearrange("(a n) -> a n", a=1).to_broadcast([P, HID])).then_inc(semaphore, 16)


def prepare_self(nc, name, g, be, wq, wk, wv, wo, bo, wq_h, wq_l, wq_s,
                 wk_h, wk_l, wk_s, wv_h, wv_l, wv_s, wo_hl, gain, shift, bo_row):
    stack = ExitStack()
    with stack:
        def sb(what, shape, dt):
            return stack.enter_context(nc.sbuf_tensor(f"{name}_{what}", shape, dt))

        raw = {w: (sb(f"raw_{w}a", [P, INNER], F32), sb(f"raw_{w}b", [P, INNER], F32)) for w in "qkv"}
        raw_o = sb("raw_o", [P, NCH, HID], F32)
        loaded = {w: stack.enter_context(nc.semaphore(f"{name}_loaded_{w}")) for w in "qkvo"}
        small = stack.enter_context(nc.semaphore(f"{name}_small"))
        rounded = stack.enter_context(nc.semaphore(f"{name}_rounded"))
        dram = {"q": wq, "k": wk, "v": wv}

        def twice(t):
            return t.rearrange("p (h d) -> p h d", d=DH)[:, :, None, :].to_broadcast([t.shape[0], HEADS, 2, DH])

        def as_heads(t):
            return t.rearrange("p h (a d) -> p h a d", a=2)

        with nc.Block() as block:
            @block.sync
            def _(sp):
                for w in "qkv":
                    sp.dma_start(raw[w][0][:, :], dram[w][0:HA, :]).then_inc(loaded[w], 16)
                    load_stacked(sp, raw[w][1], dram[w], loaded[w])
                sp.dma_start(raw_o[:, :, :], wo.rearrange("(k p) n -> p k n", p=P)).then_inc(loaded["o"], 16)
                load_vectors(sp, g, be, bo, gain, shift, bo_row, small)
                sp.wait_ge(small, 11 * 16)

            @block.scalar
            def _(act):
                for w, high, stacked in (("q", wq_h, wq_s), ("k", wk_h, wk_s)):
                    act.wait_ge(loaded[w], 5 * 16)
                    nc.scalar.copy(as_heads(high[:, :, :]), twice(raw[w][0][:, :]))
                    nc.scalar.copy(as_heads(stacked[:, :, :]), twice(raw[w][1][:, :])).then_inc(rounded, 1)
                act.wait_ge(loaded["v"], 5 * 16)
                nc.scalar.copy(wv_h[:, :], raw["v"][0][:, :])
                nc.scalar.copy(wv_s[:, :], raw["v"][1][:, :]).then_inc(rounded, 1)
                act.wait_ge(loaded["o"], 16)
                nc.scalar.copy(wo_hl[:, :, 0, :], raw_o[:, :, :]).then_inc(rounded, 1)

            @block.vector
            def _(dve):
                half = slice(P // 2, P)
                for n, (w, high, low, stacked) in enumerate((("q", wq_h, wq_l, wq_s), ("k", wk_h, wk_l, wk_s))):
                    dve.wait_ge(rounded, n + 1)
                    nc.vector.tensor_tensor(as_heads(low[:, :, :]), twice(raw[w][0][:, :]), as_heads(high[:, :, :]), ALU.subtract)
                    nc.vector.tensor_tensor(as_heads(stacked[half, :, :]), twice(raw[w][1][half, :]),
                                            as_heads(stacked[half, :, :]), ALU.subtract)
                dve.wait_ge(rounded, 3)
                nc.vector.tensor_tensor(wv_l[:, :], raw["v"][0][:, :], wv_h[:, :], ALU.subtract)
                nc.vector.tensor_tensor(wv_s[half, :], raw["v"][1][half, :], wv_s[half, :], ALU.subtract)
                dve.wait_ge(rounded, 4)
                nc.vector.tensor_tensor(wo_hl[:, :, 1, :], raw_o[:, :, :], wo_hl[:, :, 0, :], ALU.subtract)


def prepare_cross(nc, name, ident, g, be, wq, wk, wv, wo, bo,
                  wq_h, wq_l, wq_s, wv_h, wv_l, wo_hl, gain, shift, bo_row):
    stack = ExitStack()
    with stack:
        def sb(what, shape, dt):
            return stack.enter_context(nc.sbuf_tensor(f"{name}_{what}", shape, dt))

        def sem(what):
            return stack.enter_context(nc.semaphore(f"{name}_{what}"))

        raw_qa, raw_qb = sb("raw_qa", [P, INNER], F32), sb("raw_qb", [HB, INNER], F32)
        raw_k, raw_v = sb("raw_k", [CDIM, INNER], F32), sb("raw_v", [CDIM, INNER], F32)
        raw_o = sb("raw_o", [P, NCH, HID], F32)
        B4, A, K, W = 0, P, 2 * P, 2 * P + CDIM
        w_t = sb("w_t", [P, NCH, W], F32)
        turned = [stack.enter_context(nc.psum_tensor(f"{name}_turned{i}", [P, 512], F32)) for i in range(2)]
        prod = [stack.enter_context(nc.psum_tensor(f"{name}_prod{i}", [P, 512], F32)) for i in range(2)]
        loaded_qk, loaded_v, loaded_o, small = sem("loaded_qk"), sem("loaded_v"), sem("loaded_o"), sem("small")
        turned_done = sem("turned_done")
        turned_read = sem("turned_read")
        prod_done = sem("prod_done")
        prod_hi = sem("prod_hi")
        prod_read = sem("prod_read")
        rounded = sem("rounded")

        with nc.Block() as block:
            @block.sync
            def _(sp):
                sp.dma_start(raw_qa[:, :], wq[0:HA, :]).then_inc(loaded_qk, 16)
                sp.dma_start(raw_qb[:, :], wq[HA:HID, :]).then_inc(loaded_qk, 16)
                sp.dma_start(raw_k[:, :], wk).then_inc(loaded_qk, 16)
                sp.dma_start(raw_v[:, :], wv).then_inc(loaded_v, 16)
                sp.dma_start(raw_o[:, :, :], wo.rearrange("(k p) n -> p k n", p=P)).then_inc(loaded_o, 16)
                load_vectors(sp, g, be, bo, gain, shift, bo_row, small)
                sp.wait_ge(small, 11 * 16)

            @block.tensor
            def _(pe):
                pe.wait_ge(loaded_qk, 3 * 16)

                def turn(k):
                    after(pe, turned_read, k - 1)
                    cols, out = slice(k * P, (k + 1) * P), turned[k % 2]
                    nc.tensor.transpose(out[:, 0:HB], raw_qb[:, cols], ident[0:HB, 0:HB])
                    nc.tensor.transpose(out[:, HB:HID], raw_qa[:, cols], ident[:, :])
                    nc.tensor.transpose(out[:, HID:HID + CDIM], raw_k[:, cols], ident[0:CDIM, 0:CDIM]).then_inc(turned_done, 1)

                def multiply(k):
                    pe.wait_ge(turned_read, k + 1)
                    for j in range(2):
                        head, rows = 2 * k + j, slice(j * DH, (j + 1) * DH)
                        after(pe, prod_read, head - 1)
                        out = prod[head % 2]
                        nc.tensor.matmul(out[:, 0:CDIM], w_t[rows, k, A:K], w_t[rows, k, K:W], start=True, stop=True)
                        nc.tensor.matmul(out[:, CDIM:2 * CDIM], w_t[rows, k, B4:A], w_t[rows, k, K:W], start=True,
                                         stop=True).then_inc(prod_done, 1)

                for k in range(NCH + 1):
                    if k < NCH:
                        turn(k)
                    if k >= 1:
                        multiply(k - 1)

            @block.scalar
            def _(act):
                act.wait_ge(loaded_v, 16)
                nc.scalar.copy(wv_h[:, :], raw_v[:, :]).then_inc(rounded, 1)
                act.wait_ge(loaded_o, 16)
                nc.scalar.copy(wo_hl[:, :, 0, :], raw_o[:, :, :]).then_inc(rounded, 1)
                for h in range(HEADS):
                    act.wait_ge(prod_done, h + 1)
                    nc.scalar.copy(wq_h[:, h, :], prod[h % 2][:, 0:CDIM])
                    nc.scalar.copy(wq_s[:, h, :], prod[h % 2][:, CDIM:2 * CDIM]).then_inc(prod_hi, 1)

            @block.vector
            def _(dve):
                def copy_turned(k):
                    dve.wait_ge(turned_done, k + 1)
                    nc.vector.tensor_copy(w_t[:, k, B4:A].rearrange("p (r f) -> p r f", r=REP),
                                          turned[k % 2][:, None, 0:HB].to_broadcast([P, REP, HB]))
                    nc.vector.tensor_copy(w_t[:, k, A:W], turned[k % 2][:, HB:HID + CDIM]).then_inc(turned_read, 1)

                half = slice(P // 2, P)
                copy_turned(0)
                for k in range(NCH):
                    if k + 1 < NCH:
                        copy_turned(k + 1)
                    for h in (2 * k, 2 * k + 1):
                        dve.wait_ge(prod_hi, h + 1)
                        nc.vector.tensor_tensor(wq_l[:, h, :], prod[h % 2][:, 0:CDIM], wq_h[:, h, :], ALU.subtract)
                        nc.vector.tensor_tensor(wq_s[half, h, :], prod[h % 2][half, CDIM:2 * CDIM], wq_s[half, h, :],
                                                ALU.subtract).then_inc(prod_read, 1)
                dve.wait_ge(rounded, 2)
                nc.vector.tensor_tensor(wv_l[:, :], raw_v[:, :], wv_h[:, :], ALU.subtract)
                nc.vector.tensor_tensor(wo_hl[:, :, 1, :], raw_o[:, :, :], wo_hl[:, :, 0, :], ALU.subtract)


def attention(nc, name, cross, x, ident, ctx_dram, g, be, wq, wk, wv, wo, bo):
    KT = CTX // P if cross else SEQ // P
    KD = KT * P
    U = 4 if cross else 2
    UB = U * PAIRS
    MROW = CDIM if cross else DH
    QU = 1 if cross else 2
    SCALE = float(DH) ** -0.5
    VN = [(0, 512), (512, 512), (1024, 256)]
    VU = [(t, n) for t in range(KT) for n in range(3)]

    def extras(kind, s):
        out = []
        has_prev, has_nxt, has_cur = kind != "first", kind in ("first", "steady"), kind != "tail"
        if has_prev and s in (0, 2, 4):
            out.append((0, ("ot", "prev", 2 + s // 2)))
        if cross and has_nxt and s == 3:
            out.append((1, ("ctx", "nxt", 0)))
        if has_nxt and s == 4:
            out.append((1, ("ln", "nxt", 0)))
        if has_prev and s in (5, 6):
            out.append((0, ("out", "prev", s - 5)))
        if has_cur and s in (6, 8):
            out.append((1 if s == 6 else 0, ("ot", "cur", (s - 6) // 2)))
        if has_nxt:
            plan = {5: [0, 1], 6: [2, 3], 7: [4, 5, 6], 8: [7, 8], 9: [9, 10, 11]} if cross else \
                   {5: [0], 6: [1], 7: [2, 3], 8: [4], 9: [5]}
            for n, v in enumerate(plan.get(s, ())):
                out.append((min(n + 1, U - 1), ("v", "nxt", v)))
        return sorted(out, key=lambda e: e[0])

    def slot_keys(kind, s):
        keys = []
        if kind != "tail":
            keys.append(("proj", s, 0))
        mt = ("mt", "cur", s - 2) if s >= 2 else ("mt", "prev", s + PAIRS - 2)
        if (mt[1] == "cur" and kind != "tail") or (mt[1] == "prev" and kind != "first"):
            keys.append(mt)
        for step in range(U):
            if step == 1 and QU == 2 and kind != "tail":
                keys.append(("proj", s, 1))
            keys += [k for at, k in extras(kind, s) if at == step]
        return keys

    def all_keys(kind):
        if kind == "tail":
            return [k for s in range(TAIL) for k in slot_keys(kind, s)]
        pre = []
        if kind == "first":
            pre = [("ctx", "pre", 0)] * cross + [("ln", "pre", 0)] + [("v", "pre", v) for v in range(len(VU))]
        return pre + [k for s in range(PAIRS) for k in slot_keys(kind, s)]

    ring = Ring(all_keys)
    PRE = sum(key[1] == "pre" for key in ring.keys["first"])
    NCONST = 2

    def earlier(kind, period, key):
        return ring.number("last", NB - 1, key) if kind == "tail" else ring.number("steady", period - 1, key)

    def proj_number(kind, s, period, j):
        if s == 0:
            return earlier(kind, period, ("proj", PAIRS - 1, j))
        return ring.number(kind, period, ("proj", s - 1, j))

    def shift_number(kind, s, period):
        if s == 0:
            return earlier(kind, period, ("mt", "cur", PAIRS - 3))
        return ring.number(kind, period, ("mt", "cur" if s >= 3 else "prev", (s - 3) % PAIRS))

    def values_number(kind, period):
        if kind == "first":
            return ring.number("first", 0, ("v", "pre", len(VU) - 1))
        return earlier(kind, period, ("v", "nxt", len(VU) - 1))

    def before(s, d, cur, prev):
        if s >= d:
            return cur and (cur, s - d)
        return prev and (prev, s - d + PAIRS)

    stack = ExitStack()
    with stack:
        def sb(what, shape, dt):
            return stack.enter_context(nc.sbuf_tensor(f"{name}_{what}", shape, dt))

        def bank(what):
            return stack.enter_context(nc.psum_tensor(f"{name}_{what}", [P, 512], F32))

        def sem(what):
            return stack.enter_context(nc.semaphore(f"{name}_{what}"))

        QW = CDIM if cross else 2 * DH
        wq_h, wq_l, wq_s = (sb(f"wq_{i}", [P, HEADS, QW], F32R) for i in "hls")
        if cross:
            wv_h, wv_l = (sb(f"wv_{i}", [CDIM, INNER], F32R) for i in "hl")
        else:
            wk_h, wk_l, wk_s = (sb(f"wk_{i}", [P, HEADS, QW], F32R) for i in "hls")
            wv_h, wv_l, wv_s = (sb(f"wv_{i}", [P, INNER], F32R) for i in "hls")
        wo_hl = sb("wo_hl", [P, NCH, 2, HID], F32R)
        gain = sb("gain", [P, 2], F32)
        shift = sb("shift", [P, 2], F32)
        bo_row = sb("bo_row", [P, HID], F32)
        if cross:
            prepare_cross(nc, name, ident, g, be, wq, wk, wv, wo, bo,
                          wq_h, wq_l, wq_s, wv_h, wv_l, wo_hl, gain, shift, bo_row)
        else:
            prepare_self(nc, name, g, be, wq, wk, wv, wo, bo, wq_h, wq_l, wq_s,
                         wk_h, wk_l, wk_s, wv_h, wv_l, wv_s, wo_hl, gain, shift, bo_row)

        neg_eye = sb("neg_eye", [P, 2], F32)
        lo_rows = sb("lo_rows", [P, 1], F32)
        half_neg = sb("half_neg", [P, QT], F32)
        eps = sb("eps", [P, QT], F32)
        stats_seen = sb("stats_seen", [P, QT], F32)

        xn = sb("xn", [P, QT, 2, P], F32)
        stats = sb("stats", [P, QT, 6], F32)
        mean_var = sb("mean_var", [P, QT, 2], F32)
        var_eps = sb("var_eps", [P, QT], F32)
        rstd = sb("rstd", [P, QT], F32)
        ln_t = sb("ln_t", [P, 2, SEQ], F32)
        ln_h = [sb(f"ln_h{i}", [P, 2, SEQ], F32R) for i in range(2)]
        ln_l = [sb(f"ln_l{i}", [P, SEQ], F32R) for i in range(2)]
        if cross:
            ctx_rows = [sb(f"ctx_rows{i}", [P, KT, CDIM], F32) for i in range(2)]
            ctx_h = [sb(f"ctx_h{i}", [P, CTX], F32R) for i in range(2)]
            ctx_l = [sb(f"ctx_l{i}", [CDIM, CTX], F32R) for i in range(2)]
            q_h = sb("q_h", [P, 4, 2, SEQ], F32R)
            q_l = sb("q_l", [CDIM, 4, 2, SEQ], F32R)
        else:
            qk_h = sb("qk_h", [P, 8, 2, SEQ], F32R)
            q_hl = sb("q_hl", [P, 8, SEQ], F32R)
            k_l1 = sb("k_l1", [P, 8, SEQ], F32R)
        v_h = [sb(f"v_h{i}", [P, KT, HEADS, DV], BF16) for i in range(2)]
        v_l = [sb(f"v_l{i}", [P, KT, HEADS, DV], F16) for i in range(2)]
        maxima = sb("maxima", [P, 2, QT, P], F32)
        PR = 2 * U
        probs = sb("probs", [P, PR, 512], F32)
        probs_l = sb("probs_l", [P, PR, 512], F16)
        recip = sb("recip", [P, 4], F32)
        attn = sb("attn", [P, QT, INNER], F32)
        attn_th = sb("attn_th", [P, NCH, SEQ], F32R)
        attn_tl = sb("attn_tl", [P, NCH, SEQ], F32R)

        shared = [bank(f"shared{i}") for i in range(Ring.BANKS)]
        max_bank = [bank(f"max{i}") for i in range(2)]
        score_bank = [bank(f"score{i}") for i in range(2)]
        pv_bank = bank("pv")

        rows_in = [sem(f"rows_in{i}") for i in range(2)]
        eye_zero = sem("eye_zero")
        consts = sem("consts")
        filled = sem("filled")
        emptied = sem("emptied")
        stats_ready = sem("stats_ready")
        var_ready = sem("var_ready")
        var_eps_ready = sem("var_eps_ready")
        rstd_ready = sem("rstd_ready")
        xn_ready = sem("xn_ready")
        lnt_ready = sem("lnt_ready")
        ln_ready = sem("ln_ready")
        ctx_hi = sem("ctx_hi")
        v_hi = sem("v_hi")
        q_hi = sem("q_hi")
        max_filled = sem("max_filled")
        max_read = sem("max_read")
        scored = sem("scored")
        exped = sem("exped")
        probs_split = sem("probs_split")
        pv_done = sem("pv_done")
        recip_ready = sem("recip_ready")
        attn_ready = sem("attn_ready")
        attn_hi = sem("attn_hi")
        x_bo_ready = sem("x_bo_ready")
        part_ready = sem("part_ready")

        block = stack.enter_context(nc.Block())

        @block.sync
        def _(sp):
            if not cross:
                return

            def rows(b, parity):
                sp.dma_start(ctx_rows[parity][:, :, :],
                             ctx_dram[b, :, :].rearrange("(t p) c -> p t c", p=P)).then_inc(rows_in[parity], 16)

            rows(0, 0)
            rows(1, 1)
            with sp.Fori(0, (NB - 2) // 2) as i:
                for j in (0, 1):
                    b = i * 2 + j
                    sp.wait_ge(ctx_hi, b + 1)
                    rows(b + 2, j)

        @block.gpsimd
        def _(pool):
            nc.gpsimd.memset(neg_eye[:, :], 0.0).then_inc(eye_zero, 1)
            pool.wait_ge(eye_zero, 1)
            nc.gpsimd.affine_select(out=neg_eye[:, :], in_=neg_eye[:, :], compare_op=ALU.not_equal, fill=-1.0,
                                    base=-MROW, pattern=[[-1, 2]], channel_multiplier=1).then_inc(consts, 1)

            def inverse_root(b):
                pool.wait_ge(var_ready, b + 1)
                nc.gpsimd.tensor_tensor(var_eps[:, :], mean_var[:, :, 1], eps[:, :], ALU.add).then_inc(var_eps_ready, 1)
                pool.wait_ge(var_eps_ready, b + 1)
                nc.gpsimd.tensor_tensor(rstd[:, :], var_eps[:, :], half_neg[:, :], ALU.pow).then_inc(rstd_ready, 1)

            def slot(kind, s, cur, prev, nxt):
                if s == 4 and nxt is not None:
                    inverse_root(nxt[0])
                if s == 4 and prev is not None:
                    rows = x[:, bass.ds(prev[0] * QT, QT), :]
                    nc.gpsimd.tensor_tensor(rows, rows, bo_row[:, None, :].to_broadcast([P, QT, HID]), ALU.add).then_inc(x_bo_ready, 1)
                if (work := before(s, 3, cur, prev)) is not None:
                    (b, _), p = work
                    for u in range(U):
                        n = p * U + u
                        pool.wait_ge(exped, b * UB + n + 1)
                        whole = probs[:, n % PR, :]
                        nc.gpsimd.tensor_tensor(probs_l[:, n % PR, :], whole, whole.bitcast(BF16)[:, 1::2],
                                                ALU.subtract).then_inc(probs_split, 1)

            pool.wait_ge(consts, NCONST)
            inverse_root(0)
            periods(pool, slot)

        @block.scalar
        def _(act):
            def ln_transposed(kind, period, key, b):
                act.wait_ge(filled, ring.number(kind, period, key) + 1)
                bank_ = shared[ring.bank(kind, key)]
                nc.scalar.activation(ln_t[:, 0, :], bank_[:, 0:SEQ], ACT.Identity, bias=shift[:, 0:1], scale=gain[:, 0:1])
                nc.scalar.activation(ln_t[:, 1, :], bank_[:, SEQ:2 * SEQ], ACT.Identity, bias=shift[:, 1:2],
                                     scale=gain[:, 1:2]).then_inc(lnt_ready, 1)

            def extra(kind, period, key, batch):
                b, parity = batch
                what, _, i = key
                if what == "ln":
                    ln_transposed(kind, period, key, b)
                    return
                if what == "out":
                    return
                act.wait_ge(filled, ring.number(kind, period, key) + 1)
                bank_ = shared[ring.bank(kind, key)]
                if what == "ctx":
                    nc.scalar.copy(ctx_h[parity][0:CDIM, :], bank_[0:CDIM, :]).then_inc(ctx_hi, 1)
                elif what == "v":
                    t, n = VU[i]
                    at, width = VN[n]
                    nc.scalar.copy(v_h[parity][:, t, at // DH:(at + width) // DH, 0:DH],
                                   bank_[:, 0:width].rearrange("p (h d) -> p h d", d=DH)).then_inc(v_hi, 1)
                elif what == "ot":
                    nc.scalar.copy(attn_th[:, 2 * i:2 * i + 2, :],
                                   bank_[:, :].rearrange("p (k q) -> p k q", k=2)).then_inc(attn_hi, 1)

            def projected(kind, s, j, cur):
                b, parity = cur
                key = ("proj", s, j)
                act.wait_ge(filled, ring.number(kind, b, key) + 1)
                after(act, scored, b * UB + (s - 3) * U)
                bank_ = shared[ring.bank(kind, key)]
                if cross:
                    at = (parity * PAIRS + s) % 4
                    nc.scalar.copy(q_h[0:CDIM, at, :, :], bank_[0:CDIM, :].rearrange("p (h q) -> p h q", h=2)).then_inc(q_hi, 1)
                else:
                    at = (parity * HEADS + 2 * s + j) % 8
                    nc.scalar.copy(qk_h[:, at, :, :], bank_[:, :].rearrange("p (h q) -> p h q", h=2)).then_inc(q_hi, 1)

            def slot(kind, s, cur, prev, nxt):
                period = cur[0] if cur is not None else NB
                if cur is not None:
                    projected(kind, s, 0, cur)
                for step in range(U):
                    if step == 1 and QU == 2 and cur is not None:
                        projected(kind, s, 1, cur)
                    if (work := before(s, 3, cur, prev)) is not None:
                        (b, _), p = work
                        n = p * U + step
                        act.wait_ge(scored, b * UB + n + 1)
                        after(act, pv_done, b * PAIRS + p - 1)
                        nc.scalar.activation(probs[:, n % PR, :], score_bank[n % 2][:, :], ACT.Exp,
                                             scale=SCALE).then_inc(exped, 1)
                    for at, key in extras(kind, s):
                        if at == step:
                            extra(kind, period, key, {"cur": cur, "prev": prev, "nxt": nxt}[key[1]])

            for key in ring.keys["first"][:PRE]:
                extra("first", 0, key, (0, 0))
            periods(act, slot)

        @block.vector
        def _(dve):
            nc.vector.memset(half_neg[:, :], -0.5)
            nc.vector.memset(eps[:, :], EPS)
            nc.vector.memset(maxima[:, :, :, :], 0.0)
            nc.vector.memset(lo_rows[0:64, :], 0.0)
            nc.vector.memset(lo_rows[64:P, :], -1.0)
            for i in range(2):
                nc.vector.memset(v_h[i][:, :, :, DH:DV], 1.0)
                nc.vector.memset(v_l[i][:, :, :, DH:DV], 0.0)
            if cross:
                for i in range(2):
                    nc.vector.memset(ctx_h[i][CDIM:P, :].bitcast(F32), 1.0)
            else:
                nc.vector.memset(k_l1[DH:P, :, :].bitcast(F32), 1.0)
            nc.vector.memset(rstd[:, :], 0.0).then_inc(consts, 1)
            dve.wait_ge(consts, NCONST)

            def statistics(b):
                for t in range(QT):
                    nc.vector.bn_stats(stats[:, t, :], x[:, b * QT + t, :]).then_inc(stats_ready, 1)
                dve.wait_ge(stats_ready, b * QT + QT)
                nc.vector.tensor_copy(stats_seen[:, :], stats[:, :, 0])
                for t in range(QT):
                    ins = nc.vector.bn_aggr(mean_var[:, t, :], stats[:, t, :])
                ins.then_inc(var_ready, 1)

            def normalise(b):
                dve.wait_ge(rstd_ready, b + 1)
                for t in range(QT):
                    row = x[:, b * QT + t, :]
                    nc.vector.tensor_scalar(xn[:, t, 0, :], row[:, 0:HA], mean_var[:, t, 0:1], rstd[:, t:t + 1],
                                            ALU.subtract, ALU.mult)
                    ins = nc.vector.tensor_scalar(xn[:, t, 1, :].rearrange("p (r f) -> p r f", r=REP),
                                                  row[:, None, HA:HID].to_broadcast([P, REP, HB]),
                                                  mean_var[:, t, 0:1], rstd[:, t:t + 1], ALU.subtract, ALU.mult)
                ins.then_inc(xn_ready, 1)

            def extra(kind, period, key, batch):
                b, parity = batch
                what, _, i = key
                bank_ = shared[ring.bank(kind, key)]
                if what == "ln":
                    h, low = ln_h[parity], ln_l[parity]
                    dve.wait_ge(lnt_ready, b + 1)
                    nc.vector.tensor_copy(h[:, :, :], ln_t[:, :, :]).then_inc(emptied, 1)
                    dve.wait_ge(emptied, ring.number(kind, period, key) + 1)
                    nc.vector.tensor_tensor(low[:, :], ln_t[:, 0, :], h[:, 0, :], ALU.subtract)
                    nc.vector.tensor_tensor(h[HB:2 * HB, 1, :], ln_t[HB:2 * HB, 1, :], h[HB:2 * HB, 1, :], ALU.subtract)
                    nc.vector.tensor_tensor(h[3 * HB:P, 1, :], ln_t[3 * HB:P, 1, :], h[3 * HB:P, 1, :],
                                            ALU.subtract).then_inc(ln_ready, 1)
                elif what == "ctx":
                    dve.wait_ge(ctx_hi, b + 1)
                    nc.vector.tensor_tensor(ctx_l[parity][:, :], bank_[0:CDIM, :], ctx_h[parity][0:CDIM, :],
                                            ALU.subtract).then_inc(emptied, 1)
                elif what == "v":
                    t, n = VU[i]
                    at, width = VN[n]
                    heads = slice(at // DH, (at + width) // DH)
                    dve.wait_ge(v_hi, b * len(VU) + i + 1)
                    nc.vector.tensor_tensor(v_l[parity][:, t, heads, 0:DH],
                                            bank_[:, 0:width].rearrange("p (h d) -> p h d", d=DH),
                                            v_h[parity][:, t, heads, 0:DH], ALU.subtract).then_inc(emptied, 1)
                elif what == "ot":
                    dve.wait_ge(attn_hi, b * (NCH // 2) + i + 1)
                    nc.vector.tensor_tensor(attn_tl[:, 2 * i:2 * i + 2, :],
                                            bank_[:, :].rearrange("p (k q) -> p k q", k=2),
                                            attn_th[:, 2 * i:2 * i + 2, :], ALU.subtract).then_inc(emptied, 1)
                elif what == "out":
                    dve.wait_ge(x_bo_ready, b + 1)
                    dve.wait_ge(filled, ring.number(kind, period, key) + 1)
                    row = x[:, b * QT + i, :]
                    nc.vector.tensor_tensor(row, bank_[:, 0:HID], row, ALU.add).then_inc(part_ready, 1)
                    dve.wait_ge(part_ready, b * QT + i + 1)
                    nc.vector.tensor_tensor(row, bank_[:, HID:2 * HID], row, ALU.add).then_inc(emptied, 1)

            def projected(kind, s, j, cur):
                b, parity = cur
                key = ("proj", s, j)
                bank_ = shared[ring.bank(kind, key)]
                dve.wait_ge(q_hi, b * PAIRS * QU + s * QU + j + 1)
                if cross:
                    at = (parity * PAIRS + s) % 4
                    nc.vector.tensor_tensor(q_l[:, at, :, :], bank_[0:CDIM, :].rearrange("p (h q) -> p h q", h=2),
                                            q_h[0:CDIM, at, :, :], ALU.subtract).then_inc(emptied, 1)
                else:
                    at = (parity * HEADS + 2 * s + j) % 8
                    nc.vector.scalar_tensor_tensor(q_hl[:, at, :], qk_h[:, at, 0, :], lo_rows[:, 0:1], bank_[:, 0:SEQ],
                                                   ALU.mult, ALU.add)
                    nc.vector.tensor_tensor(k_l1[0:DH, at, :], bank_[0:DH, SEQ:2 * SEQ], qk_h[0:DH, at, 1, :],
                                            ALU.subtract).then_inc(emptied, 1)

            def write_shift(kind, period, key, parity):
                p = key[2]
                bank_ = shared[ring.bank(kind, key)]
                dve.wait_ge(filled, ring.number(kind, period, key) + 1)
                rows = slice(MROW, MROW + 32)
                if cross:
                    out = q_h[rows, (parity * PAIRS + p) % 4, :, :]
                else:
                    at = (parity * HEADS + 2 * p) % 8
                    out = qk_h[rows, at:at + 2, 0, :]
                nc.vector.tensor_tensor(out, bank_[rows, None, 0:SEQ].to_broadcast([32, 2, SEQ]),
                                        neg_eye[rows, :, None].to_broadcast([32, 2, SEQ]), ALU.mult).then_inc(emptied, 1)

            def slot(kind, s, cur, prev, nxt):
                period = cur[0] if cur is not None else NB
                if cur is not None:
                    projected(kind, s, 0, cur)
                if (work := before(s, 2, cur, prev)) is not None:
                    (_, parity), p = work
                    write_shift(kind, period, ("mt", "cur" if s >= 2 else "prev", p), parity)
                for step in range(U):
                    if step == 1 and QU == 2 and cur is not None:
                        projected(kind, s, 1, cur)
                    if (work := before(s, 1, cur, prev)) is not None:
                        (b, _), p = work
                        n = p * U + step
                        dve.wait_ge(max_filled, b * UB + n + 1)
                        if cross:
                            j, t = step // 2, step % 2
                            out, scores = maxima[:, p % 2, t, MROW + j:MROW + j + 1], max_bank[n % 2][:, :]
                        else:
                            out = maxima[:, p % 2, :, MROW + step]
                            scores = max_bank[n % 2][:, :].rearrange("p (t k) -> p t k", t=QT)
                        nc.vector.reduce_max(out, scores, AX.X).then_inc(max_read, 1)
                    if s == 4 and step == 0 and nxt is not None:
                        normalise(nxt[0])
                    for at, key in extras(kind, s):
                        if at == step:
                            extra(kind, period, key, {"cur": cur, "prev": prev, "nxt": nxt}[key[1]])
                if s == 3 and nxt is not None:
                    statistics(nxt[0])
                if (work := before(s, 4, cur, prev)) is not None:
                    (b, _), p = work
                    dve.wait_ge(pv_done, b * PAIRS + p + 1)
                    sums = pv_bank[:, 0:4 * DV].rearrange("p (g d) -> p g d", d=DV)
                    nc.vector.reciprocal(recip[:, :], sums[:, :, DH]).then_inc(recip_ready, 1)
                    dve.wait_ge(recip_ready, b * PAIRS + p + 1)
                    out = attn[:, :, p * P:(p + 1) * P].rearrange("p t (h d) -> p h t d", h=2)
                    nc.vector.tensor_tensor(out, pv_bank[:, 0:4 * DV].rearrange("p (h t d) -> p h t d", h=2, t=QT)[:, :, :, 0:DH],
                                            recip[:, :].rearrange("p (h t) -> p h t", h=2)[:, :, :, None].to_broadcast([P, 2, QT, DH]),
                                            ALU.mult).then_inc(attn_ready, 1)

            statistics(0)
            normalise(0)
            for key in ring.keys["first"][:PRE]:
                extra("first", 0, key, (0, 0))
            periods(dve, slot)

        @block.tensor
        def _(pe):
            pe.wait_ge(consts, NCONST)

            def claim(kind, period, key):
                back = ring.back(kind, key)
                if back is not None:
                    after(pe, emptied, ring.number(kind, period, key) - back + 1)
                return shared[ring.bank(kind, key)]

            def extra(kind, period, key, batch):
                b, parity = batch
                what, _, i = key
                h, low = ln_h[parity], ln_l[parity]
                if what == "ctx":
                    pe.wait_ge(rows_in[parity], 8 * (b - parity) + 16)
                    bank_ = claim(kind, period, key)
                    for t in range(KT):
                        mm = nc.tensor.transpose(bank_[0:CDIM, t * P:(t + 1) * P], ctx_rows[parity][:, t, :], ident[:, :])
                elif what == "ln":
                    pe.wait_ge(xn_ready, b + 1)
                    bank_ = claim(kind, period, key)
                    for c in range(2):
                        for t in range(QT):
                            mm = nc.tensor.transpose(bank_[:, c * SEQ + t * P:c * SEQ + (t + 1) * P], xn[:, t, c, :], ident[:, :])
                elif what == "v":
                    t, n = VU[i]
                    at, width = VN[n]
                    bank_ = claim(kind, period, key)
                    tok, col = slice(t * P, (t + 1) * P), slice(at, at + width)
                    if cross:
                        if i == 0:
                            pe.wait_ge(emptied, ring.number(kind, period, ("ctx", key[1], 0)) + 1)
                        passes = [(ctx_h[parity][0:CDIM, tok], wv_h[:, col]), (ctx_l[parity][:, tok], wv_h[:, col]),
                                  (ctx_h[parity][0:CDIM, tok], wv_l[:, col])]
                    else:
                        if i == 0:
                            pe.wait_ge(ln_ready, b + 1)
                        passes = [(h[:, 0, tok], wv_h[:, col]), (low[:, tok], wv_h[:, col]),
                                  (h[:, 0, tok], wv_l[:, col]), (h[:, 1, tok], wv_s[:, col])]
                    for n, (lhs, rhs) in enumerate(passes):
                        mm = nc.tensor.matmul(bank_[:, 0:width], lhs, rhs, start=n == 0, stop=n == len(passes) - 1)
                elif what == "ot":
                    pe.wait_ge(attn_ready, b * PAIRS + 2 * i + 2)
                    bank_ = claim(kind, period, key)
                    for c in range(2):
                        for t in range(QT):
                            k = 2 * i + c
                            mm = nc.tensor.transpose(bank_[:, c * SEQ + t * P:c * SEQ + (t + 1) * P],
                                                     attn[:, t, k * P:(k + 1) * P], ident[:, :])
                elif what == "out":
                    bank_ = claim(kind, period, key)
                    if i == 0:
                        pe.wait_ge(emptied, ring.number(kind, period, ("ot", "prev", 4)) + 1)
                    for k in range(NCH):
                        for c, lhs in enumerate((attn_th, attn_tl)):
                            mm = nc.tensor.matmul(bank_[:, 0:2 * HID], lhs[:, k, i * P:(i + 1) * P],
                                                  wo_hl[:, k, :, :].rearrange("p a n -> p (a n)"),
                                                  start=k == 0 and c == 0, stop=k == NCH - 1 and c == 1)
                mm.then_inc(filled, 1)

            def project(kind, s, j, cur):
                b, parity = cur
                bank_ = claim(kind, b, ("proj", s, j))
                h, low = ln_h[parity], ln_l[parity]
                for c in range(2):
                    wh, wl, ws = (wq_h, wq_l, wq_s) if cross or c == 0 else (wk_h, wk_l, wk_s)
                    head = 2 * s + (c if cross else j)
                    out = bank_[0:QW, c * SEQ:(c + 1) * SEQ]
                    nc.tensor.matmul(out, wh[:, head, :], h[:, 0, :], start=True, stop=False)
                    nc.tensor.matmul(out, wh[:, head, :], low[:, :], start=False, stop=False)
                    nc.tensor.matmul(out, wl[:, head, :], h[:, 0, :], start=False, stop=False)
                    mm = nc.tensor.matmul(out, ws[:, head, :], h[:, 1, :], start=False, stop=True)
                mm.then_inc(filled, 1)

            def find_max(kind, s, step, work, proj_number):
                (b, parity), p = work
                n = p * U + step
                pe.wait_ge(emptied, proj_number + 1)
                after(pe, max_read, b * UB + n - 1)
                if cross:
                    j, t = step // 2, step % 2
                    at = (parity * PAIRS + p) % 4
                    mm = nc.tensor.matmul(max_bank[n % 2][:, :], q_h[0:CDIM, at, j, t * P:(t + 1) * P],
                                          ctx_h[parity][0:CDIM, :], start=True, stop=True)
                else:
                    at = (parity * HEADS + 2 * p + step) % 8
                    for t in range(QT):
                        mm = nc.tensor.matmul(max_bank[n % 2][:, t * SEQ:(t + 1) * SEQ], q_hl[:, at, t * P:(t + 1) * P],
                                              qk_h[:, at, 1, :], start=True, stop=True)
                mm.then_inc(max_filled, 1)

            def score(step, work):
                (b, parity), p = work
                n = p * U + step
                after(pe, exped, b * UB + n - 1)
                out = score_bank[n % 2]
                if cross:
                    at = (parity * PAIRS + p) % 4
                    keys = slice(step * P, (step + 1) * P)
                    nc.tensor.matmul(out[:, :], ctx_h[parity][:, keys], q_h[:, at, :, :], start=True, stop=False)
                    nc.tensor.matmul(out[:, :], ctx_h[parity][0:CDIM, keys], q_l[:, at, :, :], start=False, stop=False)
                    mm = nc.tensor.matmul(out[:, :], ctx_l[parity][:, keys], q_h[0:CDIM, at, :, :], start=False, stop=True)
                else:
                    at = (parity * HEADS + 2 * p + step) % 8
                    for c in range(KT):
                        keys = slice(c * P, (c + 1) * P)
                        nc.tensor.matmul(out[:, c * SEQ:(c + 1) * SEQ], qk_h[:, at, 1, keys], q_hl[:, at, :],
                                         start=True, stop=False)
                        mm = nc.tensor.matmul(out[:, c * SEQ:(c + 1) * SEQ], k_l1[0:96, at, keys], qk_h[0:96, at, 0, :],
                                              start=False, stop=True)
                mm.then_inc(scored, 1)

            def weigh(kind, s, group, work):
                (b, parity), p = work
                j, t = group // QT, group % QT
                if group == 0:
                    pe.wait_ge(probs_split, b * UB + (p + 1) * U)
                    after(pe, attn_ready, b * PAIRS + p)
                    if p == 0:
                        pe.wait_ge(emptied, values_number(kind, b) + 1)
                out = pv_bank[:, group * DV:(group + 1) * DV]
                head = 2 * p + j
                n = 0
                for c in range(KT):
                    unit, col = (c, j * SEQ) if cross else (j, c * SEQ)
                    unit = (p * U + unit) % PR
                    cols = slice(col + t * P, col + (t + 1) * P)
                    hi = probs[:, unit, :].bitcast(BF16)[:, 1::2][:, cols]
                    lo = probs_l[:, unit, cols]
                    for lhs, rhs in ((hi, v_h), (hi, v_l), (lo, v_h)):
                        mm = nc.tensor.matmul(out, lhs, rhs[parity][:, c, head, :], start=n == 0, stop=n == 3 * KT - 1)
                        n += 1
                if group == 3:
                    mm.then_inc(pv_done, 1)

            def slot(kind, s, cur, prev, nxt):
                period = cur[0] if cur is not None else NB
                if cur is not None:
                    if s == 0:
                        pe.wait_ge(ln_ready, cur[0] + 1)
                    project(kind, s, 0, cur)
                if before(s, 2, cur, prev) is not None:
                    p = (s - 2) % PAIRS
                    key = ("mt", "cur" if s >= 2 else "prev", p)
                    bank_ = claim(kind, period, key)
                    b = before(s, 2, cur, prev)[0][0]
                    pe.wait_ge(max_read, b * UB + (p + 1) * U)
                    for t in range(QT):
                        mm = nc.tensor.transpose(bank_[:, t * P:(t + 1) * P], maxima[:, p % 2, t, :], ident[:, :])
                    mm.then_inc(filled, 1)
                for step in range(U):
                    if step == 1 and QU == 2 and cur is not None:
                        project(kind, s, 1, cur)
                    if (work := before(s, 1, cur, prev)) is not None:
                        find_max(kind, s, step, work, proj_number(kind, s, period, 0 if cross else step))
                    if (work := before(s, 3, cur, prev)) is not None:
                        if step == 0:
                            pe.wait_ge(emptied, shift_number(kind, s, period) + 1)
                        score(step, work)
                    if (work := before(s, 4, cur, prev)) is not None:
                        for group in range(step * 4 // U, (step + 1) * 4 // U):
                            weigh(kind, s, group, work)
                    for at, key in extras(kind, s):
                        if at == step:
                            extra(kind, period, key, {"cur": cur, "prev": prev, "nxt": nxt}[key[1]])

            for key in ring.keys["first"][:PRE]:
                extra("first", 0, key, (0, 0))
            periods(pe, slot)


def feed_forward(nc, x, ident, g, be, w1, b1, w2, b2, out_dram):
    name = "ff"
    FCH = DFF // P
    stack = ExitStack()
    with stack:
        def sb(what, shape, dt):
            return stack.enter_context(nc.sbuf_tensor(f"{name}_{what}", shape, dt))

        def bank(what):
            return stack.enter_context(nc.psum_tensor(f"{name}_{what}", [P, 512], F32))

        def sem(what):
            return stack.enter_context(nc.semaphore(f"{name}_{what}"))

        raw_1a, raw_1b = sb("raw_1a", [P, 2 * DFF], F32), sb("raw_1b", [P, 2 * DFF], F32)
        raw_2 = sb("raw_2", [P, FCH, HID], F32)
        w1_h, w1_l, w1_s = (sb(f"w1_{i}", [P, 2 * DFF], F32R) for i in "hls")
        w2_hl = sb("w2_hl", [P, FCH, 2, HID], F32R)
        gain, shift = sb("gain", [P, 2], F32), sb("shift", [P, 2], F32)
        b1_col = sb("b1_col", [P, 2 * FCH], F32)
        b2_row = sb("b2_row", [P, HID], F32)
        half_neg = sb("half_neg", [P, QT], F32)
        eps = sb("eps", [P, QT], F32)
        stats_seen = sb("stats_seen", [P, QT], F32)

        xn = sb("xn", [P, QT, 2, P], F32)
        stats = sb("stats", [P, QT, 6], F32)
        mean_var = sb("mean_var", [P, QT, 2], F32)
        var_eps = sb("var_eps", [P, QT], F32)
        rstd = sb("rstd", [P, QT], F32)
        ln_t = sb("ln_t", [P, 2, SEQ], F32)
        ln_h = [sb(f"ln_h{i}", [P, 2, SEQ], F32R) for i in range(2)]
        ln_l = [sb(f"ln_l{i}", [P, SEQ], F32R) for i in range(2)]
        gated = sb("gated", [P, FCH, SEQ], F32)
        hid = sb("hid", [P, FCH, SEQ], F32)
        hid_h = [sb(f"hid_h{i}", [P, FCH, SEQ], F32R) for i in range(2)]
        hid_l = [sb(f"hid_l{i}", [P, FCH, SEQ], F32R) for i in range(2)]

        ln_bank = bank("ln")
        hid_bank = [bank(f"hid{j}") for j in range(FCH)]
        out_bank = [bank(f"out{t}") for t in range(QT)]

        loaded_1, loaded_2, small = sem("loaded_1"), sem("loaded_2"), sem("small")
        rounded = sem("rounded")
        weights_ready = sem("weights_ready")
        stats_ready = sem("stats_ready")
        var_ready = sem("var_ready")
        var_eps_ready = sem("var_eps_ready")
        rstd_ready = sem("rstd_ready")
        xn_ready = sem("xn_ready")
        turned = sem("turned")
        lnt_ready = sem("lnt_ready")
        ln_hi = sem("ln_hi")
        ln_ready = sem("ln_ready")
        hid_filled = sem("hid_filled")
        gelu_ready = sem("gelu_ready")
        hid_ready = sem("hid_ready")
        hid_hi = sem("hid_hi")
        hid_lo = sem("hid_lo")
        out_filled = sem("out_filled")
        x_b2_ready = sem("x_b2_ready")
        part_ready = sem("part_ready")
        y_ready = sem("y_ready")
        stored = sem("stored")

        block = stack.enter_context(nc.Block())

        def batches(engine, period):
            period((0, 0), None, (1, 1))
            with engine.Fori(0, (NB - 2) // 2) as i:
                for j in (1, 2):
                    b = i * 2 + j
                    period((b, j % 2), (b - 1, 1 - j % 2), (b + 1, 1 - j % 2))
            period((NB - 1, 1), (NB - 2, 0), None)
            period(None, (NB - 1, 1), None)

        @block.sync
        def _(sp):
            sp.dma_start(raw_1a[:, :], w1[0:HA, :]).then_inc(loaded_1, 16)
            load_stacked(sp, raw_1b, w1, loaded_1)
            sp.dma_start(raw_2[:, :, :], w2.rearrange("(k p) n -> p k n", p=P)).then_inc(loaded_2, 16)
            load_vectors(sp, g, be, b2, gain, shift, b2_row, small)
            for c in range(2 * FCH):
                sp.dma_start(b1_col[:, c:c + 1], b1[c * P:(c + 1) * P].rearrange("(p a) -> p a", a=1)).then_inc(small, 16)

            def period(cur, prev, nxt):
                if prev is None:
                    return
                b, parity = prev
                sp.wait_ge(y_ready, b * QT + QT)
                sp.dma_start(out_dram[b, :, :].rearrange("(t p) n -> p t n", p=P),
                             x[:, bass.ds(b * QT, QT), :]).then_inc(stored, 16)

            batches(sp, period)
            sp.wait_ge(stored, 16 * NB)

        @block.gpsimd
        def _(pool):
            pool.wait_ge(weights_ready, 1)
            pool.wait_ge(small, (11 + 2 * FCH) * 16)

            def inverse_root(b):
                pool.wait_ge(var_ready, b + 1)
                nc.gpsimd.tensor_tensor(var_eps[:, :], mean_var[:, :, 1], eps[:, :], ALU.add).then_inc(var_eps_ready, 1)
                pool.wait_ge(var_eps_ready, b + 1)
                nc.gpsimd.tensor_tensor(rstd[:, :], var_eps[:, :], half_neg[:, :], ALU.pow).then_inc(rstd_ready, 1)

            def period(cur, prev, nxt):
                if nxt is not None:
                    inverse_root(nxt[0])
                if prev is not None:
                    rows = x[:, bass.ds(prev[0] * QT, QT), :]
                    nc.gpsimd.tensor_tensor(rows, rows, b2_row[:, None, :].to_broadcast([P, QT, HID]), ALU.add).then_inc(x_b2_ready, 1)
                if cur is not None:
                    b, parity = cur
                    for j in range(FCH):
                        pool.wait_ge(hid_hi, b * FCH + j + 1)
                        nc.gpsimd.tensor_tensor(hid_l[parity][:, j, :], hid[:, j, :], hid_h[parity][:, j, :],
                                                ALU.subtract).then_inc(hid_lo, 1)

            inverse_root(0)
            batches(pool, period)

        @block.scalar
        def _(act):
            act.wait_ge(loaded_1, 5 * 16)
            nc.scalar.copy(w1_h[:, :], raw_1a[:, :])
            nc.scalar.copy(w1_s[:, :], raw_1b[:, :]).then_inc(rounded, 1)
            act.wait_ge(loaded_2, 16)
            nc.scalar.copy(w2_hl[:, :, 0, :], raw_2[:, :, :]).then_inc(rounded, 1)
            act.wait_ge(small, (11 + 2 * FCH) * 16)

            def ln_transposed(b):
                act.wait_ge(turned, b + 1)
                after(act, ln_ready, b)
                for c in range(2):
                    ins = nc.scalar.activation(ln_t[:, c, :], ln_bank[:, c * SEQ:(c + 1) * SEQ], ACT.Identity,
                                               bias=shift[:, c:c + 1], scale=gain[:, c:c + 1])
                ins.then_inc(lnt_ready, 1)

            def gate(b, j):
                act.wait_ge(hid_filled, b * FCH + j + 1)
                nc.scalar.activation(gated[:, j, :], hid_bank[j][:, SEQ:2 * SEQ], ACT.Gelu_apprx_tanh,
                                     bias=b1_col[:, FCH + j:FCH + j + 1]).then_inc(gelu_ready, 1)

            def high(b, parity, j):
                act.wait_ge(hid_ready, b * FCH + j + 1)
                nc.scalar.copy(hid_h[parity][:, j, :], hid[:, j, :]).then_inc(hid_hi, 1)

            def period(cur, prev, nxt):
                if cur is None:
                    return
                b, parity = cur
                for j in range(FCH):
                    gate(b, j)
                    if j == 2 and nxt is not None:
                        ln_transposed(nxt[0])
                    if j >= 1:
                        high(b, parity, j - 1)
                high(b, parity, FCH - 1)

            ln_transposed(0)
            batches(act, period)

        @block.vector
        def _(dve):
            half = slice(P // 2, P)

            def statistics(b):
                for t in range(QT):
                    nc.vector.bn_stats(stats[:, t, :], x[:, b * QT + t, :]).then_inc(stats_ready, 1)
                dve.wait_ge(stats_ready, b * QT + QT)
                nc.vector.tensor_copy(stats_seen[:, :], stats[:, :, 0])
                for t in range(QT):
                    ins = nc.vector.bn_aggr(mean_var[:, t, :], stats[:, t, :])
                ins.then_inc(var_ready, 1)

            def normalise(b):
                dve.wait_ge(rstd_ready, b + 1)
                for t in range(QT):
                    row = x[:, b * QT + t, :]
                    nc.vector.tensor_scalar(xn[:, t, 0, :], row[:, 0:HA], mean_var[:, t, 0:1], rstd[:, t:t + 1],
                                            ALU.subtract, ALU.mult)
                    ins = nc.vector.tensor_scalar(xn[:, t, 1, :].rearrange("p (r f) -> p r f", r=REP),
                                                  row[:, None, HA:HID].to_broadcast([P, REP, HB]),
                                                  mean_var[:, t, 0:1], rstd[:, t:t + 1], ALU.subtract, ALU.mult)
                ins.then_inc(xn_ready, 1)

            def ln_parts(b, parity):
                h, low = ln_h[parity], ln_l[parity]
                dve.wait_ge(lnt_ready, b + 1)
                nc.vector.tensor_copy(h[:, :, :], ln_t[:, :, :]).then_inc(ln_hi, 1)
                dve.wait_ge(ln_hi, b + 1)
                nc.vector.tensor_tensor(low[:, :], ln_t[:, 0, :], h[:, 0, :], ALU.subtract)
                nc.vector.tensor_tensor(h[HB:2 * HB, 1, :], ln_t[HB:2 * HB, 1, :], h[HB:2 * HB, 1, :], ALU.subtract)
                nc.vector.tensor_tensor(h[3 * HB:P, 1, :], ln_t[3 * HB:P, 1, :], h[3 * HB:P, 1, :],
                                        ALU.subtract).then_inc(ln_ready, 1)

            def period(cur, prev, nxt):
                if nxt is not None:
                    statistics(nxt[0])
                for j in range(FCH):
                    if cur is not None:
                        b, parity = cur
                        dve.wait_ge(gelu_ready, b * FCH + j + 1)
                        after(dve, hid_lo, (b - 1) * FCH + j + 1)
                        nc.vector.scalar_tensor_tensor(hid[:, j, :], hid_bank[j][:, 0:SEQ], b1_col[:, j:j + 1],
                                                       gated[:, j, :], ALU.add, ALU.mult).then_inc(hid_ready, 1)
                    if j == 1 and nxt is not None:
                        normalise(nxt[0])
                    if j == 4 and nxt is not None:
                        ln_parts(*nxt)
                    if j in (1, 2) and prev is not None:
                        b, parity = prev
                        t = j - 1
                        dve.wait_ge(x_b2_ready, b + 1)
                        dve.wait_ge(out_filled, b * QT + t + 1)
                        row = x[:, b * QT + t, :]
                        nc.vector.tensor_tensor(row, out_bank[t][:, 0:HID], row, ALU.add).then_inc(part_ready, 1)
                        dve.wait_ge(part_ready, b * QT + t + 1)
                        nc.vector.tensor_tensor(row, out_bank[t][:, HID:2 * HID], row, ALU.add).then_inc(y_ready, 1)

            nc.vector.memset(half_neg[:, :], -0.5)
            nc.vector.memset(eps[:, :], EPS).then_inc(weights_ready, 1)
            statistics(0)
            normalise(0)
            dve.wait_ge(rounded, 1)
            nc.vector.tensor_tensor(w1_l[:, :], raw_1a[:, :], w1_h[:, :], ALU.subtract)
            nc.vector.tensor_tensor(w1_s[half, :], raw_1b[half, :], w1_s[half, :], ALU.subtract)
            dve.wait_ge(rounded, 2)
            nc.vector.tensor_tensor(w2_hl[:, :, 1, :], raw_2[:, :, :], w2_hl[:, :, 0, :], ALU.subtract).then_inc(weights_ready, 1)
            ln_parts(0, 0)
            batches(dve, period)

        @block.tensor
        def _(pe):
            def turn(b):
                pe.wait_ge(xn_ready, b + 1)
                after(pe, lnt_ready, b)
                for c in range(2):
                    for t in range(QT):
                        mm = nc.tensor.transpose(ln_bank[:, c * SEQ + t * P:c * SEQ + (t + 1) * P], xn[:, t, c, :], ident[:, :])
                mm.then_inc(turned, 1)

            def hidden(b, parity, j):
                after(pe, hid_ready, (b - 1) * FCH + j + 1)
                h, low = ln_h[parity], ln_l[parity]
                for c in range(2):
                    col = slice((c * FCH + j) * P, (c * FCH + j + 1) * P)
                    out = hid_bank[j][:, c * SEQ:(c + 1) * SEQ]
                    nc.tensor.matmul(out, w1_h[:, col], h[:, 0, :], start=True, stop=False)
                    nc.tensor.matmul(out, w1_h[:, col], low[:, :], start=False, stop=False)
                    nc.tensor.matmul(out, w1_l[:, col], h[:, 0, :], start=False, stop=False)
                    mm = nc.tensor.matmul(out, w1_s[:, col], h[:, 1, :], start=False, stop=True)
                mm.then_inc(hid_filled, 1)

            def output(b, parity, t):
                pe.wait_ge(hid_lo, (b + 1) * FCH)
                for k in range(FCH):
                    for c, lhs in enumerate((hid_h, hid_l)):
                        mm = nc.tensor.matmul(out_bank[t][:, 0:2 * HID], lhs[parity][:, k, t * P:(t + 1) * P],
                                              w2_hl[:, k, :, :].rearrange("p a n -> p (a n)"),
                                              start=k == 0 and c == 0, stop=k == FCH - 1 and c == 1)
                mm.then_inc(out_filled, 1)

            def period(cur, prev, nxt):
                for j in range(FCH):
                    if cur is not None:
                        if j == 0:
                            pe.wait_ge(ln_ready, cur[0] + 1)
                        hidden(*cur, j)
                    if j in (1, 2) and prev is not None:
                        output(*prev, j - 1)
                    if j == 2 and nxt is not None:
                        turn(nxt[0])

            turn(0)
            pe.wait_ge(weights_ready, 2)
            batches(pe, period)


AH, AD, APAD = 8, 20, 32
APAIRS = AH // 2
TOK = 4
KEYS = CTX - TOK
AV = AD + 1
HT = AH * TOK


def shape_constants():
    head_of = np.arange(HID) // AD
    index = np.linspace(0, CDIM - 1, SEQ).astype(np.int64)
    parts = {
        "ident": np.eye(P),
        "pick": np.arange(P)[:, None] == index[None, :],
        "ht_mask": (np.arange(P)[:, None] % HT // TOK) == np.arange(AH)[None, :],
        "ht_feature": (np.arange(P)[:, None] // TOK) == head_of[None, :],
        "feature_a": head_of[:HA, None] == np.arange(AH)[None, :],
        "feature_b": np.tile(head_of[HA:, None] == np.arange(AH)[None, :], (REP, 1)),
        "neg_eye": -1.0 * (np.arange(P)[:, None] - CDIM == np.arange(AH)[None, :]),
    }
    columns, at = {}, 0
    for what, part in parts.items():
        columns[what] = (at, part.shape[1])
        at += part.shape[1]
    return np.concatenate([np.asarray(v, np.float32) for v in parts.values()], axis=1), columns


def adapter_queries(nc, x, const, ctx_dram, wq, wq_ca, wk_ca, wv_ca, wout, branch):
    name = "aq"
    SCALE = float(AD) ** -0.5
    stack = ExitStack()
    with stack:
        def sb(what, shape, dt):
            return stack.enter_context(nc.sbuf_tensor(f"{name}_{what}", shape, dt))

        def bank(what):
            return stack.enter_context(nc.psum_tensor(f"{name}_{what}", [P, 512], F32))

        def sem(what):
            return stack.enter_context(nc.semaphore(f"{name}_{what}"))

        wq_pad = sb("wq_pad", [P, 2, AH, APAD], F32)
        wk_pad = sb("wk_pad", [CDIM, AH, APAD], F32)
        wqca = sb("wqca", [TOK, HID + 3 * HB], F32)
        wv = sb("wv", [CDIM, HID], F32)
        wo = sb("wo", [P, 2, HID], F32)
        wqt = sb("wqt", [P, 2, HID], F32)
        wkt = sb("wkt", [P, 2, CDIM], F32)
        qk = sb("qk", [CDIM, AH, HID], F32)
        wqca_t = sb("wqca_t", [P, 2, TOK], F32)
        diag = sb("diag", [P, 2, 4, HT], F32)
        diag_h = sb("diag_h", [P, 2, 4, HT], F32R)
        diag_l = sb("diag_l", [P, 4, HT], F32R)
        c_rep = sb("c_rep", [3 * HT, NB, CDIM], F32)
        c_s = sb("c_s", [3 * HT, NB, CDIM], F32R)
        c_t = sb("c_t", [CDIM, NB, HT], F32)
        g2 = sb("g2", [P, 2, NB, HT], F32)
        v2 = sb("v2", [HT, NB, HID], F32)
        two = range(2)
        xr = [sb(f"xr{i}", [P, QT, 2, P], F32) for i in two]
        x_h = [sb(f"x_h{i}", [P, 2, SEQ], F32R) for i in two]
        x_l = [sb(f"x_l{i}", [P, SEQ], F32R) for i in two]
        r_s = [sb(f"r_s{i}", [P, SEQ], F32R) for i in two]
        c_m = [sb(f"c_m{i}", [P, AH, CDIM], F32R) for i in two]
        maxima = [sb(f"maxima{i}", [CDIM, P], F32) for i in two]
        xv_h = [sb(f"xv_h{i}", [P, QT, AH, AV], BF16) for i in two]
        xv_l = [sb(f"xv_l{i}", [P, QT, AH, AV], F16) for i in two]
        probs = [sb(f"probs{i}", [P, QT, AH * CDIM], F32) for i in two]
        probs_l = [sb(f"probs_l{i}", [P, QT, AH * CDIM], F16) for i in two]
        recip = [sb(f"recip{i}", [CDIM, AH], F32) for i in two]
        hs1 = [sb(f"hs1{i}", [CDIM, HID], F32) for i in two]
        hs1_t = [sb(f"hs1_t{i}", [P, 2, CDIM], F32) for i in two]
        top2 = [sb(f"top2{i}", [CDIM, AH], F32) for i in two]
        s2 = [sb(f"s2{i}", [CDIM, AH, TOK], F32) for i in two]
        p2 = [sb(f"p2{i}", [CDIM, AH, TOK], F32) for i in two]
        sum2 = [sb(f"sum2{i}", [CDIM, AH], F32) for i in two]
        rec2 = [sb(f"rec2{i}", [CDIM, AH], F32) for i in two]
        p2n = [sb(f"p2n{i}", [CDIM, AH, TOK], F32) for i in two]
        p2_t = [sb(f"p2_t{i}", [HT, CDIM], F32) for i in two]
        hs2_t = [sb(f"hs2_t{i}", [P, 2, CDIM], F32) for i in two]

        turn_bank, row_bank = bank("turn"), bank("row")
        max_bank = [bank(f"max{i}") for i in two]
        score_bank = [bank(f"score{i}") for i in two]
        pv_bank, chain_bank = bank("pv"), bank("chain")
        tile_bank = [max_bank[0], max_bank[1], pv_bank, chain_bank]

        loaded = sem("loaded")
        zeroed = sem("zeroed")
        setup_pe = sem("setup_pe")
        setup_dve = sem("setup_dve")
        ready = sem("ready")
        xr_ready = sem("xr_ready")
        x_turned = sem("x_turned")
        x_hi = sem("x_hi")
        x_ready = sem("x_ready")
        r_filled = sem("r_filled")
        r_hi = sem("r_hi")
        r_ready = sem("r_ready")
        cm_ready = sem("cm_ready")
        max_filled = sem("max_filled")
        max_read = sem("max_read")
        mt_filled = sem("mt_filled")
        shift_ready = sem("shift_ready")
        scored = sem("scored")
        exped = sem("exped")
        probs_split = sem("probs_split")
        xv_hi = sem("xv_hi")
        xv_ready = sem("xv_ready")
        pv_done = sem("pv_done")
        recip_ready = sem("recip_ready")
        hs1_ready = sem("hs1_ready")
        chain_filled = sem("chain_filled")
        chain_read = sem("chain_read")
        soft2 = sem("soft2")
        exp2 = sem("exp2")
        p2_ready = sem("p2_ready")
        branch_hi = sem("branch_hi")

        block = stack.enter_context(nc.Block())
        STEPS = NB + 4

        @block.sync
        def _(sp):
            sp.wait_ge(zeroed, 1)
            for h in range(AH):
                cols = slice(h * AD, (h + 1) * AD)
                sp.dma_start(wq_pad[:, 0, h, 0:AD], wq[0:HA, cols]).then_inc(loaded, 16)
                sp.dma_start(wq_pad[0:HB, 1, h, 0:AD], wq[HA:HID, cols]).then_inc(loaded, 16)
                sp.dma_start(wk_pad[:, h, 0:AD], wk_ca[:, cols]).then_inc(loaded, 16)
            sp.dma_start(wqca[:, 0:HID], wq_ca).then_inc(loaded, 16)
            for r in range(3):
                sp.dma_start(wqca[:, HID + r * HB:HID + (r + 1) * HB], wq_ca[:, HA:HID]).then_inc(loaded, 16)
            sp.dma_start(wv[:, :], wv_ca).then_inc(loaded, 16)
            sp.dma_start(wo[:, 0, :], wout[0:HA, :]).then_inc(loaded, 16)
            sp.dma_start(wo[0:HB, 1, :], wout[HA:HID, :]).then_inc(loaded, 16)
            for r in range(3 * AH):
                sp.dma_start(c_rep[r * TOK:(r + 1) * TOK, :, :],
                             ctx_dram[:, KEYS:CTX, :].rearrange("b t c -> t b c")).then_inc(loaded, 16)
        LOADS = 3 * AH + 7 + 3 * AH

        @block.gpsimd
        def _(pool):
            nc.gpsimd.memset(wq_pad[:, :, :, :], 0.0)
            nc.gpsimd.memset(wk_pad[:, :, :], 0.0).then_inc(zeroed, 1)

            def mask_tokens(b):
                after(pool, scored, (b - 2) * 4 + 4)
                nc.gpsimd.tensor_tensor(c_m[b % 2][0:3 * HT, :, :], c_s[:, b, None, :].to_broadcast([3 * HT, AH, CDIM]),
                                        const["ht_mask"][0:3 * HT, :, None].to_broadcast([3 * HT, AH, CDIM]),
                                        ALU.mult).then_inc(cm_ready, 1)

            def split(b):
                for n in range(4):
                    pool.wait_ge(exped, b * 4 + n + 1)
                    t, cols = n // 2, slice(n % 2 * 4 * CDIM, (n % 2 + 1) * 4 * CDIM)
                    whole = probs[b % 2][:, t, cols]
                    nc.gpsimd.tensor_tensor(probs_l[b % 2][:, t, cols], whole, whole.bitcast(BF16)[:, 1::2],
                                            ALU.subtract).then_inc(probs_split, 1)

            pool.wait_ge(ready, 1)
            for step in range(STEPS):
                if 0 <= step - 2 < NB:
                    split(step - 2)
                if step < NB:
                    mask_tokens(step)

        @block.scalar
        def _(act):
            def x_part(b):
                act.wait_ge(x_turned, b + 1)
                nc.scalar.copy(x_h[b % 2][:, :, :], turn_bank[:, :].rearrange("p (c q) -> p c q", c=2)).then_inc(x_hi, 1)

            def value_part(b):
                after(act, pv_done, b - 1)
                nc.scalar.copy(xv_h[b % 2][:, :, :, 0:AD],
                               x[:, b * QT:(b + 1) * QT, :].rearrange("p t (h d) -> p t h d", d=AD)).then_inc(xv_hi, 1)

            def row_part(b):
                act.wait_ge(r_filled, b + 1)
                after(act, scored, (b - 1) * 4)
                nc.scalar.copy(r_s[b % 2][0:3 * HT, :], row_bank[0:3 * HT, 0:SEQ]).then_inc(r_hi, 1)

            def exponentials(b):
                after(act, pv_done, b - 1)
                for n in range(4):
                    act.wait_ge(scored, b * 4 + n + 1)
                    nc.scalar.activation(probs[b % 2][:, n // 2, n % 2 * 4 * CDIM:(n % 2 + 1) * 4 * CDIM],
                                         score_bank[n % 2][:, 0:4 * CDIM], ACT.Exp, scale=SCALE).then_inc(exped, 1)

            def second_scores(b):
                act.wait_ge(chain_filled, b * 5 + 1)
                nc.scalar.copy(hs1_t[b % 2][:, 0, :], chain_bank[:, 0:CDIM])
                nc.scalar.copy(hs1_t[b % 2][0:HB, 1, :], chain_bank[0:HB, CDIM:2 * CDIM]).then_inc(chain_read, 1)
                act.wait_ge(soft2, b * 4 + 2)
                nc.scalar.activation(p2[b % 2][:, :, :], s2[b % 2][:, :, :], ACT.Exp, scale=SCALE).then_inc(exp2, 1)

            def second_values(b):
                act.wait_ge(chain_filled, b * 5 + 3)
                nc.scalar.copy(p2_t[b % 2][:, :], chain_bank[0:HT, 0:CDIM]).then_inc(chain_read, 1)
                act.wait_ge(chain_filled, b * 5 + 4)
                nc.scalar.copy(hs2_t[b % 2][:, 0, :], chain_bank[:, 0:CDIM])
                nc.scalar.copy(hs2_t[b % 2][0:HB, 1, :], chain_bank[0:HB, CDIM:2 * CDIM]).then_inc(chain_read, 1)
                act.wait_ge(chain_filled, b * 5 + 5)
                nc.scalar.copy(branch[:, b, 0, :], chain_bank[0:CDIM, 0:HID]).then_inc(branch_hi, 1)

            act.wait_ge(ready, 1)
            for step in range(STEPS):
                for lag, part in ((0, x_part), (1, value_part), (4, second_values), (2, exponentials), (0, row_part),
                                  (3, second_scores)):
                    if 0 <= step - lag < NB:
                        part(step - lag)

        @block.vector
        def _(dve):
            count = [0]

            def told(ins):
                count[0] += 1
                ins.then_inc(setup_dve, 1)

            half = slice(P // 2, P)
            dve.wait_ge(loaded, LOADS * 16)
            told(nc.vector.tensor_copy(c_s[:, :, :], c_rep[:, :, :]))
            dve.wait_ge(setup_dve, 1)
            told(nc.vector.tensor_tensor(c_s[HT:2 * HT, :, :], c_rep[HT:2 * HT, :, :], c_s[HT:2 * HT, :, :], ALU.subtract))
            for i in two:
                nc.vector.memset(r_s[i][3 * HT:P, :].bitcast(F32), 1.0)
                nc.vector.memset(maxima[i][:, :], 0.0)
                nc.vector.memset(xv_h[i][:, :, :, AD:AV], 1.0)
                nc.vector.memset(xv_l[i][:, :, :, AD:AV], 0.0)
            nc.vector.memset(diag[:, :, :, :], 0.0)
            for k in two:
                dve.wait_ge(setup_pe, k + 1)
                nc.vector.tensor_copy(wqt[:, k, :], score_bank[k][:, 0:HID])
                told(nc.vector.tensor_copy(wkt[:, k, :], score_bank[k][:, HID:HID + CDIM]))
            dve.wait_ge(setup_pe, 3)
            told(nc.vector.tensor_copy(wqca_t[:, :, :], turn_bank[:, 0:2 * TOK].rearrange("p (c t) -> p c t", c=2)))
            dve.wait_ge(setup_pe, 4)
            told(nc.vector.tensor_copy(c_t[:, :, :], row_bank[0:CDIM, 0:NB * HT].rearrange("p (b r) -> p b r", b=NB)))
            dve.wait_ge(setup_dve, 5)
            for i, m in enumerate(("feature_a", "feature_b")):
                for r in range(3):
                    ins = nc.vector.tensor_tensor(diag[:, i, r, :].rearrange("p (h t) -> p h t", t=TOK),
                                                  wqca_t[:, i, None, :].to_broadcast([P, AH, TOK]),
                                                  const[m][:, :, None].to_broadcast([P, AH, TOK]), ALU.mult)
            told(ins)
            dve.wait_ge(setup_dve, 7)
            told(nc.vector.tensor_copy(diag_h[:, :, :, :], diag[:, :, :, :]))
            dve.wait_ge(setup_dve, 8)
            nc.vector.tensor_tensor(diag_l[:, :, :], diag[:, 0, :, :], diag_h[:, 0, :, :], ALU.subtract)
            told(nc.vector.tensor_tensor(diag_h[half, 1, :, :], diag[half, 1, :, :], diag_h[half, 1, :, :], ALU.subtract))
            for n in range(4):
                dve.wait_ge(setup_pe, 5 + n)
                told(nc.vector.tensor_copy(qk[:, n::4, :],
                                           tile_bank[n][0:CDIM, 0:2 * HID].rearrange("p (h e) -> p h e", e=HID)))
            dve.wait_ge(setup_pe, 9)
            for i in two:
                rows = slice(0, P if i == 0 else HB)
                ins = nc.vector.tensor_copy(g2[rows, i, :, :].rearrange("p b (h t) -> p b h t", t=TOK),
                                            score_bank[i][rows, 0:AH * NB * TOK].rearrange("p (h b t) -> p b h t", h=AH, b=NB))
            told(ins)
            for n, b in enumerate(range(0, NB, 3)):
                batches = min(3, NB - b)
                dve.wait_ge(setup_pe, 10 + n)
                ins = nc.vector.tensor_tensor(v2[:, b:b + batches, :],
                                              [turn_bank, row_bank, chain_bank][n][0:HT, 0:batches * HID].rearrange("p (b e) -> p b e", e=HID),
                                              const["ht_feature"][0:HT, None, :].to_broadcast([HT, batches, HID]), ALU.mult)
            told(ins)
            dve.wait_ge(setup_dve, count[0])
            nc.vector.memset(recip[0][:, :], 0.0).then_inc(ready, 1)

            def a0(b):
                after(dve, x_turned, b - 1)
                nc.vector.tensor_copy(xr[b % 2][:, :, 0, :], x[:, b * QT:(b + 1) * QT, 0:HA])
                nc.vector.tensor_copy(xr[b % 2][:, :, 1, :].rearrange("p t (r f) -> p t r f", r=REP),
                                      x[:, b * QT:(b + 1) * QT, None, HA:HID].to_broadcast([P, QT, REP, HB])).then_inc(xr_ready, 1)

            def x_part(b):
                i = b % 2
                dve.wait_ge(x_hi, b + 1)
                nc.vector.tensor_tensor(x_l[i][:, :], turn_bank[:, 0:SEQ], x_h[i][:, 0, :], ALU.subtract)
                nc.vector.tensor_tensor(x_h[i][HB:2 * HB, 1, :], turn_bank[HB:2 * HB, SEQ:2 * SEQ], x_h[i][HB:2 * HB, 1, :], ALU.subtract)
                nc.vector.tensor_tensor(x_h[i][3 * HB:P, 1, :], turn_bank[3 * HB:P, SEQ:2 * SEQ], x_h[i][3 * HB:P, 1, :],
                                        ALU.subtract).then_inc(x_ready, 1)

            def value_part(b):
                dve.wait_ge(xv_hi, b + 1)
                nc.vector.tensor_tensor(xv_l[b % 2][:, :, :, 0:AD],
                                        x[:, b * QT:(b + 1) * QT, :].rearrange("p t (h d) -> p t h d", d=AD),
                                        xv_h[b % 2][:, :, :, 0:AD], ALU.subtract).then_inc(xv_ready, 1)

            def row_part(b):
                rows = slice(2 * HT, 3 * HT)
                dve.wait_ge(r_hi, b + 1)
                nc.vector.tensor_tensor(r_s[b % 2][rows, :], row_bank[rows, 0:SEQ], r_s[b % 2][rows, :],
                                        ALU.subtract).then_inc(r_ready, 1)

            def top(b):
                for n in range(APAIRS):
                    dve.wait_ge(max_filled, b * APAIRS + n + 1)
                    nc.vector.reduce_max(maxima[b % 2][:, CDIM + 2 * n:CDIM + 2 * n + 2],
                                         max_bank[n % 2][0:CDIM, :].rearrange("p (h k) -> p h k", h=2), AX.X).then_inc(max_read, 1)

            def write_shift(b):
                dve.wait_ge(mt_filled, b + 1)
                rows = slice(CDIM, P)
                nc.vector.tensor_tensor(c_m[b % 2][rows, :, :], row_bank[rows, None, 0:CDIM].to_broadcast([P - CDIM, AH, CDIM]),
                                        const["neg_eye"][rows, :, None].to_broadcast([P - CDIM, AH, CDIM]), ALU.mult).then_inc(shift_ready, 1)

            def norm(b):
                dve.wait_ge(pv_done, b + 1)
                sums = pv_bank[0:CDIM, 0:AH * AV].rearrange("p (h d) -> p h d", d=AV)
                nc.vector.reciprocal(recip[b % 2][:, :], sums[:, :, AD]).then_inc(recip_ready, 1)
                dve.wait_ge(recip_ready, b + 1)
                nc.vector.tensor_tensor(hs1[b % 2][:, :].rearrange("p (h d) -> p h d", d=AD), sums[:, :, 0:AD],
                                        recip[b % 2][:, :, None].to_broadcast([CDIM, AH, AD]), ALU.mult).then_inc(hs1_ready, 1)

            def second_scores(b):
                i, n = b % 2, b * 4
                scores = chain_bank[0:CDIM, 0:HT].rearrange("p (h t) -> p h t", t=TOK)
                dve.wait_ge(chain_filled, b * 5 + 2)
                nc.vector.reduce_max(top2[i][:, :], scores, AX.X).then_inc(soft2, 1)
                dve.wait_ge(soft2, n + 1)
                nc.vector.tensor_tensor(s2[i][:, :, :], scores, top2[i][:, :, None].to_broadcast([CDIM, AH, TOK]),
                                        ALU.subtract).then_inc(soft2, 1)
                dve.wait_ge(exp2, b + 1)
                nc.vector.reduce_sum(sum2[i][:, :], p2[i][:, :, :], AX.X).then_inc(soft2, 1)
                dve.wait_ge(soft2, n + 3)
                nc.vector.reciprocal(rec2[i][:, :], sum2[i][:, :]).then_inc(soft2, 1)
                dve.wait_ge(soft2, n + 4)
                nc.vector.tensor_tensor(p2n[i][:, :, :], p2[i][:, :, :], rec2[i][:, :, None].to_broadcast([CDIM, AH, TOK]),
                                        ALU.mult).then_inc(p2_ready, 1)

            def branch_part(b):
                dve.wait_ge(branch_hi, b + 1)
                nc.vector.tensor_tensor(branch[:, b, 1, :], chain_bank[0:CDIM, 0:HID], branch[:, b, 0, :],
                                        ALU.subtract).then_inc(chain_read, 1)

            a0(0)
            for step in range(STEPS):
                for lag, part in ((-1, a0), (0, x_part), (1, top), (4, branch_part), (0, row_part), (1, value_part),
                                  (1, write_shift), (3, second_scores), (2, norm)):
                    if 0 <= step - lag < NB:
                        part(step - lag)

        @block.tensor
        def _(pe):
            ident = const["ident"]
            pe.wait_ge(loaded, LOADS * 16)
            for k in two:
                heads = slice(4 * k, 4 * k + 4)
                out = score_bank[k]
                nc.tensor.transpose(out[:, 0:HA], wq_pad[:, 0, heads, :].rearrange("p h d -> p (h d)"), ident)
                nc.tensor.transpose(out[:, HA:HID], wq_pad[0:HB, 1, heads, :].rearrange("p h d -> p (h d)"), ident[0:HB, 0:HB])
                nc.tensor.transpose(out[:, HID:HID + CDIM], wk_pad[:, heads, :].rearrange("p h d -> p (h d)"),
                                    ident[0:CDIM, 0:CDIM]).then_inc(setup_pe, 1)
            nc.tensor.transpose(turn_bank[:, 0:TOK], wqca[:, 0:HA], ident[0:TOK, 0:TOK])
            nc.tensor.transpose(turn_bank[:, TOK:2 * TOK], wqca[:, HA:HA + P], ident[0:TOK, 0:TOK]).then_inc(setup_pe, 1)
            for b in range(NB):
                mm = nc.tensor.transpose(row_bank[0:CDIM, b * HT:(b + 1) * HT], c_rep[0:HT, b, :], ident[0:HT, 0:HT])
            mm.then_inc(setup_pe, 1)
            pe.wait_ge(setup_dve, 4)
            for n in range(4):
                rows = slice(n * APAD, (n + 1) * APAD)
                for k in two:
                    mm = nc.tensor.matmul(tile_bank[n][0:CDIM, k * HID:(k + 1) * HID], wkt[rows, k, :], wqt[rows, k, :],
                                          start=True, stop=True)
                mm.then_inc(setup_pe, 1)
            pe.wait_ge(setup_dve, 13)
            for h in range(AH):
                cols = slice(h * NB * TOK, (h + 1) * NB * TOK)
                nc.tensor.matmul(score_bank[0][:, cols], qk[:, h, 0:HA], c_t[:, :, 0:TOK], start=True, stop=True)
                mm = nc.tensor.matmul(score_bank[1][0:HB, cols], qk[:, h, HA:HID], c_t[:, :, 0:TOK], start=True, stop=True)
            mm.then_inc(setup_pe, 1)
            for n, b0 in enumerate(range(0, NB, 3)):
                out = [turn_bank, row_bank, chain_bank][n]
                for b in range(b0, min(b0 + 3, NB)):
                    mm = nc.tensor.matmul(out[0:HT, (b - b0) * HID:(b - b0 + 1) * HID], c_t[:, b, :], wv[:, :], start=True, stop=True)
                mm.then_inc(setup_pe, 1)
            pe.wait_ge(ready, 1)

            def a(b):
                i = b % 2
                pe.wait_ge(xr_ready, b + 1)
                after(pe, x_ready, b)
                for c in range(2):
                    for t in range(QT):
                        mm = nc.tensor.transpose(turn_bank[:, c * SEQ + t * P:c * SEQ + (t + 1) * P], xr[i][:, t, c, :], ident)
                mm.then_inc(x_turned, 1)

            def rows(b):
                i = b % 2
                pe.wait_ge(x_ready, b + 1)
                after(pe, shift_ready, b - 1)
                after(pe, r_ready, b)
                out = row_bank[:, 0:SEQ]
                passes = [(diag_h[:, 0], x_h[i][:, 0, :]), (diag_h[:, 0], x_l[i][:, :]), (diag_l[:, :, :], x_h[i][:, 0, :]),
                          (diag_h[:, 1], x_h[i][:, 1, :])]
                for n, (lhs, rhs) in enumerate(passes):
                    mm = nc.tensor.matmul(out, lhs.rearrange("p r c -> p (r c)"), rhs, start=n == 0, stop=n == 3)
                mm.then_inc(r_filled, 1)

            def top(b):
                i = b % 2
                pe.wait_ge(r_ready, b + 1)
                pe.wait_ge(cm_ready, b + 1)
                for n in range(APAIRS):
                    after(pe, max_read, b * APAIRS + n - 1)
                    for j in range(2):
                        mm = nc.tensor.matmul(max_bank[n % 2][0:CDIM, j * SEQ:(j + 1) * SEQ], c_m[i][0:3 * HT, 2 * n + j, :],
                                              r_s[i][0:3 * HT, :], start=True, stop=True)
                    mm.then_inc(max_filled, 1)

            def top_turned(b):
                pe.wait_ge(max_read, (b + 1) * APAIRS)
                pe.wait_ge(r_ready, min(b + 2, NB))
                nc.tensor.transpose(row_bank[:, 0:CDIM], maxima[b % 2][:, :], ident[0:CDIM, 0:CDIM]).then_inc(mt_filled, 1)

            def score(b):
                i = b % 2
                pe.wait_ge(shift_ready, b + 1)
                for n in range(4):
                    after(pe, exped, b * 4 + n - 1)
                    t, heads = n // 2, slice(n % 2 * 4, n % 2 * 4 + 4)
                    nc.tensor.matmul(score_bank[n % 2][:, 0:4 * CDIM], r_s[i][:, t * P:(t + 1) * P], c_m[i][:, heads, :],
                                     start=True, stop=True).then_inc(scored, 1)

            def weigh(b):
                i = b % 2
                pe.wait_ge(probs_split, b * 4 + 4)
                pe.wait_ge(xv_ready, b + 1)
                after(pe, hs1_ready, b)
                for h in range(AH):
                    n = 0
                    for t in range(QT):
                        cols = slice(h * CDIM, (h + 1) * CDIM)
                        hi = probs[i][:, t, :].bitcast(BF16)[:, 1::2][:, cols]
                        for lhs, rhs in ((hi, xv_h), (hi, xv_l), (probs_l[i][:, t, cols], xv_h)):
                            mm = nc.tensor.matmul(pv_bank[0:CDIM, h * AV:(h + 1) * AV], lhs, rhs[i][:, t, h, :],
                                                  start=n == 0, stop=n == 3 * QT - 1)
                            n += 1
                mm.then_inc(pv_done, 1)

            def link(b, n):
                after(pe, chain_read, b * 4 + n)

            def d1(b):
                pe.wait_ge(hs1_ready, b + 1)
                link(b, 0)
                nc.tensor.transpose(chain_bank[:, 0:CDIM], hs1[b % 2][:, 0:HA], ident[0:CDIM, 0:CDIM])
                nc.tensor.transpose(chain_bank[0:HB, CDIM:2 * CDIM], hs1[b % 2][:, HA:HID], ident[0:CDIM, 0:CDIM]).then_inc(chain_filled, 1)

            def d2(b):
                link(b, 1)
                out = chain_bank[0:CDIM, 0:HT]
                nc.tensor.matmul(out, hs1_t[b % 2][:, 0, :], g2[:, 0, b, :], start=True, stop=False)
                nc.tensor.matmul(out, hs1_t[b % 2][0:HB, 1, :], g2[0:HB, 1, b, :], start=False, stop=True).then_inc(chain_filled, 1)

            def e1(b):
                pe.wait_ge(p2_ready, b + 1)
                nc.tensor.transpose(chain_bank[0:HT, 0:CDIM], p2n[b % 2][:, :, :].rearrange("p h t -> p (h t)"),
                                    ident[0:CDIM, 0:CDIM]).then_inc(chain_filled, 1)

            def e2(b):
                link(b, 2)
                nc.tensor.matmul(chain_bank[:, 0:CDIM], v2[:, b, 0:HA], p2_t[b % 2][:, :], start=True, stop=True)
                nc.tensor.matmul(chain_bank[0:HB, CDIM:2 * CDIM], v2[:, b, HA:HID], p2_t[b % 2][:, :], start=True,
                                 stop=True).then_inc(chain_filled, 1)

            def e3(b):
                link(b, 3)
                out = chain_bank[0:CDIM, 0:HID]
                nc.tensor.matmul(out, hs2_t[b % 2][:, 0, :], wo[:, 0, :], start=True, stop=False)
                nc.tensor.matmul(out, hs2_t[b % 2][0:HB, 1, :], wo[0:HB, 1, :], start=False, stop=True).then_inc(chain_filled, 1)

            for step in range(STEPS):
                live = lambda k: 0 <= step - k < NB
                if live(0):
                    a(step)
                if live(4):
                    e1(step - 4)
                if live(1):
                    top(step - 1)
                if live(4):
                    e2(step - 4)
                if live(0):
                    rows(step)
                if live(4):
                    e3(step - 4)
                if live(2):
                    score(step - 2)
                if live(3):
                    d1(step - 3)
                if live(1):
                    top_turned(step - 1)
                if live(3):
                    d2(step - 3)
                if live(2):
                    weigh(step - 2)


def load_padded(engine, wq, wk, wq_pad, wk_pad, semaphore):
    for h in range(AH):
        cols = slice(h * AD, (h + 1) * AD)
        engine.dma_start(wq_pad[:, 0, h, 0:AD], wq[0:HA, cols]).then_inc(semaphore, 16)
        engine.dma_start(wq_pad[0:HB, 1, h, 0:AD], wq[HA:HID, cols]).then_inc(semaphore, 16)
        engine.dma_start(wk_pad[:, h, 0:AD], wk[:, cols]).then_inc(semaphore, 16)


def prepare_adapter(nc, const, wq, wk, wv, wout, b_out, wq_h, wq_l, wq_s, wv_h, wv_l, wo_a, wo_b, pick, bo_row):
    name = "ap"
    stack = ExitStack()
    with stack:
        def sb(what, shape, dt):
            return stack.enter_context(nc.sbuf_tensor(f"{name}_{what}", shape, dt))

        def sem(what):
            return stack.enter_context(nc.semaphore(f"{name}_{what}"))

        wq_pad, wk_pad = sb("wq_pad", [P, 2, AH, APAD], F32), sb("wk_pad", [CDIM, AH, APAD], F32)
        wv_pad = sb("wv_pad", [CDIM, AH, APAD], F32)
        raw_o = sb("raw_o", [P, 2, HID], F32)
        B4, A, K, W = 0, P, 2 * P, 2 * P + CDIM
        w_t = sb("w_t", [P, 2, W], F32)
        turned = [stack.enter_context(nc.psum_tensor(f"{name}_turned{i}", [P, 512], F32)) for i in range(2)]
        prod = [stack.enter_context(nc.psum_tensor(f"{name}_prod{i}", [P, 512], F32)) for i in range(4)]
        zeroed = sem("zeroed")
        loaded_qk, loaded_v, loaded_o = sem("loaded_qk"), sem("loaded_v"), sem("loaded_o")
        turned_done = sem("turned_done")
        turned_read = sem("turned_read")
        prod_done = sem("prod_done")
        prod_hi = sem("prod_hi")
        rounded = sem("rounded")

        with nc.Block() as block:
            @block.gpsimd
            def _(pool):
                for t in (wq_pad[:, :, :, :], wk_pad[:, :, :], wv_pad[:, :, :]):
                    nc.gpsimd.memset(t, 0.0).then_inc(zeroed, 1)

            @block.sync
            def _(sp):
                sp.wait_ge(zeroed, 3)
                load_padded(sp, wq, wk, wq_pad, wk_pad, loaded_qk)
                for h in range(AH):
                    sp.dma_start(wv_pad[:, h, 0:AD], wv[:, h * AD:(h + 1) * AD]).then_inc(loaded_v, 16)
                sp.dma_start(raw_o[:, 0, :], wout[0:HA, :]).then_inc(loaded_o, 16)
                for r in range(2):
                    sp.dma_start(raw_o[r * HB:(r + 1) * HB, 1, :], wout[HA:HID, :]).then_inc(loaded_o, 16)
                sp.dma_start(bo_row[:, :], b_out.rearrange("(a n) -> a n", a=1).to_broadcast([P, HID])).then_inc(loaded_o, 16)

            @block.tensor
            def _(pe):
                ident = const["ident"]
                pe.wait_ge(loaded_qk, 3 * AH * 16)
                for k in range(2):
                    heads, out = slice(4 * k, 4 * k + 4), turned[k]
                    nc.tensor.transpose(out[:, 0:HB], wq_pad[0:HB, 1, heads, :].rearrange("p h d -> p (h d)"), ident[0:HB, 0:HB])
                    nc.tensor.transpose(out[:, HB:HID], wq_pad[:, 0, heads, :].rearrange("p h d -> p (h d)"), ident)
                    nc.tensor.transpose(out[:, HID:HID + CDIM], wk_pad[:, heads, :].rearrange("p h d -> p (h d)"),
                                        ident[0:CDIM, 0:CDIM]).then_inc(turned_done, 1)
                pe.wait_ge(turned_read, 2)
                for n in range(4):
                    rows = slice(n * APAD, (n + 1) * APAD)
                    for k in range(2):
                        for c, part in enumerate((slice(A, K), slice(B4, A))):
                            at = (2 * k + c) * CDIM
                            mm = nc.tensor.matmul(prod[n][:, at:at + CDIM], w_t[rows, k, part], w_t[rows, k, K:W],
                                                  start=True, stop=True)
                    mm.then_inc(prod_done, 1)

            def product(n, c):
                return prod[n][:, 0:4 * CDIM].rearrange("p (k c e) -> p k c e", k=2, c=2)[:, :, c, :]

            @block.scalar
            def _(act):
                act.wait_ge(loaded_v, AH * 16)
                nc.scalar.copy(wv_h[:, :], wv_pad[:, :, :].rearrange("p h d -> p (h d)")).then_inc(rounded, 1)
                act.wait_ge(loaded_o, 4 * 16)
                nc.scalar.copy(wo_a[:, 0, :], raw_o[:, 0, :])
                nc.scalar.copy(wo_b[:, 0, :], raw_o[0:2 * HB, 1, :]).then_inc(rounded, 1)
                for n in range(4):
                    act.wait_ge(prod_done, n + 1)
                    nc.scalar.copy(wq_h[:, n::4, :], product(n, 0))
                    nc.scalar.copy(wq_s[:, n::4, :], product(n, 1)).then_inc(prod_hi, 1)

            @block.vector
            def _(dve):
                nc.vector.tensor_copy(pick[:, :], const["pick"][0:CDIM, :])
                for k in range(2):
                    dve.wait_ge(turned_done, k + 1)
                    nc.vector.tensor_copy(w_t[:, k, B4:A].rearrange("p (r f) -> p r f", r=REP),
                                          turned[k][:, None, 0:HB].to_broadcast([P, REP, HB]))
                    nc.vector.tensor_copy(w_t[:, k, A:W], turned[k][:, HB:HID + CDIM]).then_inc(turned_read, 1)
                dve.wait_ge(rounded, 1)
                nc.vector.tensor_tensor(wv_l[:, :], wv_pad[:, :, :].rearrange("p h d -> p (h d)"), wv_h[:, :], ALU.subtract)
                dve.wait_ge(rounded, 2)
                nc.vector.tensor_tensor(wo_a[:, 1, :], raw_o[:, 0, :], wo_a[:, 0, :], ALU.subtract)
                nc.vector.tensor_tensor(wo_b[:, 1, :], raw_o[0:2 * HB, 1, :], wo_b[:, 0, :], ALU.subtract)
                half = slice(P // 2, P)
                for n in range(4):
                    dve.wait_ge(prod_hi, n + 1)
                    nc.vector.tensor_tensor(wq_l[:, n::4, :], product(n, 0), wq_h[:, n::4, :], ALU.subtract)
                    nc.vector.tensor_tensor(wq_s[half, n::4, :], product(n, 1)[half], wq_s[half, n::4, :], ALU.subtract)


def adapter(nc, x, const, ctx_dram, wq, wk, wv, wout, b_out, branch):
    name = "ad"
    SLOTS = 2 * APAIRS
    PERIODS = NB // 2
    END = SLOTS - 2
    KT = CTX // P
    KEY_ROWS = [P] * (KT - 1) + [KEYS - (KT - 1) * P]
    U = KT
    UP = U * SLOTS
    PR = 2 * U
    SCALE = float(AD) ** -0.5

    def extras(kind, s):
        prev, cur, nxt = kind != "first", kind != "tail", kind in ("first", "steady")
        table = {0: [(1, prev, ("ot", "prev", 0)), (2, cur, ("v", "cur", 0))],
                 1: [(0, prev, ("out", "prev", 0)), (2, prev, ("out", "prev", 1))],
                 2: [(0, cur, ("x", "cur", 1)), (2, cur, ("v", "cur", 1))],
                 3: [(1, cur, ("ctx", "cur", 1))],
                 4: [(1, prev, ("ot", "prev", 1)), (2, cur, ("v", "cur", 2))],
                 5: [(0, prev, ("out", "prev", 2)), (2, prev, ("out", "prev", 3)), (3, nxt, ("x", "nxt", 0))],
                 6: [(2, cur, ("v", "cur", 3))],
                 7: [(1, nxt, ("ctx", "nxt", 0))]}
        return [(at, key) for at, live, key in table[s] if live]

    def slot_keys(kind, s):
        keys = [] if kind == "tail" else [("proj", s)]
        if (kind != "tail") if s >= 2 else (kind != "first"):
            keys.append(("mt", s))
        return keys + [key for _, key in extras(kind, s)]

    def all_keys(kind):
        pre = [("ctx", "pre", 0), ("x", "pre", 0)] if kind == "first" else []
        return pre + [k for s in range(END if kind == "tail" else SLOTS) for k in slot_keys(kind, s)]

    ring = Ring(all_keys, PERIODS)

    def earlier(kind, period, key):
        return ring.number("last", PERIODS - 1, key) if kind == "tail" else ring.number("steady", period - 1, key)

    def unit_of(kind, s, period, what, lag):
        if s >= lag:
            return ring.number(kind, period, (what, s - lag))
        return earlier(kind, period, (what, s - lag + SLOTS))

    def context_number(kind, period, j):
        if j == 1:
            return ring.number(kind, period, ("ctx", "cur", 1))
        return 0 if kind == "first" else earlier(kind, period, ("ctx", "nxt", 0))

    def before(s, d, cur, prev):
        if s >= d:
            return None if cur is None else (cur, s - d)
        return None if prev is None else (prev, s - d + SLOTS)

    def run(slot):
        def whole(kind, r, prev, nxt):
            for s in range(SLOTS):
                slot(kind, s, r, r, prev, nxt)

        def program(engine):
            whole("first", 0, None, 1)
            with engine.Fori(0, PERIODS - 2) as i:
                whole("steady", i + 1, i, i + 2)
            whole("last", PERIODS - 1, PERIODS - 2, None)
            for s in range(END):
                slot("tail", s, PERIODS, None, PERIODS - 1, None)
        return program

    def batch_of(key, cur, prev, nxt):
        what, whose, i = key
        j = i // 2 if what in ("v", "out") else i
        return {"pre": 0, "cur": cur, "prev": prev, "nxt": nxt}[whose] * 2 + j, j

    stack = ExitStack()
    with stack:
        def sb(what, shape, dt):
            return stack.enter_context(nc.sbuf_tensor(f"{name}_{what}", shape, dt))

        def bank(what):
            return stack.enter_context(nc.psum_tensor(f"{name}_{what}", [P, 512], F32))

        def sem(what):
            return stack.enter_context(nc.semaphore(f"{name}_{what}"))

        wq_h, wq_l, wq_s = (sb(f"wq_{i}", [P, AH, CDIM], F32R) for i in "hls")
        wv_h, wv_l = (sb(f"wv_{i}", [CDIM, AH * APAD], F32R) for i in "hl")
        wo_a = sb("wo_a", [P, 2, HID], F32R)
        wo_b = sb("wo_b", [2 * HB, 2, HID], F32R)
        pick = sb("pick", [CDIM, SEQ], F32R)
        bo_row = sb("bo_row", [P, HID], F32)
        prepare_adapter(nc, const, wq, wk, wv, wout, b_out, wq_h, wq_l, wq_s, wv_h, wv_l, wo_a, wo_b, pick, bo_row)

        two = range(2)
        xr = sb("xr", [P, QT, 2, P], F32)
        x_h = [sb(f"x_h{j}", [P, 2, SEQ], F32R) for j in two]
        x_l = [sb(f"x_l{j}", [P, SEQ], F32R) for j in two]
        ctx_rows = [sb(f"ctx_rows{j}", [P, KT, CDIM], F32) for j in two]
        ctx_h = [sb(f"ctx_h{j}", [P, CTX], F32R) for j in two]
        ctx_l = [sb(f"ctx_l{j}", [CDIM, CTX], F32R) for j in two]
        v_h = [sb(f"v_h{j}", [P, KT, AH, AV], BF16) for j in two]
        v_l = [sb(f"v_l{j}", [P, KT, AH, AV], F16) for j in two]
        attn = [sb(f"attn{j}", [P, QT, HID], F32) for j in two]
        q_h = sb("q_h", [P, 4, 2, SEQ], F32R)
        q_l = sb("q_l", [CDIM, 4, 2, SEQ], F32R)
        maxima = sb("maxima", [P, 2, QT, P], F32)
        probs = sb("probs", [P, PR, 512], F32)
        probs_l = sb("probs_l", [P, PR, 512], F16)
        recip = sb("recip", [P, 4], F32)
        attn_th = sb("attn_th", [P, SEQ], F32R)
        attn_tl = sb("attn_tl", [P, SEQ], F32R)
        attn_tb = sb("attn_tb", [2 * HB, SEQ], F32R)

        shared = [bank(f"shared{i}") for i in range(Ring.BANKS)]
        max_bank = [bank(f"max{i}") for i in range(2)]
        score_bank = [bank(f"score{i}") for i in range(2)]
        pv_bank = bank("pv")

        rows_in = [sem(f"rows_in{i}") for i in two]
        consts = sem("consts")
        filled = sem("filled")
        emptied = sem("emptied")
        xr_ready = sem("xr_ready")
        x_hi = sem("x_hi")
        ctx_hi = sem("ctx_hi")
        v_hi = sem("v_hi")
        q_hi = sem("q_hi")
        max_filled = sem("max_filled")
        max_read = sem("max_read")
        scored = sem("scored")
        exped = sem("exped")
        probs_split = sem("probs_split")
        pv_done = sem("pv_done")
        recip_ready = sem("recip_ready")
        attn_ready = sem("attn_ready")
        attn_hi = sem("attn_hi")
        x_bo_ready = sem("x_bo_ready")
        part_ready = sem("part_ready")

        block = stack.enter_context(nc.Block())

        @block.sync
        def _(sp):
            def rows(b, j):
                sp.dma_start(ctx_rows[j][:, :, :],
                             ctx_dram[b, :, :].rearrange("(t p) c -> p t c", p=P)).then_inc(rows_in[j], 16)

            rows(0, 0)
            rows(1, 1)
            with sp.Fori(0, PERIODS - 1) as r:
                for j in two:
                    b = r * 2 + j
                    sp.wait_ge(ctx_hi, b + 1)
                    rows(b + 2, j)

        @block.gpsimd
        def _(pool):
            def slot(kind, s, period, cur, prev, nxt):
                if s in (0, 4) and prev is not None:
                    b = prev * 2 + s // 4
                    rows = x[:, bass.ds(b * QT, QT), :]
                    nc.gpsimd.tensor_tensor(rows, rows, bo_row[:, None, :].to_broadcast([P, QT, HID]), ALU.add).then_inc(x_bo_ready, 1)
                if (work := before(s, 3, cur, prev)) is not None:
                    r, v = work
                    for u in range(U):
                        n, rows = v * U + u, slice(0, KEY_ROWS[u])
                        pool.wait_ge(exped, r * UP + n + 1)
                        whole = probs[rows, n % PR, :]
                        nc.gpsimd.tensor_tensor(probs_l[rows, n % PR, :], whole, whole.bitcast(BF16)[:, 1::2],
                                                ALU.subtract).then_inc(probs_split, 1)

            run(slot)(pool)

        @block.scalar
        def _(act):
            def extra(kind, period, key, batch):
                (b, j), (what, _, i) = batch, key
                if what == "out":
                    return
                act.wait_ge(filled, ring.number(kind, period, key) + 1)
                bank_ = shared[ring.bank(kind, key)]
                if what == "x":
                    nc.scalar.copy(x_h[j][:, :, :], bank_[:, :].rearrange("p (c q) -> p c q", c=2)).then_inc(x_hi, 1)
                elif what == "ctx":
                    nc.scalar.copy(ctx_h[j][0:CDIM, :], bank_[0:CDIM, :]).then_inc(ctx_hi, 1)
                elif what == "v":
                    t = i % 2 * 2
                    for c in range(2):
                        ins = nc.scalar.copy(v_h[j][:, t + c, :, 0:AD], bank_[:, c * SEQ:(c + 1) * SEQ].rearrange(
                            "p (h d) -> p h d", d=APAD)[:, :, 0:AD])
                    ins.then_inc(v_hi, 1)
                elif what == "ot":
                    nc.scalar.copy(attn_th[:, :], bank_[:, 0:SEQ])
                    nc.scalar.copy(attn_tb[0:HB, :], bank_[0:HB, SEQ:2 * SEQ]).then_inc(attn_hi, 1)

            def slot(kind, s, period, cur, prev, nxt):
                if cur is not None:
                    act.wait_ge(filled, ring.number(kind, period, ("proj", s)) + 1)
                    after(act, scored, cur * UP + (s - 3) * U)
                    nc.scalar.copy(q_h[0:CDIM, s % 4, :, :],
                                   shared[ring.bank(kind, ("proj", s))][0:CDIM, :].rearrange("p (h q) -> p h q", h=2)).then_inc(q_hi, 1)
                for step in range(U):
                    if (work := before(s, 3, cur, prev)) is not None:
                        r, v = work
                        n, rows = v * U + step, slice(0, KEY_ROWS[step])
                        act.wait_ge(scored, r * UP + n + 1)
                        after(act, pv_done, r * SLOTS + v - 1)
                        nc.scalar.activation(probs[rows, n % PR, :], score_bank[n % 2][rows, :], ACT.Exp,
                                             scale=SCALE).then_inc(exped, 1)
                    for at, key in extras(kind, s):
                        if at == step:
                            extra(kind, period, key, batch_of(key, cur, prev, nxt))

            extra("first", 0, ("ctx", "pre", 0), (0, 0))
            extra("first", 0, ("x", "pre", 0), (0, 0))
            run(slot)(act)

        @block.vector
        def _(dve):
            nc.vector.memset(maxima[:, :, :, :], 0.0)
            for j in two:
                nc.vector.memset(v_h[j][:, :, :, AD:AV], 1.0)
                nc.vector.memset(v_l[j][:, :, :, AD:AV], 0.0)
                ins = nc.vector.memset(ctx_h[j][CDIM:P, :].bitcast(F32), 1.0)
            ins.then_inc(consts, 1)

            def lay_out(b):
                tiles = x[:, bass.ds(b * QT, QT), :]
                nc.vector.tensor_copy(xr[:, :, 0, :], tiles[:, :, 0:HA])
                for t in range(QT):
                    ins = nc.vector.tensor_copy(xr[:, t, 1, :].rearrange("p (r f) -> p r f", r=REP),
                                                x[:, b * QT + t, None, HA:HID].to_broadcast([P, REP, HB]))
                ins.then_inc(xr_ready, 1)

            def extra(kind, period, key, batch):
                (b, j), (what, _, i) = batch, key
                bank_ = shared[ring.bank(kind, key)]
                if what == "x":
                    dve.wait_ge(x_hi, b + 1)
                    nc.vector.tensor_tensor(x_l[j][:, :], bank_[:, 0:SEQ], x_h[j][:, 0, :], ALU.subtract)
                    for rows in (slice(HB, 2 * HB), slice(3 * HB, P)):
                        ins = nc.vector.tensor_tensor(x_h[j][rows, 1, :], bank_[rows, SEQ:2 * SEQ], x_h[j][rows, 1, :], ALU.subtract)
                    ins.then_inc(emptied, 1)
                elif what == "ctx":
                    dve.wait_ge(ctx_hi, b + 1)
                    nc.vector.tensor_tensor(ctx_l[j][:, :], bank_[0:CDIM, :], ctx_h[j][0:CDIM, :],
                                            ALU.subtract).then_inc(emptied, 1)
                elif what == "v":
                    t = i % 2 * 2
                    dve.wait_ge(v_hi, b * 2 + i % 2 + 1)
                    for c in range(2):
                        ins = nc.vector.tensor_tensor(v_l[j][:, t + c, :, 0:AD], bank_[:, c * SEQ:(c + 1) * SEQ].rearrange(
                            "p (h d) -> p h d", d=APAD)[:, :, 0:AD], v_h[j][:, t + c, :, 0:AD], ALU.subtract)
                    ins.then_inc(emptied, 1)
                elif what == "ot":
                    dve.wait_ge(attn_hi, b + 1)
                    nc.vector.tensor_tensor(attn_tl[:, :], bank_[:, 0:SEQ], attn_th[:, :], ALU.subtract)
                    nc.vector.tensor_tensor(attn_tb[HB:2 * HB, :], bank_[0:HB, SEQ:2 * SEQ], attn_tb[0:HB, :],
                                            ALU.subtract).then_inc(emptied, 1)
                elif what == "out":
                    t = i % 2
                    dve.wait_ge(x_bo_ready, b + 1)
                    dve.wait_ge(filled, ring.number(kind, period, key) + 1)
                    row = x[:, b * QT + t, :]
                    nc.vector.tensor_tensor(row, bank_[:, 0:HID], row, ALU.add).then_inc(part_ready, 1)
                    dve.wait_ge(part_ready, b * QT + t + 1)
                    nc.vector.tensor_tensor(row, bank_[:, HID:2 * HID], row, ALU.add).then_inc(emptied, 1)

            def slot(kind, s, period, cur, prev, nxt):
                if cur is not None:
                    dve.wait_ge(q_hi, cur * SLOTS + s + 1)
                    nc.vector.tensor_tensor(q_l[:, s % 4, :, :],
                                            shared[ring.bank(kind, ("proj", s))][0:CDIM, :].rearrange("p (h q) -> p h q", h=2),
                                            q_h[0:CDIM, s % 4, :, :], ALU.subtract).then_inc(emptied, 1)
                if (work := before(s, 2, cur, prev)) is not None:
                    bank_, rows = shared[ring.bank(kind, ("mt", s))], slice(CDIM, P)
                    dve.wait_ge(filled, ring.number(kind, period, ("mt", s)) + 1)
                    nc.vector.tensor_tensor(q_h[rows, work[1] % 4, :, :], bank_[rows, None, 0:SEQ].to_broadcast([P - CDIM, 2, SEQ]),
                                            const["neg_eye"][rows, 0:2, None].to_broadcast([P - CDIM, 2, SEQ]),
                                            ALU.mult).then_inc(emptied, 1)
                for step in range(U):
                    if (work := before(s, 1, cur, prev)) is not None:
                        r, v = work
                        n = v * U + step
                        at = CDIM + step // 2
                        dve.wait_ge(max_filled, r * UP + n + 1)
                        nc.vector.reduce_max(maxima[:, v % 2, step % 2, at:at + 1], max_bank[n % 2][:, 0:KEYS],
                                             AX.X).then_inc(max_read, 1)
                    for at, key in extras(kind, s):
                        if at == step:
                            extra(kind, period, key, batch_of(key, cur, prev, nxt))
                if s == 1 and cur is not None:
                    lay_out(cur * 2 + 1)
                if s == 4 and nxt is not None:
                    lay_out(nxt * 2)
                if (work := before(s, 4, cur, prev)) is not None:
                    r, v = work
                    dve.wait_ge(pv_done, r * SLOTS + v + 1)
                    groups = pv_bank[:, 0:4 * AV]
                    nc.vector.reciprocal(recip[:, :], groups.rearrange("p (g d) -> p g d", d=AV)[:, :, AD]).then_inc(recip_ready, 1)
                    dve.wait_ge(recip_ready, r * SLOTS + v + 1)
                    head = v % APAIRS * 2
                    out = attn[v // APAIRS][:, :, head * AD:(head + 2) * AD].rearrange("p t (h d) -> p h t d", h=2)
                    nc.vector.tensor_tensor(out, groups.rearrange("p (h t d) -> p h t d", h=2, t=QT)[:, :, :, 0:AD],
                                            recip[:, :].rearrange("p (h t) -> p h t", h=2)[:, :, :, None].to_broadcast([P, 2, QT, AD]),
                                            ALU.mult).then_inc(attn_ready, 1)

            lay_out(0)
            extra("first", 0, ("ctx", "pre", 0), (0, 0))
            extra("first", 0, ("x", "pre", 0), (0, 0))
            run(slot)(dve)

        @block.tensor
        def _(pe):
            ident = const["ident"]
            pe.wait_ge(consts, 1)

            def claim(kind, period, key):
                back = ring.back(kind, key)
                if back is not None:
                    after(pe, emptied, ring.number(kind, period, key) - back + 1)
                return shared[ring.bank(kind, key)]

            def extra(kind, period, key, batch):
                (b, j), (what, _, i) = batch, key
                if what == "x":
                    pe.wait_ge(xr_ready, b + 1)
                    bank_ = claim(kind, period, key)
                    for c in range(2):
                        for t in range(QT):
                            mm = nc.tensor.transpose(bank_[:, c * SEQ + t * P:c * SEQ + (t + 1) * P], xr[:, t, c, :], ident)
                elif what == "ctx":
                    pe.wait_ge(rows_in[j], (b - j) * 8 + 16)
                    bank_ = claim(kind, period, key)
                    for t in range(KT):
                        mm = nc.tensor.transpose(bank_[0:CDIM, t * P:(t + 1) * P], ctx_rows[j][:, t, :], ident)
                elif what == "v":
                    pe.wait_ge(emptied, context_number(kind, period, j) + 1)
                    bank_ = claim(kind, period, key)
                    for c in range(2):
                        t = i % 2 * 2 + c
                        tok, out = slice(t * P, (t + 1) * P), bank_[:, c * SEQ:(c + 1) * SEQ]
                        nc.tensor.matmul(out, ctx_h[j][0:CDIM, tok], wv_h[:, :], start=True, stop=False)
                        nc.tensor.matmul(out, ctx_l[j][:, tok], wv_h[:, :], start=False, stop=False)
                        mm = nc.tensor.matmul(out, ctx_h[j][0:CDIM, tok], wv_l[:, :], start=False, stop=True)
                elif what == "ot":
                    pe.wait_ge(attn_ready, b * APAIRS + APAIRS)
                    bank_ = claim(kind, period, key)
                    for t in range(QT):
                        nc.tensor.transpose(bank_[:, t * P:(t + 1) * P], attn[j][:, t, 0:HA], ident)
                        mm = nc.tensor.transpose(bank_[0:HB, SEQ + t * P:SEQ + (t + 1) * P], attn[j][:, t, HA:HID], ident)
                elif what == "out":
                    bank_ = claim(kind, period, key)
                    pe.wait_ge(emptied, ring.number(kind, period, ("ot", "prev", j)) + 1)
                    cols, out = slice(i % 2 * P, (i % 2 + 1) * P), bank_[:, 0:2 * HID]
                    for n, (lhs, rhs) in enumerate(((attn_th, wo_a), (attn_tl, wo_a), (attn_tb, wo_b))):
                        nc.tensor.matmul(out, lhs[:, cols], rhs[:, :, :].rearrange("p a n -> p (a n)"), start=n == 0, stop=False)
                    mm = nc.tensor.matmul(out, pick[:, cols], branch[:, b, :, :].rearrange("p a n -> p (a n)"), start=False, stop=True)
                mm.then_inc(filled, 1)

            def project(kind, s, period):
                j = s // APAIRS
                if s % APAIRS == 0:
                    if j == 1:
                        number = ring.number(kind, period, ("x", "cur", 1))
                    else:
                        number = ring.number("first", 0, ("x", "pre", 0)) if kind == "first" else earlier(kind, period, ("x", "nxt", 0))
                    pe.wait_ge(emptied, number + 1)
                bank_ = claim(kind, period, ("proj", s))
                for c in range(2):
                    head = s % APAIRS * 2 + c
                    out = bank_[0:CDIM, c * SEQ:(c + 1) * SEQ]
                    nc.tensor.matmul(out, wq_h[:, head, :], x_h[j][:, 0, :], start=True, stop=False)
                    nc.tensor.matmul(out, wq_h[:, head, :], x_l[j][:, :], start=False, stop=False)
                    nc.tensor.matmul(out, wq_l[:, head, :], x_h[j][:, 0, :], start=False, stop=False)
                    mm = nc.tensor.matmul(out, wq_s[:, head, :], x_h[j][:, 1, :], start=False, stop=True)
                mm.then_inc(filled, 1)

            def find_max(kind, s, step, period, work):
                r, v = work
                n, j, t = v * U + step, v // APAIRS, step % 2
                pe.wait_ge(emptied, unit_of(kind, s, period, "proj", 1) + 1)
                after(pe, max_read, r * UP + n - 1)
                nc.tensor.matmul(max_bank[n % 2][:, 0:KEYS], q_h[0:CDIM, v % 4, step // 2, t * P:(t + 1) * P],
                                 ctx_h[j][0:CDIM, 0:KEYS], start=True, stop=True).then_inc(max_filled, 1)

            def score(kind, s, step, period, work):
                r, v = work
                n, j = v * U + step, v // APAIRS
                if step == 0:
                    pe.wait_ge(emptied, unit_of(kind, s, period, "mt", 1) + 1)
                after(pe, exped, r * UP + n - 1)
                out = score_bank[n % 2][0:KEY_ROWS[step], :]
                keys = slice(step * P, step * P + KEY_ROWS[step])
                nc.tensor.matmul(out, ctx_h[j][:, keys], q_h[:, v % 4, :, :], start=True, stop=False)
                nc.tensor.matmul(out, ctx_h[j][0:CDIM, keys], q_l[:, v % 4, :, :], start=False, stop=False)
                nc.tensor.matmul(out, ctx_l[j][:, keys], q_h[0:CDIM, v % 4, :, :], start=False, stop=True).then_inc(scored, 1)

            def weigh(kind, s, group, period, work):
                r, v = work
                j = v // APAIRS
                if group == 0:
                    pe.wait_ge(probs_split, r * UP + (v + 1) * U)
                    after(pe, attn_ready, r * SLOTS + v)
                    if v % APAIRS == 0:
                        number = earlier(kind, period, ("v", "cur", 3)) if j else ring.number(kind, period, ("v", "cur", 1))
                        pe.wait_ge(emptied, number + 1)
                head, col = v % APAIRS * 2 + group // QT, group * P
                out = pv_bank[:, group * AV:(group + 1) * AV]
                n = 0
                for c in range(KT):
                    rows, unit = slice(0, KEY_ROWS[c]), (v * U + c) % PR
                    hi = probs[rows, unit, :].bitcast(BF16)[:, 1::2][:, col:col + P]
                    lo = probs_l[rows, unit, col:col + P]
                    for lhs, rhs in ((hi, v_h), (hi, v_l), (lo, v_h)):
                        mm = nc.tensor.matmul(out, lhs, rhs[j][rows, c, head, :], start=n == 0, stop=n == 3 * KT - 1)
                        n += 1
                if group == 3:
                    mm.then_inc(pv_done, 1)

            def slot(kind, s, period, cur, prev, nxt):
                if cur is not None:
                    project(kind, s, period)
                if (work := before(s, 2, cur, prev)) is not None:
                    r, v = work
                    bank_ = claim(kind, period, ("mt", s))
                    pe.wait_ge(max_read, r * UP + (v + 1) * U)
                    for t in range(QT):
                        mm = nc.tensor.transpose(bank_[:, t * P:(t + 1) * P], maxima[:, v % 2, t, :], ident)
                    mm.then_inc(filled, 1)
                for step in range(U):
                    if (work := before(s, 1, cur, prev)) is not None:
                        find_max(kind, s, step, period, work)
                    if (work := before(s, 3, cur, prev)) is not None:
                        score(kind, s, step, period, work)
                    if (work := before(s, 4, cur, prev)) is not None:
                        weigh(kind, s, step, period, work)
                    for at, key in extras(kind, s):
                        if at == step:
                            extra(kind, period, key, batch_of(key, cur, prev, nxt))

            extra("first", 0, ("ctx", "pre", 0), (0, 0))
            extra("first", 0, ("x", "pre", 0), (0, 0))
            run(slot)(pe)


def build(nc, columns, shapes, a, out):
    l0 = {n[len("L0_xattn_"):]: v for n, v in a.items() if n.startswith("L0_xattn_")}
    l1 = {n[len("L1_xattn_"):]: v for n, v in a.items() if n.startswith("L1_xattn_")}
    stack = ExitStack()
    with stack:
        x = stack.enter_context(nc.sbuf_tensor("x_rows", [P, NT, HID], F32))
        ident = stack.enter_context(nc.sbuf_tensor("ident", [P, P], F32))
        start = stack.enter_context(nc.semaphore("start"))
        adapter_stack = stack.enter_context(ExitStack())
        consts = adapter_stack.enter_context(nc.sbuf_tensor("shape_consts", list(shapes), F32))
        branch = adapter_stack.enter_context(nc.sbuf_tensor("branch", [CDIM, NB, 2, HID], F32R))

        with nc.Block() as block:
            @block.sync
            def _(sp):
                sp.dma_start(consts[:, :], a["shapes"]).then_inc(start, 16)
                sp.dma_start(x[:, :, :], a["x"].rearrange("b (t p) h -> p (b t) h", p=P)).then_inc(start, 16)
                at, width = columns["ident"]
                sp.dma_start(ident[:, :], a["shapes"][:, at:at + width]).then_inc(start, 16)
                sp.wait_ge(start, 3 * 16)

        const = {what: consts[:, at:at + width] for what, (at, width) in columns.items()}
        context = a["ctx_768"]
        with adapter_stack:
            adapter_queries(nc, x, const, context, l0["Wq"], l0["Wq_ca"], l0["Wk_ca"], l0["Wv_ca"], l0["Wout"], branch)
            adapter(nc, x, const, context, l0["Wq"], l0["Wk"], l0["Wv"], l0["Wout"], l0["b_out"], branch)
        attention(nc, "self", False, x, ident, context, *(l1[w] for w in ("g1", "be1", "wq1", "wk1", "wv1", "wo1", "bo1")))
        attention(nc, "cross", True, x, ident, context, *(l1[w] for w in ("g2", "be2", "wq2", "wk2", "wv2", "wo2", "bo2")))
        feed_forward(nc, x, ident, *(l1[w] for w in ("g3", "be3", "w_ff1", "b_ff1", "w_ff2", "b_ff2")), out)


def kernel(**inputs):
    import concourse.bacc as bacc
    from concourse.bass_utils import run_bass_kernel_spmd

    nc = bacc.Bacc("TRN2", target_bir_lowering=False, num_devices=1)
    arrays = {name: np.ascontiguousarray(v) for name, v in inputs.items()}
    arrays["shapes"], columns = shape_constants()
    drams = {name: nc.dram_tensor(f"in_{name}", v.shape, mybir.dt.from_np(v.dtype), kind="ExternalInput").ap()
             for name, v in arrays.items()}
    out = nc.dram_tensor("out", (NB, SEQ, HID), F32, kind="ExternalOutput").ap()
    build(nc, columns, arrays["shapes"].shape, drams, out)
    result = run_bass_kernel_spmd(nc, [{f"in_{name}": v for name, v in arrays.items()}], core_ids=[0])
    return result.results[0]["out"]
```

```python
from contextlib import ExitStack

import numpy as np

import concourse.bass as bass
from concourse import mybir

F32 = mybir.dt.float32
F32R = mybir.dt.float32r
BF16 = mybir.dt.bfloat16
F16 = mybir.dt.float16
ACT = mybir.ActivationFunctionType
ALU = mybir.AluOpType
AX = mybir.AxisListType

P = 128
NB, SEQ, HID = 8, 256, 160
QT = SEQ // P
NT = NB * QT
HA, HB = P, HID - P
REP = P // HB
CTX, CDIM = 512, 96
HEADS, DH = 20, 64
INNER = HEADS * DH
PAIRS = HEADS // 2
NCH = INNER // P
DFF = 640
EPS = 1e-5
DV = DH + 1


def after(engine, semaphore, count):
    if isinstance(count, int) and count <= 0:
        return
    engine.wait_ge(semaphore, count)


class Ring:

    BANKS = 3
    BEFORE = {"first": (), "steady": ("first", "steady"), "last": ("steady",), "tail": ("last",)}

    def __init__(self, units, periods=NB, apart=()):
        self.periods, self.apart = periods, apart
        self.keys = {kind: units(kind) for kind in ("first", "steady", "last", "tail")}

    def count(self, kind, period, pos, which=None):
        def of(keys):
            return sum(which is None or (key[0] in self.apart) == which for key in keys)

        here = of(self.keys[kind][:pos])
        first, steady, last = (of(self.keys[k]) for k in ("first", "steady", "last"))
        if kind == "first":
            return here
        if kind == "tail":
            return first + (self.periods - 2) * steady + last + here
        return (period - 1) * steady + first + here

    def number(self, kind, period, key):
        return self.count(kind, period, self.keys[kind].index(key))

    def bank(self, kind, key):
        return self.keys[kind].index(key) % self.BANKS

    def read(self, kind, period, key):
        return self.count(kind, period, self.keys[kind].index(key) + 1, False)

    def free(self, kind, period, key):
        keys, pos = self.keys[kind], self.keys[kind].index(key)
        if pos >= self.BANKS:
            pos -= self.BANKS
            user_apart = keys[pos][0] in self.apart
            n = self.count(kind, period, pos + 1, user_apart)
            return (0, n) if user_apart else (n, 0)
        back = []
        for before in self.BEFORE[kind]:
            n = len(self.keys[before])
            back += [n - q for q in range(n) if q % self.BANKS == pos][-1:]
        if not back:
            return 0, 0
        later = self.keys[self.BEFORE[kind][-1]][-min(back):][1:]
        apart = sum(key[0] in self.apart for key in later)
        return (self.count(kind, period, 0, False) - (len(later) - apart),
                self.count(kind, period, 0, True) - apart if self.apart else 0)


def periods(engine, slot):
    for s in range(PAIRS):
        slot("first", s, (0, 0), None, (1, 1))
    with engine.Fori(0, (NB - 2) // 2) as i:
        for j in (1, 2):
            b = i * 2 + j
            for s in range(PAIRS):
                slot("steady", s, (b, j % 2), (b - 1, 1 - j % 2), (b + 1, 1 - j % 2))
    for s in range(PAIRS):
        slot("last", s, (NB - 1, 1), (NB - 2, 0), None)
    for s in range(TAIL):
        slot("tail", s, None, (NB - 1, 1), None)


TAIL = 8


def load_stacked(engine, out, w, semaphore):
    engine.dma_start(out, w[HA:HID, :][None, :, :].to_broadcast([REP, HB, w.shape[1]])).then_inc(semaphore, 16)


VECTORS = 5


def load_vectors(engine, g, be, bo, gain, shift, bo_row, semaphore):
    for out, v in ((gain, g), (shift, be)):
        column = v.rearrange("(p a) -> p a", a=1)
        engine.dma_start(out[:, 0:1], column[0:HA, :]).then_inc(semaphore, 16)
        load_stacked(engine, out[:, 1:2], column, semaphore)
    engine.dma_start(bo_row[:, :], bo.rearrange("(a n) -> a n", a=1).to_broadcast([P, HID])).then_inc(semaphore, 16)


class SelfWeights:

    PIECES = (("q", "a"), ("q", "b"), ("k", "a"), ("k", "b"), ("v", "a"), ("v", "b"), ("o", "a"))

    def __init__(self, nc, stack, dram):
        def sb(what, shape, dt):
            return stack.enter_context(nc.sbuf_tensor(f"sw_{what}", shape, dt))

        self.nc, self.dram = nc, dram
        self.qk = [sb(f"wqk_{i}", [P, HEADS, 2 * DH], F32R) for i in "hls"]
        self.v = [sb(f"wv_{i}", [P, INNER], F32R) for i in "hls"]
        self.wo_hl = sb("wo_hl", [P, NCH, 2, HID], F32R)
        self.gain = sb("gain", [P, 2], F32)
        self.shift = sb("shift", [P, 2], F32)
        self.bo_row = sb("bo_row", [P, HID], F32)
        self.loaded = [stack.enter_context(nc.semaphore(f"sw_loaded{i}")) for i in range(2)]
        self.vectors = stack.enter_context(nc.semaphore("sw_vectors"))
        self.rounded = stack.enter_context(nc.semaphore("sw_rounded"))
        self.split = stack.enter_context(nc.semaphore("sw_split"))

    def allocate_raw(self, stack):
        raw = stack.enter_context(self.nc.sbuf_tensor("sw_raw", [P, 2 * INNER], F32))
        self.raw = {"a": raw[:, 0:INNER], "b": raw[:, INNER:2 * INNER]}
        self.raw_o = raw[:, 0:NCH * HID].rearrange("p (k n) -> p k n", k=NCH)

    def load(self, engine):
        d = self.dram
        load_vectors(engine, d["g"], d["be"], d["bo"], self.gain, self.shift, self.bo_row, self.vectors)
        for n, w in enumerate("qkv"):
            after(engine, self.split, 2 * n - 1)
            engine.dma_start(self.raw["a"], d["w" + w][0:HA, :]).then_inc(self.loaded[0], 16)
            after(engine, self.split, 2 * n)
            load_stacked(engine, self.raw["b"], d["w" + w], self.loaded[1])
        engine.wait_ge(self.split, 6)
        engine.dma_start(self.raw_o, d["wo"].rearrange("(k p) n -> p k n", p=P)).then_inc(self.loaded[0], 16)
        engine.wait_ge(self.vectors, VECTORS * 16)

    def operands(self, n):
        w, part = self.PIECES[n]
        if w == "o":
            return self.raw_o, self.wo_hl[:, :, 0, :], self.wo_hl[:, :, 1, :], slice(0, P)
        raw = self.raw[part]
        rows = slice(0, P) if part == "a" else slice(P // 2, P)
        if w == "v":
            parts = [t[:, :] for t in self.v]
        else:
            raw = raw.rearrange("p (h d) -> p h d", d=DH)
            parts = [t[:, :, :].rearrange("p h (a d) -> p h a d", a=2)[:, :, "qk".index(w), :] for t in self.qk]
        high, low, stacked = parts
        return (raw, high, low, rows) if part == "a" else (raw, stacked, stacked, rows)

    def high(self, engine, n):
        w, part = self.PIECES[n]
        engine.wait_ge(self.loaded["ab".index(part)], ("qkvo".index(w) + 1) * 16)
        raw, high, _, _ = self.operands(n)
        self.nc.scalar.copy(high, raw).then_inc(self.rounded, 1)

    def low(self, engine, n):
        engine.wait_ge(self.rounded, n + 1)
        raw, high, low, rows = self.operands(n)
        self.nc.vector.tensor_tensor(low[rows], raw[rows], high[rows], ALU.subtract).then_inc(self.split, 1)


class CrossRaw:

    def __init__(self, nc, stack, dram):
        def sb(what, shape):
            return stack.enter_context(nc.sbuf_tensor(f"cr_{what}", shape, F32, side="right"))

        self.dram = dram
        self.q, self.v, self.o = sb("q", [P, INNER]), sb("v", [CDIM, INNER]), sb("o", [P, NCH, HID])
        self.kq = sb("kq", [P, INNER])
        self.loaded = stack.enter_context(nc.semaphore("cr_loaded"))

    def load(self, engine):
        wq, wk, wv, wo = self.dram
        for out, w in ((self.q[:, :], wq[0:HA, :]), (self.kq[CDIM:P, :], wq[HA:HID, :]), (self.kq[0:CDIM, :], wk),
                       (self.v[:, :], wv), (self.o[:, :, :], wo.rearrange("(k p) n -> p k n", p=P))):
            engine.dma_start(out, w).then_inc(self.loaded, 16)
        engine.wait_ge(self.loaded, 5 * 16)


def prepare_cross(nc, name, ident, g, be, bo, raw,
                  wq_h, wq_l, wq_s, wv_h, wv_l, wo_hl, gain, shift, bo_row):
    stack = ExitStack()
    with stack:
        def sb(what, shape, dt):
            return stack.enter_context(nc.sbuf_tensor(f"{name}_{what}", shape, dt))

        def sem(what):
            return stack.enter_context(nc.semaphore(f"{name}_{what}"))

        raw_v, raw_o = raw.v, raw.o
        B4, A, K, W = 0, P, 2 * P, 2 * P + CDIM
        w_t = sb("w_t", [P, NCH, W], F32)
        turned = [stack.enter_context(nc.psum_tensor(f"{name}_turned{i}", [P, 512], F32)) for i in range(2)]
        prod = [stack.enter_context(nc.psum_tensor(f"{name}_prod{i}", [P, 512], F32)) for i in range(2)]
        small = sem("small")
        turned_done = sem("turned_done")
        turned_read = sem("turned_read")
        prod_done = sem("prod_done")
        prod_hi = sem("prod_hi")
        prod_read = sem("prod_read")
        rounded = sem("rounded")

        with nc.Block() as block:
            @block.sync
            def _(sp):
                load_vectors(sp, g, be, bo, gain, shift, bo_row, small)
                sp.wait_ge(small, VECTORS * 16)

            @block.tensor
            def _(pe):
                def turn(k):
                    after(pe, turned_read, k - 1)
                    cols, out = slice(k * P, (k + 1) * P), turned[k % 2]
                    nc.tensor.transpose(out[:, 0:HB], raw.kq[CDIM:P, cols], ident[CDIM:P, CDIM:P])
                    nc.tensor.transpose(out[:, HB:HID], raw.q[:, cols], ident[:, :])
                    nc.tensor.transpose(out[:, HID:HID + CDIM], raw.kq[0:CDIM, cols], ident[0:CDIM, 0:CDIM]).then_inc(turned_done, 1)

                def multiply(k):
                    pe.wait_ge(turned_read, k + 1)
                    for j in range(2):
                        head, rows = 2 * k + j, slice(j * DH, (j + 1) * DH)
                        after(pe, prod_read, head - 1)
                        out = prod[head % 2]
                        nc.tensor.matmul(out[:, 0:CDIM], w_t[rows, k, A:K], w_t[rows, k, K:W], start=True, stop=True)
                        nc.tensor.matmul(out[:, CDIM:2 * CDIM], w_t[rows, k, B4:A], w_t[rows, k, K:W], start=True,
                                         stop=True).then_inc(prod_done, 1)

                for k in range(NCH + 1):
                    if k < NCH:
                        turn(k)
                    if k >= 1:
                        multiply(k - 1)

            @block.scalar
            def _(act):
                nc.scalar.copy(wv_h[:, :], raw_v[:, :]).then_inc(rounded, 1)
                nc.scalar.copy(wo_hl[:, :, 0, :], raw_o[:, :, :]).then_inc(rounded, 1)
                for h in range(HEADS):
                    act.wait_ge(prod_done, h + 1)
                    nc.scalar.copy(wq_h[:, h, :], prod[h % 2][:, 0:CDIM])
                    nc.scalar.copy(wq_s[:, h, :], prod[h % 2][:, CDIM:2 * CDIM]).then_inc(prod_hi, 1)

            @block.vector
            def _(dve):
                def copy_turned(k):
                    dve.wait_ge(turned_done, k + 1)
                    nc.vector.tensor_copy(w_t[:, k, B4:A].rearrange("p (r f) -> p r f", r=REP),
                                          turned[k % 2][:, None, 0:HB].to_broadcast([P, REP, HB]))
                    nc.vector.tensor_copy(w_t[:, k, A:W], turned[k % 2][:, HB:HID + CDIM]).then_inc(turned_read, 1)

                half = slice(P // 2, P)
                copy_turned(0)
                for k in range(NCH):
                    if k + 1 < NCH:
                        copy_turned(k + 1)
                    for h in (2 * k, 2 * k + 1):
                        dve.wait_ge(prod_hi, h + 1)
                        nc.vector.tensor_tensor(wq_l[:, h, :], prod[h % 2][:, 0:CDIM], wq_h[:, h, :], ALU.subtract)
                        nc.vector.tensor_tensor(wq_s[half, h, :], prod[h % 2][half, CDIM:2 * CDIM], wq_s[half, h, :],
                                                ALU.subtract).then_inc(prod_read, 1)
                dve.wait_ge(rounded, 2)
                nc.vector.tensor_tensor(wv_l[:, :], raw_v[:, :], wv_h[:, :], ALU.subtract)
                nc.vector.tensor_tensor(wo_hl[:, :, 1, :], raw_o[:, :, :], wo_hl[:, :, 0, :], ALU.subtract)


def attention(nc, name, cross, x, ident, ctx_dram, weights, next_loads):
    KT = CTX // P if cross else SEQ // P
    U = 4 if cross else 2
    UB = U * PAIRS
    MAX, MT, SCORE, WEIGH = 2, 3, 4, 5
    KEPT = 5
    GROUPS = ((), (0,), (1,), (2, 3)) if cross else ((), (0, 1, 2, 3))
    MROW = CDIM if cross else DH
    SCALE = float(DH) ** -0.5
    VN = [(0, 512), (512, 512), (1024, 256)]
    VU = [(t, n) for t in range(KT) for n in range(3)]

    VALUES = (({5: [0, 1], 6: [2], 7: [3], 8: [4, 5], 9: [6, 7]}, {0: [8, 9], 2: [10, 11]}) if cross else
              ({5: [0], 8: [1, 2], 9: [3]}, {0: [4], 2: [5]}))
    AHEAD = VALUES[1][0][0]

    def extras(kind, s):
        out = []
        has_prev, has_nxt, has_cur = kind != "first", kind in ("first", "steady"), kind != "tail"
        if has_prev and s in (1, 3, 5):
            out.append((1, ("ot", "prev", 2 + s // 2)))
        if cross and has_nxt and s == 4:
            out.append((2, ("ctx", "nxt", 0)))
        if has_nxt and s == 4:
            out.append((1, ("ln", "nxt", 0)))
        if has_prev and s in (6, 7):
            out.append((U - 1, ("out", "prev", s - 6)))
        if has_cur and s in (8, 9):
            out.append((1, ("ot", "cur", s - 8)))
        for n, v in enumerate(VALUES[0].get(s, ()) if has_nxt else ()):
            out.append((min(n + 1, U - 1), ("v", "nxt", v)))
        for n, v in enumerate(VALUES[1].get(s, ()) if has_cur else ()):
            out.append((min(n + 1, U - 1), ("v", "cur", v)))
        return sorted(out, key=lambda e: e[0])

    def slot_keys(kind, s):
        keys = []
        mt = ("mt", "cur", s - MT) if s >= MT else ("mt", "prev", s + PAIRS - MT)
        if (mt[1] == "cur" and kind != "tail") or (mt[1] == "prev" and kind != "first"):
            keys.append(mt)
        if kind != "tail":
            keys.append(("proj", s))
        for step in range(U):
            keys += [k for at, k in extras(kind, s) if at == step]
        return keys

    def all_keys(kind):
        if kind == "tail":
            return [k for s in range(TAIL) for k in slot_keys(kind, s)]
        pre = []
        if kind == "first":
            pre = [("ctx", "pre", 0)] * cross + [("ln", "pre", 0)] + [("v", "pre", v) for v in range(AHEAD)]
        return pre + [k for s in range(PAIRS) for k in slot_keys(kind, s)]

    ring = Ring(all_keys, NB, ("mt",))
    PRE = sum(key[1] == "pre" for key in ring.keys["first"])

    def earlier(kind, period, key):
        return ring.read("last", NB - 1, key) if kind == "tail" else ring.read("steady", period - 1, key)

    def projections_read(kind, s, period):
        if s < MAX:
            return earlier(kind, period, ("proj", PAIRS + s - MAX))
        return ring.read(kind, period, ("proj", s - MAX))

    def before(s, d, cur, prev):
        if s >= d:
            return cur and (cur, s - d)
        return prev and (prev, s - d + PAIRS)

    stack = ExitStack()
    with stack:
        def sb(what, shape, dt):
            return stack.enter_context(nc.sbuf_tensor(f"{name}_{what}", shape, dt))

        def bank(what):
            return stack.enter_context(nc.psum_tensor(f"{name}_{what}", [P, 512], F32))

        def sem(what):
            return stack.enter_context(nc.semaphore(f"{name}_{what}"))

        QW = CDIM if cross else 2 * DH
        if cross:
            wq_h, wq_l, wq_s = (sb(f"wq_{i}", [P, HEADS, QW], F32R) for i in "hls")
            wv_h, wv_l = (sb(f"wv_{i}", [CDIM, INNER], F32R) for i in "hl")
            wo_hl = sb("wo_hl", [P, NCH, 2, HID], F32R)
            gain = sb("gain", [P, 2], F32)
            shift = sb("shift", [P, 2], F32)
            bo_row = sb("bo_row", [P, HID], F32)
            prepare_cross(nc, name, ident, *weights, wq_h, wq_l, wq_s, wv_h, wv_l, wo_hl, gain, shift, bo_row)
        else:
            (wq_h, wq_l, wq_s), (wv_h, wv_l, wv_s) = weights.qk, weights.v
            wo_hl, gain, shift, bo_row = weights.wo_hl, weights.gain, weights.shift, weights.bo_row

        load_next = next_loads()

        neg_eye = sb("neg_eye", [P, 2], F32)
        half_neg = sb("half_neg", [P, QT], F32)
        eps = sb("eps", [P, QT], F32)
        stats_seen = sb("stats_seen", [P, QT], F32)

        xn = sb("xn", [P, QT, 2, P], F32)
        stats = sb("stats", [P, QT, 6], F32)
        mean_var = sb("mean_var", [P, QT, 2], F32)
        var_eps = sb("var_eps", [P, QT], F32)
        rstd = sb("rstd", [P, QT], F32)
        ln_t = sb("ln_t", [P, 2, SEQ], F32)
        ln_h = [sb(f"ln_h{i}", [P, 2, SEQ], F32R) for i in range(2)]
        ln_l = [sb(f"ln_l{i}", [P, SEQ], F32R) for i in range(2)]
        if cross:
            ctx_rows = [sb(f"ctx_rows{i}", [P, KT, CDIM], F32) for i in range(2)]
            ctx_h = [sb(f"ctx_h{i}", [P, CTX], F32R) for i in range(2)]
            ctx_l = [sb(f"ctx_l{i}", [CDIM, CTX], F32R) for i in range(2)]
            q_h = sb("q_h", [P, KEPT, 2, SEQ], F32R)
            q_l = sb("q_l", [CDIM, KEPT, 2, SEQ], F32R)
        else:
            q_t = sb("q_t", [P, 2 * KEPT, 2, SEQ], F32R)
            k_t = sb("k_t", [P, 2 * KEPT, 2, SEQ], F32R)
        v_h = [sb(f"v_h{i}", [P, KT, HEADS, DV], BF16) for i in range(2)]
        v_l = [sb(f"v_l{i}", [P, KT, HEADS, DV], F16) for i in range(2)]
        maxima = sb("maxima", [P, 2, QT, P], F32)
        PR = 2 * U
        probs = sb("probs", [P, PR, 512], F32)
        probs_l = sb("probs_l", [P, PR, 512], F16)
        recip = sb("recip", [P, 4], F32)
        attn = sb("attn", [P, QT, INNER], F32)
        attn_th = sb("attn_th", [P, NCH, SEQ], F32R)
        attn_tl = sb("attn_tl", [P, NCH, SEQ], F32R)

        shared = [bank(f"shared{i}") for i in range(Ring.BANKS)]
        max_bank = [bank(f"max{i}") for i in range(2)]
        score_bank = [bank(f"score{i}") for i in range(2)]
        pv_bank = bank("pv")

        if cross:
            rows_in = [sem(f"rows_in{i}") for i in range(2)]
            ctx_hi = sem("ctx_hi")
        else:
            k_hi = sem("k_hi")
        eye_zero = sem("eye_zero")
        consts = sem("consts")
        filled = sem("filled")
        emptied = sem("emptied")
        shifted = sem("shifted")
        stats_ready = sem("stats_ready")
        var_ready = sem("var_ready")
        var_eps_ready = sem("var_eps_ready")
        rstd_ready = sem("rstd_ready")
        xn_ready = sem("xn_ready")
        lnt_ready = sem("lnt_ready")
        ln_ready = sem("ln_ready")
        v_hi = sem("v_hi")
        q_hi = sem("q_hi")
        max_filled = sem("max_filled")
        max_read = sem("max_read")
        scored = sem("scored")
        exped = sem("exped")
        probs_split = sem("probs_split")
        pv_done = sem("pv_done")
        recip_ready = sem("recip_ready")
        attn_ready = sem("attn_ready")
        attn_hi = sem("attn_hi")
        x_bo_ready = sem("x_bo_ready")
        part_ready = sem("part_ready")

        block = stack.enter_context(nc.Block())

        @block.sync
        def _(sp):
            if not cross:
                load_next(sp)
                return

            def rows(b, parity):
                sp.dma_start(ctx_rows[parity][:, :, :],
                             ctx_dram[b, :, :].rearrange("(t p) c -> p t c", p=P)).then_inc(rows_in[parity], 16)

            rows(0, 0)
            rows(1, 1)
            with sp.Fori(0, (NB - 2) // 2) as i:
                for j in (0, 1):
                    b = i * 2 + j
                    sp.wait_ge(ctx_hi, b + 1)
                    rows(b + 2, j)
            load_next(sp)

        @block.gpsimd
        def _(pool):
            def inverse_root(b):
                pool.wait_ge(var_ready, b + 1)
                nc.gpsimd.tensor_tensor(var_eps[:, :], mean_var[:, :, 1], eps[:, :], ALU.add).then_inc(var_eps_ready, 1)
                pool.wait_ge(var_eps_ready, b + 1)
                nc.gpsimd.tensor_tensor(rstd[:, :], var_eps[:, :], half_neg[:, :], ALU.pow).then_inc(rstd_ready, 1)

            def slot(kind, s, cur, prev, nxt):
                if s == 4 and nxt is not None:
                    inverse_root(nxt[0])
                if s == 4 and prev is not None:
                    rows = x[:, bass.ds(prev[0] * QT, QT), :]
                    nc.gpsimd.tensor_tensor(rows, rows, bo_row[:, None, :].to_broadcast([P, QT, HID]), ALU.add).then_inc(x_bo_ready, 1)
                if (work := before(s, SCORE, cur, prev)) is not None:
                    (b, _), p = work
                    for u in range(U):
                        n = p * U + u
                        pool.wait_ge(exped, b * UB + n + 1)
                        whole = probs[:, n % PR, :]
                        nc.gpsimd.tensor_tensor(probs_l[:, n % PR, :], whole, whole.bitcast(BF16)[:, 1::2],
                                                ALU.subtract).then_inc(probs_split, 1)

            nc.gpsimd.memset(half_neg[:, :], -0.5)
            nc.gpsimd.memset(eps[:, :], EPS).then_inc(eye_zero, 1)
            pool.wait_ge(eye_zero, 1)
            inverse_root(0)
            nc.gpsimd.memset(neg_eye[:, :], 0.0).then_inc(eye_zero, 1)
            pool.wait_ge(eye_zero, 2)
            nc.gpsimd.affine_select(out=neg_eye[:, :], in_=neg_eye[:, :], compare_op=ALU.not_equal, fill=-1.0,
                                    base=-MROW, pattern=[[-1, 2]], channel_multiplier=1)
            nc.gpsimd.memset(maxima[:, :, :, :], 0.0)
            for i in range(2):
                nc.gpsimd.memset(v_h[i][:, :, :, DH:DV], 1.0)
                ins = nc.gpsimd.memset(v_l[i][:, :, :, DH:DV], 0.0)
            ins.then_inc(consts, 1)
            periods(pool, slot)

        @block.scalar
        def _(act):
            def ln_transposed(kind, period, key, b):
                act.wait_ge(filled, ring.number(kind, period, key) + 1)
                bank_ = shared[ring.bank(kind, key)]
                nc.scalar.activation(ln_t[:, 0, :], bank_[:, 0:SEQ], ACT.Identity, bias=shift[:, 0:1], scale=gain[:, 0:1])
                nc.scalar.activation(ln_t[:, 1, :], bank_[:, SEQ:2 * SEQ], ACT.Identity, bias=shift[:, 1:2],
                                     scale=gain[:, 1:2]).then_inc(lnt_ready, 1)

            def extra(kind, period, key, batch):
                b, parity = batch
                what, _, i = key
                if what == "ln":
                    ln_transposed(kind, period, key, b)
                    return
                if what == "out":
                    return
                act.wait_ge(filled, ring.number(kind, period, key) + 1)
                bank_ = shared[ring.bank(kind, key)]
                if what == "ctx":
                    nc.scalar.copy(ctx_h[parity][0:CDIM, :], bank_[0:CDIM, :]).then_inc(ctx_hi, 1)
                elif what == "v":
                    t, n = VU[i]
                    at, width = VN[n]
                    nc.scalar.copy(v_h[parity][:, t, at // DH:(at + width) // DH, 0:DH],
                                   bank_[:, 0:width].rearrange("p (h d) -> p h d", d=DH)).then_inc(v_hi, 1)
                elif what == "ot":
                    nc.scalar.copy(attn_th[:, 2 * i:2 * i + 2, :],
                                   bank_[:, :].rearrange("p (k q) -> p k q", k=2)).then_inc(attn_hi, 1)

            def projected(kind, s, cur):
                b, parity = cur
                key = ("proj", s)
                act.wait_ge(filled, ring.number(kind, b, key) + 1)
                after(act, scored, b * UB + (s - KEPT + 1) * U)
                bank_ = shared[ring.bank(kind, key)]
                if cross:
                    at = s % KEPT
                    nc.scalar.copy(q_h[0:CDIM, at, :, :], bank_[0:CDIM, :].rearrange("p (h q) -> p h q", h=2)).then_inc(q_hi, 1)
                else:
                    at = s % KEPT * 2
                    both = bank_[:, :].rearrange("p (h q) -> p h q", h=2)
                    nc.scalar.copy(k_t[DH:P, at:at + 2, 0, :], both[DH:P])
                    nc.scalar.copy(k_t[0:DH, at:at + 2, 0, :], both[DH:P]).then_inc(k_hi, 1)
                    nc.scalar.copy(q_t[0:DH, at:at + 2, :, :], both[0:DH, :, None, :].to_broadcast([DH, 2, 2, SEQ])).then_inc(q_hi, 1)

            def write_shift(kind, period, key):
                p, rows = key[2], slice(MROW, MROW + 32)
                act.wait_ge(filled, ring.number(kind, period, key) + 1)
                for j in range(2):
                    out = q_h[rows, p % KEPT, j, :] if cross else q_t[rows, p % KEPT * 2 + j, 1, :]
                    ins = nc.scalar.activation(out, shared[ring.bank(kind, key)][rows, 0:SEQ], ACT.Copy, scale=neg_eye[rows, j:j + 1])
                ins.then_inc(shifted, 1)

            def slot(kind, s, cur, prev, nxt):
                period = cur[0] if cur is not None else NB
                for step in range(U):
                    if (work := before(s, SCORE, cur, prev)) is not None:
                        (b, _), p = work
                        n = p * U + step
                        act.wait_ge(scored, b * UB + n + 1)
                        after(act, pv_done, b * PAIRS + p - 1)
                        nc.scalar.activation(probs[:, n % PR, :], score_bank[n % 2][:, :], ACT.Exp,
                                             scale=SCALE).then_inc(exped, 1)
                    if step == 0 and before(s, MT, cur, prev) is not None:
                        write_shift(kind, period, ("mt", "cur" if s >= MT else "prev", (s - MT) % PAIRS))
                    if step == 0 and cur is not None:
                        projected(kind, s, cur)
                    for at, key in extras(kind, s):
                        if at == step:
                            extra(kind, period, key, {"cur": cur, "prev": prev, "nxt": nxt}[key[1]])

            for key in ring.keys["first"][:PRE]:
                extra("first", 0, key, (0, 0))
            act.wait_ge(consts, 2)
            periods(act, slot)

        @block.vector
        def _(dve):
            def statistics(b):
                for t in range(QT):
                    nc.vector.bn_stats(stats[:, t, :], x[:, b * QT + t, :]).then_inc(stats_ready, 1)
                dve.wait_ge(stats_ready, b * QT + QT)
                nc.vector.tensor_copy(stats_seen[:, :], stats[:, :, 0])
                for t in range(QT):
                    ins = nc.vector.bn_aggr(mean_var[:, t, :], stats[:, t, :])
                ins.then_inc(var_ready, 1)

            def normalise(b):
                dve.wait_ge(rstd_ready, b + 1)
                for t in range(QT):
                    row = x[:, b * QT + t, :]
                    nc.vector.tensor_scalar(xn[:, t, 0, :], row[:, 0:HA], mean_var[:, t, 0:1], rstd[:, t:t + 1],
                                            ALU.subtract, ALU.mult)
                    ins = nc.vector.tensor_scalar(xn[:, t, 1, :].rearrange("p (r f) -> p r f", r=REP),
                                                  row[:, None, HA:HID].to_broadcast([P, REP, HB]),
                                                  mean_var[:, t, 0:1], rstd[:, t:t + 1], ALU.subtract, ALU.mult)
                ins.then_inc(xn_ready, 1)

            def extra(kind, period, key, batch):
                b, parity = batch
                what, _, i = key
                bank_ = shared[ring.bank(kind, key)]
                if what == "ln":
                    h, low = ln_h[parity], ln_l[parity]
                    dve.wait_ge(lnt_ready, b + 1)
                    nc.vector.tensor_copy(h[:, :, :], ln_t[:, :, :]).then_inc(emptied, 1)
                    dve.wait_ge(emptied, ring.read(kind, period, key))
                    nc.vector.tensor_tensor(low[:, :], ln_t[:, 0, :], h[:, 0, :], ALU.subtract)
                    nc.vector.tensor_tensor(h[HB:2 * HB, 1, :], ln_t[HB:2 * HB, 1, :], h[HB:2 * HB, 1, :], ALU.subtract)
                    nc.vector.tensor_tensor(h[3 * HB:P, 1, :], ln_t[3 * HB:P, 1, :], h[3 * HB:P, 1, :],
                                            ALU.subtract).then_inc(ln_ready, 1)
                elif what == "ctx":
                    dve.wait_ge(ctx_hi, b + 1)
                    nc.vector.tensor_tensor(ctx_l[parity][:, :], bank_[0:CDIM, :], ctx_h[parity][0:CDIM, :],
                                            ALU.subtract).then_inc(emptied, 1)
                elif what == "v":
                    t, n = VU[i]
                    at, width = VN[n]
                    heads = slice(at // DH, (at + width) // DH)
                    dve.wait_ge(v_hi, b * len(VU) + i + 1)
                    nc.vector.tensor_tensor(v_l[parity][:, t, heads, 0:DH],
                                            bank_[:, 0:width].rearrange("p (h d) -> p h d", d=DH),
                                            v_h[parity][:, t, heads, 0:DH], ALU.subtract).then_inc(emptied, 1)
                elif what == "ot":
                    dve.wait_ge(attn_hi, b * (NCH // 2) + i + 1)
                    nc.vector.tensor_tensor(attn_tl[:, 2 * i:2 * i + 2, :],
                                            bank_[:, :].rearrange("p (k q) -> p k q", k=2),
                                            attn_th[:, 2 * i:2 * i + 2, :], ALU.subtract).then_inc(emptied, 1)
                elif what == "out":
                    dve.wait_ge(x_bo_ready, b + 1)
                    dve.wait_ge(filled, ring.number(kind, period, key) + 1)
                    row = x[:, b * QT + i, :]
                    nc.vector.tensor_tensor(row, bank_[:, 0:HID], row, ALU.add).then_inc(part_ready, 1)
                    dve.wait_ge(part_ready, b * QT + i + 1)
                    nc.vector.tensor_tensor(row, bank_[:, HID:2 * HID], row, ALU.add).then_inc(emptied, 1)

            def projected(kind, s, cur):
                b, parity = cur
                bank_ = shared[ring.bank(kind, ("proj", s))]
                if cross:
                    at = s % KEPT
                    dve.wait_ge(q_hi, b * PAIRS + s + 1)
                    nc.vector.tensor_tensor(q_l[:, at, :, :], bank_[0:CDIM, :].rearrange("p (h q) -> p h q", h=2),
                                            q_h[0:CDIM, at, :, :], ALU.subtract).then_inc(emptied, 1)
                else:
                    at = s % KEPT * 2
                    both = bank_[:, :].rearrange("p (h q) -> p h q", h=2)
                    dve.wait_ge(k_hi, b * PAIRS + s + 1)
                    nc.vector.tensor_tensor(k_t[0:DH, at:at + 2, 1, :], both[DH:P], k_t[DH:P, at:at + 2, 0, :], ALU.subtract)
                    dve.wait_ge(q_hi, b * PAIRS + s + 1)
                    nc.vector.tensor_tensor(q_t[DH:P, at:at + 2, 0, :], both[0:DH], q_t[0:DH, at:at + 2, 0, :],
                                            ALU.subtract).then_inc(emptied, 1)

            def slot(kind, s, cur, prev, nxt):
                period = cur[0] if cur is not None else NB
                for step in range(U):
                    if (work := before(s, MAX, cur, prev)) is not None:
                        (b, _), p = work
                        n = p * U + step
                        dve.wait_ge(max_filled, b * UB + n + 1)
                        if cross:
                            j, t = step // 2, step % 2
                            out, scores = maxima[:, p % 2, t, MROW + j:MROW + j + 1], max_bank[n % 2][:, :]
                        else:
                            out = maxima[:, p % 2, :, MROW + step]
                            scores = max_bank[n % 2][:, :].rearrange("p (t k) -> p t k", t=QT)
                        nc.vector.reduce_max(out, scores, AX.X).then_inc(max_read, 1)
                    if s == 4 and step == 0 and nxt is not None:
                        normalise(nxt[0])
                    if step == 1 and cur is not None:
                        projected(kind, s, cur)
                    for at, key in extras(kind, s):
                        if max(at, 1) == step:
                            extra(kind, period, key, {"cur": cur, "prev": prev, "nxt": nxt}[key[1]])
                if s == 3 and nxt is not None:
                    statistics(nxt[0])
                if (work := before(s, WEIGH, cur, prev)) is not None:
                    (b, _), p = work
                    dve.wait_ge(pv_done, b * PAIRS + p + 1)
                    sums = pv_bank[:, 0:4 * DV].rearrange("p (g d) -> p g d", d=DV)
                    nc.vector.reciprocal(recip[:, :], sums[:, :, DH]).then_inc(recip_ready, 1)
                    dve.wait_ge(recip_ready, b * PAIRS + p + 1)
                    out = attn[:, :, p * P:(p + 1) * P].rearrange("p t (h d) -> p h t d", h=2)
                    nc.vector.tensor_tensor(out, pv_bank[:, 0:4 * DV].rearrange("p (h t d) -> p h t d", h=2, t=QT)[:, :, :, 0:DH],
                                            recip[:, :].rearrange("p (h t) -> p h t", h=2)[:, :, :, None].to_broadcast([P, 2, QT, DH]),
                                            ALU.mult).then_inc(attn_ready, 1)

            statistics(0)
            normalise(0)
            ones = [c[CDIM:P, :] for c in ctx_h] if cross else [k_t[DH:P, :, 1, :]]
            for rows in ones:
                ins = nc.vector.memset(rows.bitcast(F32), 1.0)
            ins.then_inc(consts, 1)
            for key in ring.keys["first"][:PRE]:
                extra("first", 0, key, (0, 0))
            dve.wait_ge(consts, 2)
            periods(dve, slot)

        @block.tensor
        def _(pe):
            def claim(kind, period, key):
                by_vector, by_scalar = ring.free(kind, period, key)
                after(pe, emptied, by_vector)
                after(pe, shifted, by_scalar)
                return shared[ring.bank(kind, key)]

            def extra(kind, period, key, batch):
                b, parity = batch
                what, _, i = key
                h, low = ln_h[parity], ln_l[parity]
                if what == "ctx":
                    pe.wait_ge(rows_in[parity], 8 * (b - parity) + 16)
                    bank_ = claim(kind, period, key)
                    for t in range(KT):
                        mm = nc.tensor.transpose(bank_[0:CDIM, t * P:(t + 1) * P], ctx_rows[parity][:, t, :], ident[:, :])
                elif what == "ln":
                    pe.wait_ge(xn_ready, b + 1)
                    bank_ = claim(kind, period, key)
                    for c in range(2):
                        for t in range(QT):
                            mm = nc.tensor.transpose(bank_[:, c * SEQ + t * P:c * SEQ + (t + 1) * P], xn[:, t, c, :], ident[:, :])
                elif what == "v":
                    t, n = VU[i]
                    at, width = VN[n]
                    bank_ = claim(kind, period, key)
                    tok, col = slice(t * P, (t + 1) * P), slice(at, at + width)
                    if cross:
                        if i == 0:
                            pe.wait_ge(emptied, ring.read(kind, period, ("ctx", key[1], 0)))
                        passes = [(ctx_h[parity][0:CDIM, tok], wv_h[:, col]), (ctx_l[parity][:, tok], wv_h[:, col]),
                                  (ctx_h[parity][0:CDIM, tok], wv_l[:, col])]
                    else:
                        if i == 0:
                            pe.wait_ge(ln_ready, b + 1)
                        passes = [(h[:, 0, tok], wv_h[:, col]), (low[:, tok], wv_h[:, col]),
                                  (h[:, 0, tok], wv_l[:, col]), (h[:, 1, tok], wv_s[:, col])]
                    for n, (lhs, rhs) in enumerate(passes):
                        mm = nc.tensor.matmul(bank_[:, 0:width], lhs, rhs, start=n == 0, stop=n == len(passes) - 1)
                elif what == "ot":
                    pe.wait_ge(attn_ready, b * PAIRS + 2 * i + 2)
                    bank_ = claim(kind, period, key)
                    for c in range(2):
                        for t in range(QT):
                            k = 2 * i + c
                            mm = nc.tensor.transpose(bank_[:, c * SEQ + t * P:c * SEQ + (t + 1) * P],
                                                     attn[:, t, k * P:(k + 1) * P], ident[:, :])
                elif what == "out":
                    bank_ = claim(kind, period, key)
                    if i == 0:
                        pe.wait_ge(emptied, ring.read(kind, period, ("ot", "prev", 4)))
                    for k in range(NCH):
                        for c, lhs in enumerate((attn_th, attn_tl)):
                            mm = nc.tensor.matmul(bank_[:, 0:2 * HID], lhs[:, k, i * P:(i + 1) * P],
                                                  wo_hl[:, k, :, :].rearrange("p a n -> p (a n)"),
                                                  start=k == 0 and c == 0, stop=k == NCH - 1 and c == 1)
                mm.then_inc(filled, 1)

            def project(kind, s, cur):
                b, parity = cur
                bank_ = claim(kind, b, ("proj", s))
                h, low = ln_h[parity], ln_l[parity]
                for c in range(2):
                    head = 2 * s + c
                    out = bank_[0:QW, c * SEQ:(c + 1) * SEQ]
                    nc.tensor.matmul(out, wq_h[:, head, :], h[:, 0, :], start=True, stop=False)
                    nc.tensor.matmul(out, wq_h[:, head, :], low[:, :], start=False, stop=False)
                    nc.tensor.matmul(out, wq_l[:, head, :], h[:, 0, :], start=False, stop=False)
                    mm = nc.tensor.matmul(out, wq_s[:, head, :], h[:, 1, :], start=False, stop=True)
                mm.then_inc(filled, 1)

            def find_max(kind, s, step, work, projected):
                (b, parity), p = work
                n = p * U + step
                pe.wait_ge(emptied, projected)
                after(pe, max_read, b * UB + n - 1)
                if cross:
                    j, t = step // 2, step % 2
                    at = p % KEPT
                    mm = nc.tensor.matmul(max_bank[n % 2][:, :], q_h[0:CDIM, at, j, t * P:(t + 1) * P],
                                          ctx_h[parity][0:CDIM, :], start=True, stop=True)
                else:
                    at = p % KEPT * 2 + step
                    for t in range(QT):
                        mm = nc.tensor.matmul(max_bank[n % 2][:, t * SEQ:(t + 1) * SEQ], q_t[:, at, 0, t * P:(t + 1) * P],
                                              k_t[:, at, 0, :], start=True, stop=True)
                mm.then_inc(max_filled, 1)

            def score(step, work):
                (b, parity), p = work
                n = p * U + step
                after(pe, exped, b * UB + n - 1)
                out = score_bank[n % 2]
                if cross:
                    at = p % KEPT
                    keys = slice(step * P, (step + 1) * P)
                    nc.tensor.matmul(out[:, :], ctx_h[parity][:, keys], q_h[:, at, :, :], start=True, stop=False)
                    nc.tensor.matmul(out[:, :], ctx_h[parity][0:CDIM, keys], q_l[:, at, :, :], start=False, stop=False)
                    mm = nc.tensor.matmul(out[:, :], ctx_l[parity][:, keys], q_h[0:CDIM, at, :, :], start=False, stop=True)
                else:
                    at = p % KEPT * 2 + step
                    for c in range(KT):
                        keys = slice(c * P, (c + 1) * P)
                        nc.tensor.matmul(out[:, c * SEQ:(c + 1) * SEQ], k_t[:, at, 0, keys], q_t[:, at, 0, :],
                                         start=True, stop=False)
                        mm = nc.tensor.matmul(out[:, c * SEQ:(c + 1) * SEQ], k_t[0:DH + 32, at, 1, keys], q_t[0:DH + 32, at, 1, :],
                                              start=False, stop=True)
                mm.then_inc(scored, 1)

            def weigh(kind, s, group, work):
                (b, parity), p = work
                j, t = group // QT, group % QT
                if group == 0:
                    pe.wait_ge(probs_split, b * UB + (p + 1) * U)
                    after(pe, attn_ready, b * PAIRS + p)
                    if p == 0:
                        pe.wait_ge(emptied, ring.read(kind, b, ("v", "cur", len(VU) - 1)))
                out = pv_bank[:, group * DV:(group + 1) * DV]
                head = 2 * p + j
                n = 0
                for c in range(KT):
                    unit, col = (c, j * SEQ) if cross else (j, c * SEQ)
                    unit = (p * U + unit) % PR
                    cols = slice(col + t * P, col + (t + 1) * P)
                    hi = probs[:, unit, :].bitcast(BF16)[:, 1::2][:, cols]
                    lo = probs_l[:, unit, cols]
                    for lhs, rhs in ((hi, v_h), (hi, v_l), (lo, v_h)):
                        mm = nc.tensor.matmul(out, lhs, rhs[parity][:, c, head, :], start=n == 0, stop=n == 3 * KT - 1)
                        n += 1
                if group == 3:
                    mm.then_inc(pv_done, 1)

            def slot(kind, s, cur, prev, nxt):
                period = cur[0] if cur is not None else NB
                for step in range(U):
                    if (work := before(s, MAX, cur, prev)) is not None:
                        find_max(kind, s, step, work, projections_read(kind, s, period))
                    if (work := before(s, SCORE, cur, prev)) is not None:
                        if step == 0:
                            pe.wait_ge(shifted, work[0][0] * PAIRS + work[1] + 1)
                        score(step, work)
                    if step == 0 and before(s, MT, cur, prev) is not None:
                        p = (s - MT) % PAIRS
                        key = ("mt", "cur" if s >= MT else "prev", p)
                        bank_ = claim(kind, period, key)
                        b = before(s, MT, cur, prev)[0][0]
                        pe.wait_ge(max_read, b * UB + (p + 1) * U)
                        for t in range(QT):
                            mm = nc.tensor.transpose(bank_[:, t * P:(t + 1) * P], maxima[:, p % 2, t, :], ident[:, :])
                        mm.then_inc(filled, 1)
                    if step == 0 and cur is not None:
                        if s == 0:
                            pe.wait_ge(ln_ready, cur[0] + 1)
                        project(kind, s, cur)
                    if (work := before(s, WEIGH, cur, prev)) is not None:
                        for group in GROUPS[step]:
                            weigh(kind, s, group, work)
                    for at, key in extras(kind, s):
                        if at == step:
                            extra(kind, period, key, {"cur": cur, "prev": prev, "nxt": nxt}[key[1]])

            for key in ring.keys["first"][:PRE]:
                extra("first", 0, key, (0, 0))
            pe.wait_ge(consts, 2)
            periods(pe, slot)


class FeedForwardRaw:

    def __init__(self, nc, stack, dram):
        def sb(what, shape):
            return stack.enter_context(nc.sbuf_tensor(f"fr_{what}", shape, F32, side="right"))

        self.dram = dram
        self.first_a, self.first_b = sb("first_a", [P, 2 * DFF]), sb("first_b", [P, 2 * DFF])
        self.second = sb("second", [P, DFF // P, HID])
        self.loaded = stack.enter_context(nc.semaphore("fr_loaded"))

    def load(self, engine):
        w1, w2 = self.dram
        engine.dma_start(self.first_a[:, :], w1[0:HA, :]).then_inc(self.loaded, 16)
        load_stacked(engine, self.first_b[:, :], w1, self.loaded)
        engine.dma_start(self.second[:, :, :], w2.rearrange("(k p) n -> p k n", p=P)).then_inc(self.loaded, 16)
        engine.wait_ge(self.loaded, 3 * 16)


def feed_forward(nc, x, ident, g, be, b1, b2, raw, out_dram):
    name = "ff"
    FCH = DFF // P
    stack = ExitStack()
    with stack:
        def sb(what, shape, dt):
            return stack.enter_context(nc.sbuf_tensor(f"{name}_{what}", shape, dt))

        def bank(what):
            return stack.enter_context(nc.psum_tensor(f"{name}_{what}", [P, 512], F32))

        def sem(what):
            return stack.enter_context(nc.semaphore(f"{name}_{what}"))

        raw_1a, raw_1b, raw_2 = raw.first_a, raw.first_b, raw.second
        w1_h, w1_l, w1_s = (sb(f"w1_{i}", [P, 2 * DFF], F32R) for i in "hls")
        w2_hl = sb("w2_hl", [P, FCH, 2, HID], F32R)
        gain, shift = sb("gain", [P, 2], F32), sb("shift", [P, 2], F32)
        b1_col = sb("b1_col", [P, 2 * FCH], F32)
        b2_row = sb("b2_row", [P, HID], F32)
        half_neg = sb("half_neg", [P, QT], F32)
        eps = sb("eps", [P, QT], F32)
        stats_seen = sb("stats_seen", [P, QT], F32)

        xn = sb("xn", [P, QT, 2, P], F32)
        stats = sb("stats", [P, QT, 6], F32)
        mean_var = sb("mean_var", [P, QT, 2], F32)
        var_eps = sb("var_eps", [P, QT], F32)
        rstd = sb("rstd", [P, QT], F32)
        ln_t = sb("ln_t", [P, 2, SEQ], F32)
        ln_h = [sb(f"ln_h{i}", [P, 2, SEQ], F32R) for i in range(2)]
        ln_l = [sb(f"ln_l{i}", [P, SEQ], F32R) for i in range(2)]
        gated = sb("gated", [P, FCH, SEQ], F32)
        hid = sb("hid", [P, FCH, SEQ], F32)
        hid_h = [sb(f"hid_h{i}", [P, FCH, SEQ], F32R) for i in range(2)]
        hid_l = [sb(f"hid_l{i}", [P, FCH, SEQ], F32R) for i in range(2)]

        ln_bank = bank("ln")
        hid_bank = [bank(f"hid{j}") for j in range(FCH)]
        out_bank = [bank(f"out{t}") for t in range(QT)]

        small = sem("small")
        rounded = sem("rounded")
        weights_ready = sem("weights_ready")
        stats_ready = sem("stats_ready")
        var_ready = sem("var_ready")
        var_eps_ready = sem("var_eps_ready")
        rstd_ready = sem("rstd_ready")
        xn_ready = sem("xn_ready")
        turned = sem("turned")
        lnt_ready = sem("lnt_ready")
        ln_hi = sem("ln_hi")
        ln_ready = sem("ln_ready")
        hid_filled = sem("hid_filled")
        gelu_ready = sem("gelu_ready")
        hid_ready = sem("hid_ready")
        hid_hi = sem("hid_hi")
        hid_lo = sem("hid_lo")
        out_filled = sem("out_filled")
        x_b2_ready = sem("x_b2_ready")
        part_ready = sem("part_ready")
        y_ready = sem("y_ready")
        stored = sem("stored")

        block = stack.enter_context(nc.Block())

        def batches(engine, period):
            period((0, 0), None, (1, 1))
            with engine.Fori(0, (NB - 2) // 2) as i:
                for j in (1, 2):
                    b = i * 2 + j
                    period((b, j % 2), (b - 1, 1 - j % 2), (b + 1, 1 - j % 2))
            period((NB - 1, 1), (NB - 2, 0), None)
            period(None, (NB - 1, 1), None)

        @block.sync
        def _(sp):
            load_vectors(sp, g, be, b2, gain, shift, b2_row, small)
            for c in range(2 * FCH):
                sp.dma_start(b1_col[:, c:c + 1], b1[c * P:(c + 1) * P].rearrange("(p a) -> p a", a=1)).then_inc(small, 16)

            def period(cur, prev, nxt):
                if prev is None:
                    return
                b, parity = prev
                sp.wait_ge(y_ready, b * QT + QT)
                sp.dma_start(out_dram[b, :, :].rearrange("(t p) n -> p t n", p=P),
                             x[:, bass.ds(b * QT, QT), :]).then_inc(stored, 16)

            batches(sp, period)
            sp.wait_ge(stored, 16 * NB)

        @block.gpsimd
        def _(pool):
            pool.wait_ge(weights_ready, 1)
            pool.wait_ge(small, (VECTORS + 2 * FCH) * 16)

            def inverse_root(b):
                pool.wait_ge(var_ready, b + 1)
                nc.gpsimd.tensor_tensor(var_eps[:, :], mean_var[:, :, 1], eps[:, :], ALU.add).then_inc(var_eps_ready, 1)
                pool.wait_ge(var_eps_ready, b + 1)
                nc.gpsimd.tensor_tensor(rstd[:, :], var_eps[:, :], half_neg[:, :], ALU.pow).then_inc(rstd_ready, 1)

            def period(cur, prev, nxt):
                if nxt is not None:
                    inverse_root(nxt[0])
                if prev is not None:
                    rows = x[:, bass.ds(prev[0] * QT, QT), :]
                    nc.gpsimd.tensor_tensor(rows, rows, b2_row[:, None, :].to_broadcast([P, QT, HID]), ALU.add).then_inc(x_b2_ready, 1)
                if cur is not None:
                    b, parity = cur
                    for j in range(FCH):
                        pool.wait_ge(hid_hi, b * FCH + j + 1)
                        nc.gpsimd.tensor_tensor(hid_l[parity][:, j, :], hid[:, j, :], hid_h[parity][:, j, :],
                                                ALU.subtract).then_inc(hid_lo, 1)

            inverse_root(0)
            batches(pool, period)

        @block.scalar
        def _(act):
            nc.scalar.copy(w1_h[:, :], raw_1a[:, :])
            nc.scalar.copy(w1_s[:, :], raw_1b[:, :]).then_inc(rounded, 1)
            nc.scalar.copy(w2_hl[:, :, 0, :], raw_2[:, :, :]).then_inc(rounded, 1)
            act.wait_ge(small, (VECTORS + 2 * FCH) * 16)

            def ln_transposed(b):
                act.wait_ge(turned, b + 1)
                after(act, ln_ready, b)
                for c in range(2):
                    ins = nc.scalar.activation(ln_t[:, c, :], ln_bank[:, c * SEQ:(c + 1) * SEQ], ACT.Identity,
                                               bias=shift[:, c:c + 1], scale=gain[:, c:c + 1])
                ins.then_inc(lnt_ready, 1)

            def gate(b, j):
                act.wait_ge(hid_filled, b * FCH + j + 1)
                nc.scalar.activation(gated[:, j, :], hid_bank[j][:, SEQ:2 * SEQ], ACT.Gelu_apprx_tanh,
                                     bias=b1_col[:, FCH + j:FCH + j + 1]).then_inc(gelu_ready, 1)

            def high(b, parity, j):
                act.wait_ge(hid_ready, b * FCH + j + 1)
                nc.scalar.copy(hid_h[parity][:, j, :], hid[:, j, :]).then_inc(hid_hi, 1)

            def period(cur, prev, nxt):
                if cur is None:
                    return
                b, parity = cur
                for j in range(FCH):
                    if j == 3 and nxt is not None:
                        ln_transposed(nxt[0])
                    gate(b, j)
                    if j >= 1:
                        high(b, parity, j - 1)
                high(b, parity, FCH - 1)

            ln_transposed(0)
            batches(act, period)

        @block.vector
        def _(dve):
            half = slice(P // 2, P)

            def statistics(b):
                for t in range(QT):
                    nc.vector.bn_stats(stats[:, t, :], x[:, b * QT + t, :]).then_inc(stats_ready, 1)
                dve.wait_ge(stats_ready, b * QT + QT)
                nc.vector.tensor_copy(stats_seen[:, :], stats[:, :, 0])
                for t in range(QT):
                    ins = nc.vector.bn_aggr(mean_var[:, t, :], stats[:, t, :])
                ins.then_inc(var_ready, 1)

            def normalise(b):
                dve.wait_ge(rstd_ready, b + 1)
                for t in range(QT):
                    row = x[:, b * QT + t, :]
                    nc.vector.tensor_scalar(xn[:, t, 0, :], row[:, 0:HA], mean_var[:, t, 0:1], rstd[:, t:t + 1],
                                            ALU.subtract, ALU.mult)
                    ins = nc.vector.tensor_scalar(xn[:, t, 1, :].rearrange("p (r f) -> p r f", r=REP),
                                                  row[:, None, HA:HID].to_broadcast([P, REP, HB]),
                                                  mean_var[:, t, 0:1], rstd[:, t:t + 1], ALU.subtract, ALU.mult)
                ins.then_inc(xn_ready, 1)

            def ln_parts(b, parity):
                h, low = ln_h[parity], ln_l[parity]
                dve.wait_ge(lnt_ready, b + 1)
                nc.vector.tensor_copy(h[:, :, :], ln_t[:, :, :]).then_inc(ln_hi, 1)
                dve.wait_ge(ln_hi, b + 1)
                nc.vector.tensor_tensor(low[:, :], ln_t[:, 0, :], h[:, 0, :], ALU.subtract)
                nc.vector.tensor_tensor(h[HB:2 * HB, 1, :], ln_t[HB:2 * HB, 1, :], h[HB:2 * HB, 1, :], ALU.subtract)
                nc.vector.tensor_tensor(h[3 * HB:P, 1, :], ln_t[3 * HB:P, 1, :], h[3 * HB:P, 1, :],
                                        ALU.subtract).then_inc(ln_ready, 1)

            def period(cur, prev, nxt):
                if nxt is not None:
                    statistics(nxt[0])
                for j in range(FCH):
                    if j == 3 and nxt is not None:
                        ln_parts(*nxt)
                    if j in (3, 4) and prev is not None:
                        b, t = prev[0], j - 3
                        dve.wait_ge(x_b2_ready, b + 1)
                        dve.wait_ge(out_filled, b * QT + t + 1)
                        row = x[:, b * QT + t, :]
                        nc.vector.tensor_tensor(row, out_bank[t][:, 0:HID], row, ALU.add).then_inc(part_ready, 1)
                        dve.wait_ge(part_ready, b * QT + t + 1)
                        nc.vector.tensor_tensor(row, out_bank[t][:, HID:2 * HID], row, ALU.add).then_inc(y_ready, 1)
                    if cur is not None:
                        b, parity = cur
                        dve.wait_ge(gelu_ready, b * FCH + j + 1)
                        after(dve, hid_lo, (b - 1) * FCH + j + 1)
                        nc.vector.scalar_tensor_tensor(hid[:, j, :], hid_bank[j][:, 0:SEQ], b1_col[:, j:j + 1],
                                                       gated[:, j, :], ALU.add, ALU.mult).then_inc(hid_ready, 1)
                    if j == 0 and nxt is not None:
                        normalise(nxt[0])

            nc.vector.memset(half_neg[:, :], -0.5)
            nc.vector.memset(eps[:, :], EPS).then_inc(weights_ready, 1)
            statistics(0)
            normalise(0)
            dve.wait_ge(rounded, 1)
            nc.vector.tensor_tensor(w1_l[:, :], raw_1a[:, :], w1_h[:, :], ALU.subtract)
            nc.vector.tensor_tensor(w1_s[half, :], raw_1b[half, :], w1_s[half, :], ALU.subtract)
            dve.wait_ge(rounded, 2)
            nc.vector.tensor_tensor(w2_hl[:, :, 1, :], raw_2[:, :, :], w2_hl[:, :, 0, :], ALU.subtract).then_inc(weights_ready, 1)
            ln_parts(0, 0)
            batches(dve, period)

        @block.tensor
        def _(pe):
            def turn(b):
                pe.wait_ge(xn_ready, b + 1)
                after(pe, lnt_ready, b)
                for c in range(2):
                    for t in range(QT):
                        mm = nc.tensor.transpose(ln_bank[:, c * SEQ + t * P:c * SEQ + (t + 1) * P], xn[:, t, c, :], ident[:, :])
                mm.then_inc(turned, 1)

            def hidden(b, parity, j):
                after(pe, hid_ready, (b - 1) * FCH + j + 1)
                h, low = ln_h[parity], ln_l[parity]
                for c in range(2):
                    col = slice((c * FCH + j) * P, (c * FCH + j + 1) * P)
                    out = hid_bank[j][:, c * SEQ:(c + 1) * SEQ]
                    nc.tensor.matmul(out, w1_h[:, col], h[:, 0, :], start=True, stop=False)
                    nc.tensor.matmul(out, w1_h[:, col], low[:, :], start=False, stop=False)
                    nc.tensor.matmul(out, w1_l[:, col], h[:, 0, :], start=False, stop=False)
                    mm = nc.tensor.matmul(out, w1_s[:, col], h[:, 1, :], start=False, stop=True)
                mm.then_inc(hid_filled, 1)

            def output(b, parity, t):
                pe.wait_ge(hid_lo, (b + 1) * FCH)
                for k in range(FCH):
                    for c, lhs in enumerate((hid_h, hid_l)):
                        mm = nc.tensor.matmul(out_bank[t][:, 0:2 * HID], lhs[parity][:, k, t * P:(t + 1) * P],
                                              w2_hl[:, k, :, :].rearrange("p a n -> p (a n)"),
                                              start=k == 0 and c == 0, stop=k == FCH - 1 and c == 1)
                mm.then_inc(out_filled, 1)

            def period(cur, prev, nxt):
                for j in range(FCH):
                    if cur is not None:
                        if j == 0:
                            pe.wait_ge(ln_ready, cur[0] + 1)
                        hidden(*cur, j)
                    if j in (2, 3) and prev is not None:
                        output(*prev, j - 2)
                    if j == 2 and nxt is not None:
                        turn(nxt[0])

            turn(0)
            pe.wait_ge(weights_ready, 2)
            batches(pe, period)


RAW_LOADS = 7
CONSTANT_LOADS = 2


AH, AD, APAD = 8, 20, 32
APAIRS = AH // 2
TOK = 4
KEYS = CTX - TOK
AV = AD + 1
HT = AH * TOK


def shape_constants():
    head_of = np.arange(HID) // AD
    index = np.linspace(0, CDIM - 1, SEQ).astype(np.int64)
    parts = {
        "ident": np.eye(P),
        "pick": np.arange(P)[:, None] == index[None, :],
        "ht_mask": (np.arange(P)[:, None] % HT // TOK) == np.arange(AH)[None, :],
        "ht_feature": (np.arange(P)[:, None] // TOK) == head_of[None, :],
        "feature_a": head_of[:HA, None] == np.arange(AH)[None, :],
        "feature_b": np.tile(head_of[HA:, None] == np.arange(AH)[None, :], (REP, 1)),
        "neg_eye": -1.0 * (np.arange(P)[:, None] - CDIM == np.arange(AH)[None, :]),
    }
    columns, at = {}, 0
    for what, part in parts.items():
        columns[what] = (at, part.shape[1])
        at += part.shape[1]
    return np.concatenate([np.asarray(v, np.float32) for v in parts.values()], axis=1), columns


def pad_heads(engine_copy, out, raw):
    return engine_copy(out[:, :, 0:AD], raw.rearrange("p (h d) -> p h d", d=AD))


def adapter_queries(nc, x, x_dram, const, load_constants, ctx_dram, wq_ca, wk_ca, wv_ca, raw, load_raw, self_weights, branch):
    name = "aq"
    SCALE = float(AD) ** -0.5
    stack = ExitStack()
    with stack:
        def sb(what, shape, dt):
            return stack.enter_context(nc.sbuf_tensor(f"{name}_{what}", shape, dt))

        def bank(what):
            return stack.enter_context(nc.psum_tensor(f"{name}_{what}", [P, 512], F32))

        def sem(what):
            return stack.enter_context(nc.semaphore(f"{name}_{what}"))

        wq_pad = sb("wq_pad", [P, 2, AH, APAD], F32)
        wk_pad = sb("wk_pad", [CDIM, AH, APAD], F32)
        raw_k = sb("raw_k", [CDIM, HID], F32)
        self_weights.allocate_raw(stack)
        wqca = sb("wqca", [TOK, HID + 3 * HB], F32)
        wv = sb("wv", [CDIM, HID], F32)
        wo = raw["wo"]
        wqt = sb("wqt", [P, 2, HID], F32)
        wkt = sb("wkt", [P, 2, CDIM], F32)
        qk = sb("qk", [CDIM, AH, HID], F32)
        wqca_t = sb("wqca_t", [P, 2, TOK], F32)
        diag = sb("diag", [P, 2, 4, HT], F32)
        diag_h = sb("diag_h", [P, 2, 4, HT], F32R)
        diag_l = sb("diag_l", [P, 4, HT], F32R)
        c_rep = sb("c_rep", [3 * HT, NB, CDIM], F32)
        c_s = sb("c_s", [3 * HT, NB, CDIM], F32R)
        c_t = sb("c_t", [CDIM, NB, HT], F32)
        g2 = sb("g2", [P, 2, NB, HT], F32)
        v2 = sb("v2", [HT, NB, HID], F32)
        two = range(2)
        xr = [sb(f"xr{i}", [P, QT, 2, P], F32) for i in two]
        x_h = [sb(f"x_h{i}", [P, 2, SEQ], F32R) for i in two]
        x_l = [sb(f"x_l{i}", [P, SEQ], F32R) for i in two]
        r_s = [sb(f"r_s{i}", [P, SEQ], F32R) for i in two]
        c_m = [sb(f"c_m{i}", [P, AH, CDIM], F32R) for i in two]
        maxima = [sb(f"maxima{i}", [CDIM, P], F32) for i in two]
        xv_h = [sb(f"xv_h{i}", [P, QT, AH, AV], BF16) for i in two]
        xv_l = [sb(f"xv_l{i}", [P, QT, AH, AV], F16) for i in two]
        WIDE = AH * CDIM + P - CDIM
        probs = [sb(f"probs{i}", [P, QT, WIDE], F32) for i in two]
        probs_l = [sb(f"probs_l{i}", [P, QT, WIDE], F16) for i in two]
        recip = [sb(f"recip{i}", [CDIM, AH], F32) for i in two]
        hs1 = [sb(f"hs1{i}", [CDIM, HID], F32) for i in two]
        hs1_t = [sb(f"hs1_t{i}", [P, 2, CDIM], F32) for i in two]
        top2 = [sb(f"top2{i}", [CDIM, AH], F32) for i in two]
        s2 = [sb(f"s2{i}", [CDIM, AH, TOK], F32) for i in two]
        p2 = [sb(f"p2{i}", [CDIM, AH, TOK], F32) for i in two]
        sum2 = [sb(f"sum2{i}", [CDIM, AH], F32) for i in two]
        rec2 = [sb(f"rec2{i}", [CDIM, AH], F32) for i in two]
        p2n = [sb(f"p2n{i}", [CDIM, AH, TOK], F32) for i in two]
        p2_t = [sb(f"p2_t{i}", [HT, CDIM], F32) for i in two]
        hs2_t = [sb(f"hs2_t{i}", [P, 2, CDIM], F32) for i in two]

        turn_bank, row_bank = bank("turn"), bank("row")
        max_bank = [bank(f"max{i}") for i in two]
        score_bank = [bank(f"score{i}") for i in two]
        pv_bank, chain_bank = bank("pv"), bank("chain")
        tile_bank = [max_bank[0], max_bank[1], pv_bank, chain_bank]

        loaded = sem("loaded")
        x_in = sem("x_in")
        padded = sem("padded")
        zeroed = sem("zeroed")
        setup_pe = sem("setup_pe")
        setup_dve = sem("setup_dve")
        ready = sem("ready")
        xr_ready = sem("xr_ready")
        x_turned = sem("x_turned")
        x_hi = sem("x_hi")
        x_ready = sem("x_ready")
        r_filled = sem("r_filled")
        r_hi = sem("r_hi")
        r_ready = sem("r_ready")
        cm_ready = sem("cm_ready")
        max_filled = sem("max_filled")
        max_read = sem("max_read")
        mt_filled = sem("mt_filled")
        shift_ready = sem("shift_ready")
        scored = sem("scored")
        exped = sem("exped")
        probs_split = sem("probs_split")
        xv_hi = sem("xv_hi")
        xv_ready = sem("xv_ready")
        pv_done = sem("pv_done")
        recip_ready = sem("recip_ready")
        hs1_ready = sem("hs1_ready")
        chain_filled = sem("chain_filled")
        chain_read = sem("chain_read")
        soft2 = sem("soft2")
        exp2 = sem("exp2")
        p2_ready = sem("p2_ready")
        branch_hi = sem("branch_hi")

        block = stack.enter_context(nc.Block())
        STEPS = NB + 4

        weight_steps = [1, 2, 3, 4, 5, 6, 8]

        @block.sync
        def _(sp):
            load_constants(sp, loaded)
            sp.dma_start(raw_k[:, :], wk_ca).then_inc(loaded, 16)
            sp.dma_start(wqca[:, 0:HID], wq_ca).then_inc(loaded, 16)
            sp.dma_start(wqca[:, HID:HID + 3 * HB].rearrange("p (r f) -> p r f", r=3),
                         wq_ca[:, None, HA:HID].to_broadcast([TOK, 3, HB])).then_inc(loaded, 16)
            load_raw(sp)
            for b in range(NB):
                sp.dma_start(c_rep[:, b, :], ctx_dram[b, KEYS:CTX, :][None, :, :].to_broadcast([3 * AH, TOK, CDIM])).then_inc(loaded, 16)
            sp.dma_start(wv[:, :], wv_ca).then_inc(loaded, 16)
            sp.dma_start(x[:, :, :], x_dram.rearrange("b (t p) h -> p (b t) h", p=P)).then_inc(x_in, 16)
            self_weights.load(sp)
        LOADS = CONSTANT_LOADS + 4 + NB

        @block.gpsimd
        def _(pool):
            nc.gpsimd.memset(wq_pad[:, :, :, :], 0.0)
            nc.gpsimd.memset(wk_pad[:, :, :], 0.0).then_inc(zeroed, 1)
            nc.gpsimd.memset(diag[:, :, :, :], 0.0)
            for i in two:
                nc.gpsimd.memset(maxima[i][:, :], 0.0)
                nc.gpsimd.memset(probs[i][:, :, AH * CDIM:WIDE], 0.0)
                nc.gpsimd.memset(probs_l[i][:, :, AH * CDIM:WIDE], 0.0)
                nc.gpsimd.memset(xv_h[i][:, :, :, AD:AV], 1.0)
                ins = nc.gpsimd.memset(xv_l[i][:, :, :, AD:AV], 0.0)
            ins.then_inc(zeroed, 1)

            def mask_tokens(b):
                after(pool, scored, (b - 2) * 4 + 4)
                nc.gpsimd.tensor_tensor(c_m[b % 2][0:3 * HT, :, :], c_s[:, b, None, :].to_broadcast([3 * HT, AH, CDIM]),
                                        const["ht_mask"][0:3 * HT, :, None].to_broadcast([3 * HT, AH, CDIM]),
                                        ALU.mult).then_inc(cm_ready, 1)

            def split(b):
                for n in range(4):
                    pool.wait_ge(exped, b * 4 + n + 1)
                    t, cols = n // 2, slice(n % 2 * 4 * CDIM, (n % 2 + 1) * 4 * CDIM)
                    whole = probs[b % 2][:, t, cols]
                    nc.gpsimd.tensor_tensor(probs_l[b % 2][:, t, cols], whole, whole.bitcast(BF16)[:, 1::2],
                                            ALU.subtract).then_inc(probs_split, 1)

            pool.wait_ge(ready, 1)
            for step in range(STEPS):
                if 0 <= step - 2 < NB:
                    split(step - 2)
                if step < NB:
                    mask_tokens(step)

        @block.scalar
        def _(act):
            act.wait_ge(zeroed, 1)
            act.wait_ge(loaded, LOADS * 16)
            act.wait_ge(raw["loaded"], RAW_LOADS * 16)
            pad_heads(nc.scalar.copy, wq_pad[:, 0, :, :], raw["wq"][:, 0, :])
            pad_heads(nc.scalar.copy, wq_pad[0:HB, 1, :, :], raw["wq"][0:HB, 1, :])
            pad_heads(nc.scalar.copy, wk_pad[:, :, :], raw_k[:, :]).then_inc(padded, 1)

            def x_part(b):
                act.wait_ge(x_turned, b + 1)
                nc.scalar.copy(x_h[b % 2][:, :, :], turn_bank[:, :].rearrange("p (c q) -> p c q", c=2)).then_inc(x_hi, 1)

            def value_part(b):
                after(act, pv_done, b - 1)
                nc.scalar.copy(xv_h[b % 2][:, :, :, 0:AD],
                               x[:, b * QT:(b + 1) * QT, :].rearrange("p t (h d) -> p t h d", d=AD)).then_inc(xv_hi, 1)

            def row_part(b):
                act.wait_ge(r_filled, b + 1)
                after(act, scored, (b - 1) * 4)
                nc.scalar.copy(r_s[b % 2][0:3 * HT, :], row_bank[0:3 * HT, 0:SEQ]).then_inc(r_hi, 1)

            def exponential(b, n):
                after(act, pv_done, b - 1)
                act.wait_ge(scored, b * 4 + n + 1)
                nc.scalar.activation(probs[b % 2][:, n // 2, n % 2 * 4 * CDIM:(n % 2 + 1) * 4 * CDIM],
                                     score_bank[n % 2][:, 0:4 * CDIM], ACT.Exp, scale=SCALE).then_inc(exped, 1)

            def second_scores(b):
                act.wait_ge(chain_filled, b * 5 + 1)
                nc.scalar.copy(hs1_t[b % 2][:, 0, :], chain_bank[:, 0:CDIM])
                nc.scalar.copy(hs1_t[b % 2][0:HB, 1, :], chain_bank[0:HB, CDIM:2 * CDIM]).then_inc(chain_read, 1)
                act.wait_ge(soft2, b * 4 + 2)
                nc.scalar.activation(p2[b % 2][:, :, :], s2[b % 2][:, :, :], ACT.Exp, scale=SCALE).then_inc(exp2, 1)

            def second_turned(b):
                act.wait_ge(chain_filled, b * 5 + 3)
                nc.scalar.copy(p2_t[b % 2][:, :], chain_bank[0:HT, 0:CDIM]).then_inc(chain_read, 1)

            def second_values(b):
                act.wait_ge(chain_filled, b * 5 + 4)
                nc.scalar.copy(hs2_t[b % 2][:, 0, :], chain_bank[:, 0:CDIM])
                nc.scalar.copy(hs2_t[b % 2][0:HB, 1, :], chain_bank[0:HB, CDIM:2 * CDIM]).then_inc(chain_read, 1)

            def branch_part(b):
                act.wait_ge(chain_filled, b * 5 + 5)
                nc.scalar.copy(branch[:, b, 0, :], chain_bank[0:CDIM, 0:HID]).then_inc(branch_hi, 1)

            act.wait_ge(ready, 1)
            for step in range(STEPS):
                if step in weight_steps:
                    self_weights.high(act, weight_steps.index(step))
                for lag, part, *n in ((2, exponential, 0), (0, x_part), (1, value_part), (4, second_turned), (2, exponential, 1),
                                      (4, second_values), (2, exponential, 2), (2, exponential, 3), (0, row_part),
                                      (4, branch_part), (3, second_scores)):
                    if 0 <= step - lag < NB:
                        part(step - lag, *n)

        @block.vector
        def _(dve):
            count = [0]

            def told(ins):
                count[0] += 1
                ins.then_inc(setup_dve, 1)

            half = slice(P // 2, P)
            dve.wait_ge(loaded, LOADS * 16)
            told(nc.vector.tensor_copy(c_s[:, :, :], c_rep[:, :, :]))
            dve.wait_ge(setup_dve, 1)
            told(nc.vector.tensor_tensor(c_s[HT:2 * HT, :, :], c_rep[HT:2 * HT, :, :], c_s[HT:2 * HT, :, :], ALU.subtract))
            for i in two:
                nc.vector.memset(r_s[i][3 * HT:P, :].bitcast(F32), 1.0)
            for k in two:
                dve.wait_ge(setup_pe, k + 1)
                nc.vector.tensor_copy(wqt[:, k, :], score_bank[k][:, 0:HID])
                told(nc.vector.tensor_copy(wkt[:, k, :], score_bank[k][:, HID:HID + CDIM]))
            dve.wait_ge(setup_pe, 3)
            told(nc.vector.tensor_copy(wqca_t[:, :, :], turn_bank[:, 0:2 * TOK].rearrange("p (c t) -> p c t", c=2)))
            dve.wait_ge(setup_pe, 4)
            told(nc.vector.tensor_copy(c_t[:, :, :], row_bank[0:CDIM, 0:NB * HT].rearrange("p (b r) -> p b r", b=NB)))
            dve.wait_ge(setup_dve, 5)
            dve.wait_ge(zeroed, 2)
            for i, m in enumerate(("feature_a", "feature_b")):
                for r in range(3):
                    ins = nc.vector.tensor_tensor(diag[:, i, r, :].rearrange("p (h t) -> p h t", t=TOK),
                                                  wqca_t[:, i, None, :].to_broadcast([P, AH, TOK]),
                                                  const[m][:, :, None].to_broadcast([P, AH, TOK]), ALU.mult)
            told(ins)
            dve.wait_ge(setup_dve, 7)
            told(nc.vector.tensor_copy(diag_h[:, :, :, :], diag[:, :, :, :]))
            dve.wait_ge(setup_dve, 8)
            nc.vector.tensor_tensor(diag_l[:, :, :], diag[:, 0, :, :], diag_h[:, 0, :, :], ALU.subtract)
            told(nc.vector.tensor_tensor(diag_h[half, 1, :, :], diag[half, 1, :, :], diag_h[half, 1, :, :], ALU.subtract))
            for n in range(4):
                dve.wait_ge(setup_pe, 5 + n)
                told(nc.vector.tensor_copy(qk[:, n::4, :],
                                           tile_bank[n][0:CDIM, 0:2 * HID].rearrange("p (h e) -> p h e", e=HID)))
            dve.wait_ge(setup_pe, 9)
            for i in two:
                rows = slice(0, P if i == 0 else HB)
                ins = nc.vector.tensor_copy(g2[rows, i, :, :].rearrange("p b (h t) -> p b h t", t=TOK),
                                            score_bank[i][rows, 0:AH * NB * TOK].rearrange("p (h b t) -> p b h t", h=AH, b=NB))
            told(ins)
            for n, b in enumerate(range(0, NB, 3)):
                batches = min(3, NB - b)
                dve.wait_ge(setup_pe, 10 + n)
                ins = nc.vector.tensor_tensor(v2[:, b:b + batches, :],
                                              [turn_bank, row_bank, chain_bank][n][0:HT, 0:batches * HID].rearrange("p (b e) -> p b e", e=HID),
                                              const["ht_feature"][0:HT, None, :].to_broadcast([HT, batches, HID]), ALU.mult)
            told(ins)
            dve.wait_ge(setup_dve, count[0])
            nc.vector.memset(recip[0][:, :], 0.0).then_inc(ready, 1)

            def a0(b):
                after(dve, x_turned, b - 1)
                nc.vector.tensor_copy(xr[b % 2][:, :, 0, :], x[:, b * QT:(b + 1) * QT, 0:HA])
                nc.vector.tensor_copy(xr[b % 2][:, :, 1, :].rearrange("p t (r f) -> p t r f", r=REP),
                                      x[:, b * QT:(b + 1) * QT, None, HA:HID].to_broadcast([P, QT, REP, HB])).then_inc(xr_ready, 1)

            def x_part(b):
                i = b % 2
                dve.wait_ge(x_hi, b + 1)
                nc.vector.tensor_tensor(x_l[i][:, :], turn_bank[:, 0:SEQ], x_h[i][:, 0, :], ALU.subtract)
                nc.vector.tensor_tensor(x_h[i][HB:2 * HB, 1, :], turn_bank[HB:2 * HB, SEQ:2 * SEQ], x_h[i][HB:2 * HB, 1, :], ALU.subtract)
                nc.vector.tensor_tensor(x_h[i][3 * HB:P, 1, :], turn_bank[3 * HB:P, SEQ:2 * SEQ], x_h[i][3 * HB:P, 1, :],
                                        ALU.subtract).then_inc(x_ready, 1)

            def value_part(b):
                dve.wait_ge(xv_hi, b + 1)
                nc.vector.tensor_tensor(xv_l[b % 2][:, :, :, 0:AD],
                                        x[:, b * QT:(b + 1) * QT, :].rearrange("p t (h d) -> p t h d", d=AD),
                                        xv_h[b % 2][:, :, :, 0:AD], ALU.subtract).then_inc(xv_ready, 1)

            def row_part(b):
                rows = slice(2 * HT, 3 * HT)
                dve.wait_ge(r_hi, b + 1)
                nc.vector.tensor_tensor(r_s[b % 2][rows, :], row_bank[rows, 0:SEQ], r_s[b % 2][rows, :],
                                        ALU.subtract).then_inc(r_ready, 1)

            def top(b, n):
                dve.wait_ge(max_filled, b * APAIRS + n + 1)
                nc.vector.reduce_max(maxima[b % 2][:, CDIM + 2 * n:CDIM + 2 * n + 2],
                                     max_bank[n % 2][0:CDIM, :].rearrange("p (h k) -> p h k", h=2), AX.X).then_inc(max_read, 1)

            def write_shift(b):
                dve.wait_ge(mt_filled, b + 1)
                rows = slice(CDIM, P)
                nc.vector.tensor_tensor(c_m[b % 2][rows, :, :], row_bank[rows, None, 0:CDIM].to_broadcast([P - CDIM, AH, CDIM]),
                                        const["neg_eye"][rows, :, None].to_broadcast([P - CDIM, AH, CDIM]), ALU.mult).then_inc(shift_ready, 1)

            def norm(b):
                dve.wait_ge(pv_done, b + 1)
                sums = pv_bank[0:CDIM, 0:AH * AV].rearrange("p (h d) -> p h d", d=AV)
                nc.vector.reciprocal(recip[b % 2][:, :], sums[:, :, AD]).then_inc(recip_ready, 1)
                dve.wait_ge(recip_ready, b + 1)
                nc.vector.tensor_tensor(hs1[b % 2][:, :].rearrange("p (h d) -> p h d", d=AD), sums[:, :, 0:AD],
                                        recip[b % 2][:, :, None].to_broadcast([CDIM, AH, AD]), ALU.mult).then_inc(hs1_ready, 1)

            def second_scores(b):
                i, n = b % 2, b * 4
                scores = chain_bank[0:CDIM, 0:HT].rearrange("p (h t) -> p h t", t=TOK)
                dve.wait_ge(chain_filled, b * 5 + 2)
                nc.vector.reduce_max(top2[i][:, :], scores, AX.X).then_inc(soft2, 1)
                dve.wait_ge(soft2, n + 1)
                nc.vector.tensor_tensor(s2[i][:, :, :], scores, top2[i][:, :, None].to_broadcast([CDIM, AH, TOK]),
                                        ALU.subtract).then_inc(soft2, 1)
                dve.wait_ge(exp2, b + 1)
                nc.vector.reduce_sum(sum2[i][:, :], p2[i][:, :, :], AX.X).then_inc(soft2, 1)
                dve.wait_ge(soft2, n + 3)
                nc.vector.reciprocal(rec2[i][:, :], sum2[i][:, :]).then_inc(soft2, 1)
                dve.wait_ge(soft2, n + 4)
                nc.vector.tensor_tensor(p2n[i][:, :, :], p2[i][:, :, :], rec2[i][:, :, None].to_broadcast([CDIM, AH, TOK]),
                                        ALU.mult).then_inc(p2_ready, 1)

            def branch_part(b):
                dve.wait_ge(branch_hi, b + 1)
                nc.vector.tensor_tensor(branch[:, b, 1, :], chain_bank[0:CDIM, 0:HID], branch[:, b, 0, :],
                                        ALU.subtract).then_inc(chain_read, 1)

            dve.wait_ge(x_in, 16)
            a0(0)
            for step in range(STEPS):
                for lag, part, *n in ((0, x_part), (1, top, 0), (-1, a0), (1, top, 1), (1, value_part), (1, top, 2),
                                      (0, row_part), (4, branch_part), (1, top, 3), (1, write_shift),
                                      (3, second_scores)):
                    if 0 <= step - lag < NB:
                        part(step - lag, *n)
                if step in weight_steps:
                    self_weights.low(dve, weight_steps.index(step))
                if 0 <= step - 2 < NB:
                    norm(step - 2)

        @block.tensor
        def _(pe):
            ident = const["ident"]
            pe.wait_ge(loaded, LOADS * 16)
            pe.wait_ge(padded, 1)
            for k in two:
                heads = slice(4 * k, 4 * k + 4)
                out = score_bank[k]
                nc.tensor.transpose(out[:, 0:HA], wq_pad[:, 0, heads, :].rearrange("p h d -> p (h d)"), ident)
                nc.tensor.transpose(out[:, HA:HID], wq_pad[0:HB, 1, heads, :].rearrange("p h d -> p (h d)"), ident[0:HB, 0:HB])
                nc.tensor.transpose(out[:, HID:HID + CDIM], wk_pad[:, heads, :].rearrange("p h d -> p (h d)"),
                                    ident[0:CDIM, 0:CDIM]).then_inc(setup_pe, 1)
            nc.tensor.transpose(turn_bank[:, 0:TOK], wqca[:, 0:HA], ident[0:TOK, 0:TOK])
            nc.tensor.transpose(turn_bank[:, TOK:2 * TOK], wqca[:, HA:HA + P], ident[0:TOK, 0:TOK]).then_inc(setup_pe, 1)
            for b in range(NB):
                mm = nc.tensor.transpose(row_bank[0:CDIM, b * HT:(b + 1) * HT], c_rep[0:HT, b, :], ident[0:HT, 0:HT])
            mm.then_inc(setup_pe, 1)
            pe.wait_ge(setup_dve, 4)
            for n in range(4):
                rows = slice(n * APAD, (n + 1) * APAD)
                for k in two:
                    mm = nc.tensor.matmul(tile_bank[n][0:CDIM, k * HID:(k + 1) * HID], wkt[rows, k, :], wqt[rows, k, :],
                                          start=True, stop=True)
                mm.then_inc(setup_pe, 1)
            pe.wait_ge(setup_dve, 13)
            for h in range(AH):
                cols = slice(h * NB * TOK, (h + 1) * NB * TOK)
                nc.tensor.matmul(score_bank[0][:, cols], qk[:, h, 0:HA], c_t[:, :, 0:TOK], start=True, stop=True)
                mm = nc.tensor.matmul(score_bank[1][0:HB, cols], qk[:, h, HA:HID], c_t[:, :, 0:TOK], start=True, stop=True)
            mm.then_inc(setup_pe, 1)
            for n, b0 in enumerate(range(0, NB, 3)):
                out = [turn_bank, row_bank, chain_bank][n]
                for b in range(b0, min(b0 + 3, NB)):
                    mm = nc.tensor.matmul(out[0:HT, (b - b0) * HID:(b - b0 + 1) * HID], c_t[:, b, :], wv[:, :], start=True, stop=True)
                mm.then_inc(setup_pe, 1)
            pe.wait_ge(ready, 1)

            def a(b):
                i = b % 2
                pe.wait_ge(xr_ready, b + 1)
                after(pe, x_ready, b)
                for c in range(2):
                    for t in range(QT):
                        mm = nc.tensor.transpose(turn_bank[:, c * SEQ + t * P:c * SEQ + (t + 1) * P], xr[i][:, t, c, :], ident)
                mm.then_inc(x_turned, 1)

            def rows(b):
                i = b % 2
                pe.wait_ge(x_ready, b + 1)
                after(pe, shift_ready, b - 1)
                after(pe, r_ready, b)
                out = row_bank[:, 0:SEQ]
                passes = [(diag_h[:, 0], x_h[i][:, 0, :]), (diag_h[:, 0], x_l[i][:, :]), (diag_l[:, :, :], x_h[i][:, 0, :]),
                          (diag_h[:, 1], x_h[i][:, 1, :])]
                for n, (lhs, rhs) in enumerate(passes):
                    mm = nc.tensor.matmul(out, lhs.rearrange("p r c -> p (r c)"), rhs, start=n == 0, stop=n == 3)
                mm.then_inc(r_filled, 1)

            def top(b, n):
                i = b % 2
                if n == 0:
                    pe.wait_ge(r_ready, b + 1)
                    pe.wait_ge(cm_ready, b + 1)
                after(pe, max_read, b * APAIRS + n - 1)
                for j in range(2):
                    mm = nc.tensor.matmul(max_bank[n % 2][0:CDIM, j * SEQ:(j + 1) * SEQ], c_m[i][0:3 * HT, 2 * n + j, :],
                                          r_s[i][0:3 * HT, :], start=True, stop=True)
                mm.then_inc(max_filled, 1)

            def top_turned(b):
                pe.wait_ge(max_read, (b + 1) * APAIRS)
                pe.wait_ge(r_ready, min(b + 2, NB))
                nc.tensor.transpose(row_bank[:, 0:CDIM], maxima[b % 2][:, :], ident[0:CDIM, 0:CDIM]).then_inc(mt_filled, 1)

            def score(b, n):
                i = b % 2
                pe.wait_ge(shift_ready, b + 1)
                after(pe, exped, b * 4 + n - 1)
                t, heads = n // 2, slice(n % 2 * 4, n % 2 * 4 + 4)
                nc.tensor.matmul(score_bank[n % 2][:, 0:4 * CDIM], r_s[i][:, t * P:(t + 1) * P], c_m[i][:, heads, :],
                                 start=True, stop=True).then_inc(scored, 1)

            def weigh(b):
                i = b % 2
                pe.wait_ge(probs_split, b * 4 + 4)
                pe.wait_ge(xv_ready, b + 1)
                after(pe, hs1_ready, b)
                for h in range(AH):
                    n = 0
                    for t in range(QT):
                        cols = slice(h * CDIM, h * CDIM + P)
                        hi = probs[i][:, t, :].bitcast(BF16)[:, 1::2][:, cols]
                        for lhs, rhs in ((hi, xv_h), (hi, xv_l), (probs_l[i][:, t, cols], xv_h)):
                            mm = nc.tensor.matmul(pv_bank[:, h * AV:(h + 1) * AV], lhs, rhs[i][:, t, h, :],
                                                  start=n == 0, stop=n == 3 * QT - 1)
                            n += 1
                mm.then_inc(pv_done, 1)

            def link(b, n):
                after(pe, chain_read, b * 4 + n)

            def d1(b):
                pe.wait_ge(hs1_ready, b + 1)
                link(b, 0)
                nc.tensor.transpose(chain_bank[:, 0:CDIM], hs1[b % 2][:, 0:HA], ident[0:CDIM, 0:CDIM])
                nc.tensor.transpose(chain_bank[0:HB, CDIM:2 * CDIM], hs1[b % 2][:, HA:HID], ident[0:CDIM, 0:CDIM]).then_inc(chain_filled, 1)

            def d2(b):
                link(b, 1)
                out = chain_bank[0:CDIM, 0:HT]
                nc.tensor.matmul(out, hs1_t[b % 2][:, 0, :], g2[:, 0, b, :], start=True, stop=False)
                nc.tensor.matmul(out, hs1_t[b % 2][0:HB, 1, :], g2[0:HB, 1, b, :], start=False, stop=True).then_inc(chain_filled, 1)

            def e1(b):
                pe.wait_ge(p2_ready, b + 1)
                nc.tensor.transpose(chain_bank[0:HT, 0:CDIM], p2n[b % 2][:, :, :].rearrange("p h t -> p (h t)"),
                                    ident[0:CDIM, 0:CDIM]).then_inc(chain_filled, 1)

            def e2(b):
                link(b, 2)
                nc.tensor.matmul(chain_bank[:, 0:CDIM], v2[:, b, 0:HA], p2_t[b % 2][:, :], start=True, stop=True)
                nc.tensor.matmul(chain_bank[0:HB, CDIM:2 * CDIM], v2[:, b, HA:HID], p2_t[b % 2][:, :], start=True,
                                 stop=True).then_inc(chain_filled, 1)

            def e3(b):
                link(b, 3)
                out = chain_bank[0:CDIM, 0:HID]
                nc.tensor.matmul(out, hs2_t[b % 2][:, 0, :], wo[:, 0, :], start=True, stop=False)
                nc.tensor.matmul(out, hs2_t[b % 2][0:HB, 1, :], wo[0:HB, 1, :], start=False, stop=True).then_inc(chain_filled, 1)

            for step in range(STEPS):
                for lag, part, *n in ((2, score, 0), (0, a), (1, top, 0), (4, e1), (2, score, 1), (1, top, 1), (4, e2),
                                      (2, score, 2), (0, rows), (1, top, 2), (2, score, 3), (4, e3), (1, top, 3),
                                      (3, d1), (1, top_turned), (3, d2), (2, weigh)):
                    if 0 <= step - lag < NB:
                        part(step - lag, *n)


def prepare_adapter(nc, const, raw, wq_h, wq_l, wq_s, wv_h, wv_l, wo_a, wo_b, pick):
    name = "ap"
    stack = ExitStack()
    with stack:
        def sb(what, shape, dt):
            return stack.enter_context(nc.sbuf_tensor(f"{name}_{what}", shape, dt))

        def sem(what):
            return stack.enter_context(nc.semaphore(f"{name}_{what}"))

        wq_pad, wk_pad = sb("wq_pad", [P, 2, AH, APAD], F32), sb("wk_pad", [CDIM, AH, APAD], F32)
        raw_v, raw_o = raw["wv"][:, :].rearrange("p (h d) -> p h d", d=AD), raw["wo"]
        B4, A, K, W = 0, P, 2 * P, 2 * P + CDIM
        w_t = sb("w_t", [P, 2, W], F32)
        turned = [stack.enter_context(nc.psum_tensor(f"{name}_turned{i}", [P, 512], F32)) for i in range(2)]
        prod = [stack.enter_context(nc.psum_tensor(f"{name}_prod{i}", [P, 512], F32)) for i in range(4)]
        zeroed = sem("zeroed")
        padded = sem("padded")
        turned_done = sem("turned_done")
        turned_read = sem("turned_read")
        prod_done = sem("prod_done")
        prod_hi = sem("prod_hi")
        rounded = sem("rounded")

        with nc.Block() as block:
            @block.gpsimd
            def _(pool):
                for t in (wq_pad[:, :, :, :], wk_pad[:, :, :], wv_h[:, :, :].bitcast(F32), wv_l[:, :, :].bitcast(F32)):
                    nc.gpsimd.memset(t, 0.0).then_inc(zeroed, 1)

            @block.tensor
            def _(pe):
                ident = const["ident"]
                pe.wait_ge(padded, 1)
                for k in range(2):
                    heads, out = slice(4 * k, 4 * k + 4), turned[k]
                    nc.tensor.transpose(out[:, 0:HB], wq_pad[0:HB, 1, heads, :].rearrange("p h d -> p (h d)"), ident[0:HB, 0:HB])
                    nc.tensor.transpose(out[:, HB:HID], wq_pad[:, 0, heads, :].rearrange("p h d -> p (h d)"), ident)
                    nc.tensor.transpose(out[:, HID:HID + CDIM], wk_pad[:, heads, :].rearrange("p h d -> p (h d)"),
                                        ident[0:CDIM, 0:CDIM]).then_inc(turned_done, 1)
                pe.wait_ge(turned_read, 2)
                for n in range(4):
                    rows = slice(n * APAD, (n + 1) * APAD)
                    for k in range(2):
                        for c, part in enumerate((slice(A, K), slice(B4, A))):
                            at = (2 * k + c) * CDIM
                            mm = nc.tensor.matmul(prod[n][:, at:at + CDIM], w_t[rows, k, part], w_t[rows, k, K:W],
                                                  start=True, stop=True)
                    mm.then_inc(prod_done, 1)

            def product(n, c):
                return prod[n][:, 0:4 * CDIM].rearrange("p (k c e) -> p k c e", k=2, c=2)[:, :, c, :]

            @block.scalar
            def _(act):
                act.wait_ge(zeroed, 4)
                pad_heads(nc.scalar.copy, wk_pad[:, :, :], raw["wk"][:, :])
                pad_heads(nc.scalar.copy, wq_pad[:, 0, :, :], raw["wq"][:, 0, :])
                pad_heads(nc.scalar.copy, wq_pad[0:HB, 1, :, :], raw["wq"][0:HB, 1, :]).then_inc(padded, 1)
                nc.scalar.copy(wv_h[:, :, 0:AD], raw_v).then_inc(rounded, 1)
                nc.scalar.copy(wo_a[:, 0, :], raw_o[:, 0, :])
                nc.scalar.copy(wo_b[:, 0, :], raw_o[0:2 * HB, 1, :]).then_inc(rounded, 1)
                for n in range(4):
                    act.wait_ge(prod_done, n + 1)
                    nc.scalar.copy(wq_h[:, n::4, :], product(n, 0))
                    nc.scalar.copy(wq_s[:, n::4, :], product(n, 1)).then_inc(prod_hi, 1)

            @block.vector
            def _(dve):
                nc.vector.tensor_copy(pick[:, :], const["pick"][0:CDIM, :])
                for k in range(2):
                    dve.wait_ge(turned_done, k + 1)
                    nc.vector.tensor_copy(w_t[:, k, B4:A].rearrange("p (r f) -> p r f", r=REP),
                                          turned[k][:, None, 0:HB].to_broadcast([P, REP, HB]))
                    nc.vector.tensor_copy(w_t[:, k, A:W], turned[k][:, HB:HID + CDIM]).then_inc(turned_read, 1)
                dve.wait_ge(rounded, 1)
                nc.vector.tensor_tensor(wv_l[:, :, 0:AD], raw_v, wv_h[:, :, 0:AD], ALU.subtract)
                dve.wait_ge(rounded, 2)
                nc.vector.tensor_tensor(wo_a[:, 1, :], raw_o[:, 0, :], wo_a[:, 0, :], ALU.subtract)
                nc.vector.tensor_tensor(wo_b[:, 1, :], raw_o[0:2 * HB, 1, :], wo_b[:, 0, :], ALU.subtract)
                half = slice(P // 2, P)
                for n in range(4):
                    dve.wait_ge(prod_hi, n + 1)
                    nc.vector.tensor_tensor(wq_l[:, n::4, :], product(n, 0), wq_h[:, n::4, :], ALU.subtract)
                    nc.vector.tensor_tensor(wq_s[half, n::4, :], product(n, 1)[half], wq_s[half, n::4, :], ALU.subtract)


def adapter(nc, x, const, ctx_dram, raw, branch):
    name = "ad"
    SLOTS = 2 * APAIRS
    PERIODS = NB // 2
    END = SLOTS - 2
    KT = CTX // P
    KEY_ROWS = [P] * (KT - 1) + [KEYS - (KT - 1) * P]
    U = KT
    UP = U * SLOTS
    PR = 2 * U
    SCALE = float(AD) ** -0.5

    def extras(kind, s):
        prev, cur, nxt = kind != "first", kind != "tail", kind in ("first", "steady")
        table = {0: [(1, prev, ("ot", "prev", 0)), (2, cur, ("v", "cur", 0))],
                 1: [(0, prev, ("out", "prev", 0)), (2, prev, ("out", "prev", 1))],
                 2: [(0, cur, ("x", "cur", 1)), (2, cur, ("v", "cur", 1))],
                 3: [(1, cur, ("ctx", "cur", 1))],
                 4: [(1, prev, ("ot", "prev", 1)), (2, cur, ("v", "cur", 2))],
                 5: [(0, prev, ("out", "prev", 2)), (2, prev, ("out", "prev", 3)), (3, nxt, ("x", "nxt", 0))],
                 6: [(2, cur, ("v", "cur", 3))],
                 7: [(1, nxt, ("ctx", "nxt", 0))]}
        return [(at, key) for at, live, key in table[s] if live]

    def slot_keys(kind, s):
        keys = [] if kind == "tail" else [("proj", s)]
        if (kind != "tail") if s >= 2 else (kind != "first"):
            keys.append(("mt", s))
        return keys + [key for _, key in extras(kind, s)]

    def all_keys(kind):
        pre = [("ctx", "pre", 0), ("x", "pre", 0)] if kind == "first" else []
        return pre + [k for s in range(END if kind == "tail" else SLOTS) for k in slot_keys(kind, s)]

    ring = Ring(all_keys, PERIODS)

    def earlier(kind, period, key):
        return ring.number("last", PERIODS - 1, key) if kind == "tail" else ring.number("steady", period - 1, key)

    def unit_of(kind, s, period, what, lag):
        if s >= lag:
            return ring.number(kind, period, (what, s - lag))
        return earlier(kind, period, (what, s - lag + SLOTS))

    def context_number(kind, period, j):
        if j == 1:
            return ring.number(kind, period, ("ctx", "cur", 1))
        return 0 if kind == "first" else earlier(kind, period, ("ctx", "nxt", 0))

    def before(s, d, cur, prev):
        if s >= d:
            return None if cur is None else (cur, s - d)
        return None if prev is None else (prev, s - d + SLOTS)

    def run(slot):
        def whole(kind, r, prev, nxt):
            for s in range(SLOTS):
                slot(kind, s, r, r, prev, nxt)

        def program(engine):
            whole("first", 0, None, 1)
            with engine.Fori(0, PERIODS - 2) as i:
                whole("steady", i + 1, i, i + 2)
            whole("last", PERIODS - 1, PERIODS - 2, None)
            for s in range(END):
                slot("tail", s, PERIODS, None, PERIODS - 1, None)
        return program

    def batch_of(key, cur, prev, nxt):
        what, whose, i = key
        j = i // 2 if what in ("v", "out") else i
        return {"pre": 0, "cur": cur, "prev": prev, "nxt": nxt}[whose] * 2 + j, j

    stack = ExitStack()
    with stack:
        def sb(what, shape, dt):
            return stack.enter_context(nc.sbuf_tensor(f"{name}_{what}", shape, dt))

        def bank(what):
            return stack.enter_context(nc.psum_tensor(f"{name}_{what}", [P, 512], F32))

        def sem(what):
            return stack.enter_context(nc.semaphore(f"{name}_{what}"))

        wq_h, wq_l, wq_s = (sb(f"wq_{i}", [P, AH, CDIM], F32R) for i in "hls")
        wv_h, wv_l = (sb(f"wv_{i}", [CDIM, AH, APAD], F32R) for i in "hl")
        wo_a = sb("wo_a", [P, 2, HID], F32R)
        wo_b = sb("wo_b", [2 * HB, 2, HID], F32R)
        pick = sb("pick", [CDIM, SEQ], F32R)
        bo_row = raw["bo"]
        prepare_adapter(nc, const, raw, wq_h, wq_l, wq_s, wv_h, wv_l, wo_a, wo_b, pick)

        two = range(2)
        xr = sb("xr", [P, QT, 2, P], F32)
        x_h = [sb(f"x_h{j}", [P, 2, SEQ], F32R) for j in two]
        x_l = [sb(f"x_l{j}", [P, SEQ], F32R) for j in two]
        ctx_rows = [sb(f"ctx_rows{j}", [P, KT, CDIM], F32) for j in two]
        ctx_h = [sb(f"ctx_h{j}", [P, CTX], F32R) for j in two]
        ctx_l = [sb(f"ctx_l{j}", [CDIM, CTX], F32R) for j in two]
        v_h = [sb(f"v_h{j}", [P, KT, AH, AV], BF16) for j in two]
        v_l = [sb(f"v_l{j}", [P, KT, AH, AV], F16) for j in two]
        attn = [sb(f"attn{j}", [P, QT, HID], F32) for j in two]
        q_h = sb("q_h", [P, 4, 2, SEQ], F32R)
        q_l = sb("q_l", [CDIM, 4, 2, SEQ], F32R)
        maxima = sb("maxima", [P, 2, QT, P], F32)
        probs = sb("probs", [P, PR, 512], F32)
        probs_l = sb("probs_l", [P, PR, 512], F16)
        recip = sb("recip", [P, 4], F32)
        attn_th = sb("attn_th", [P, SEQ], F32R)
        attn_tl = sb("attn_tl", [P, SEQ], F32R)
        attn_tb = sb("attn_tb", [2 * HB, SEQ], F32R)

        shared = [bank(f"shared{i}") for i in range(Ring.BANKS)]
        max_bank = [bank(f"max{i}") for i in range(2)]
        score_bank = [bank(f"score{i}") for i in range(2)]
        pv_bank = bank("pv")

        rows_in = [sem(f"rows_in{i}") for i in two]
        consts = sem("consts")
        filled = sem("filled")
        emptied = sem("emptied")
        xr_ready = sem("xr_ready")
        x_hi = sem("x_hi")
        ctx_hi = sem("ctx_hi")
        v_hi = sem("v_hi")
        q_hi = sem("q_hi")
        max_filled = sem("max_filled")
        max_read = sem("max_read")
        scored = sem("scored")
        exped = sem("exped")
        probs_split = sem("probs_split")
        pv_done = sem("pv_done")
        recip_ready = sem("recip_ready")
        attn_ready = sem("attn_ready")
        attn_hi = sem("attn_hi")
        x_bo_ready = sem("x_bo_ready")
        part_ready = sem("part_ready")

        block = stack.enter_context(nc.Block())

        @block.sync
        def _(sp):
            def rows(b, j):
                sp.dma_start(ctx_rows[j][:, :, :],
                             ctx_dram[b, :, :].rearrange("(t p) c -> p t c", p=P)).then_inc(rows_in[j], 16)

            rows(0, 0)
            rows(1, 1)
            with sp.Fori(0, PERIODS - 1) as r:
                for j in two:
                    b = r * 2 + j
                    sp.wait_ge(ctx_hi, b + 1)
                    rows(b + 2, j)

        @block.gpsimd
        def _(pool):
            def slot(kind, s, period, cur, prev, nxt):
                if s in (0, 4) and prev is not None:
                    b = prev * 2 + s // 4
                    rows = x[:, bass.ds(b * QT, QT), :]
                    nc.gpsimd.tensor_tensor(rows, rows, bo_row[:, None, :].to_broadcast([P, QT, HID]), ALU.add).then_inc(x_bo_ready, 1)
                if (work := before(s, 3, cur, prev)) is not None:
                    r, v = work
                    for u in range(U):
                        n, rows = v * U + u, slice(0, KEY_ROWS[u])
                        pool.wait_ge(exped, r * UP + n + 1)
                        whole = probs[rows, n % PR, :]
                        nc.gpsimd.tensor_tensor(probs_l[rows, n % PR, :], whole, whole.bitcast(BF16)[:, 1::2],
                                                ALU.subtract).then_inc(probs_split, 1)

            nc.gpsimd.memset(maxima[:, :, :, :], 0.0)
            for j in two:
                nc.gpsimd.memset(v_h[j][:, :, :, AD:AV], 1.0)
                ins = nc.gpsimd.memset(v_l[j][:, :, :, AD:AV], 0.0)
            ins.then_inc(consts, 1)
            run(slot)(pool)

        @block.scalar
        def _(act):
            def extra(kind, period, key, batch):
                (b, j), (what, _, i) = batch, key
                if what == "out":
                    return
                act.wait_ge(filled, ring.number(kind, period, key) + 1)
                bank_ = shared[ring.bank(kind, key)]
                if what == "x":
                    nc.scalar.copy(x_h[j][:, :, :], bank_[:, :].rearrange("p (c q) -> p c q", c=2)).then_inc(x_hi, 1)
                elif what == "ctx":
                    nc.scalar.copy(ctx_h[j][0:CDIM, :], bank_[0:CDIM, :]).then_inc(ctx_hi, 1)
                elif what == "v":
                    t = i % 2 * 2
                    for c in range(2):
                        ins = nc.scalar.copy(v_h[j][:, t + c, :, 0:AD], bank_[:, c * SEQ:(c + 1) * SEQ].rearrange(
                            "p (h d) -> p h d", d=APAD)[:, :, 0:AD])
                    ins.then_inc(v_hi, 1)
                elif what == "ot":
                    nc.scalar.copy(attn_th[:, :], bank_[:, 0:SEQ])
                    nc.scalar.copy(attn_tb[0:HB, :], bank_[0:HB, SEQ:2 * SEQ]).then_inc(attn_hi, 1)

            def slot(kind, s, period, cur, prev, nxt):
                if cur is not None:
                    act.wait_ge(filled, ring.number(kind, period, ("proj", s)) + 1)
                    after(act, scored, cur * UP + (s - 3) * U)
                    nc.scalar.copy(q_h[0:CDIM, s % 4, :, :],
                                   shared[ring.bank(kind, ("proj", s))][0:CDIM, :].rearrange("p (h q) -> p h q", h=2)).then_inc(q_hi, 1)
                for step in range(U):
                    if (work := before(s, 3, cur, prev)) is not None:
                        r, v = work
                        n, rows = v * U + step, slice(0, KEY_ROWS[step])
                        act.wait_ge(scored, r * UP + n + 1)
                        after(act, pv_done, r * SLOTS + v - 1)
                        nc.scalar.activation(probs[rows, n % PR, :], score_bank[n % 2][rows, :], ACT.Exp,
                                             scale=SCALE).then_inc(exped, 1)
                    for at, key in extras(kind, s):
                        if at == step:
                            extra(kind, period, key, batch_of(key, cur, prev, nxt))

            extra("first", 0, ("ctx", "pre", 0), (0, 0))
            extra("first", 0, ("x", "pre", 0), (0, 0))
            run(slot)(act)

        @block.vector
        def _(dve):
            def lay_out(b):
                tiles = x[:, bass.ds(b * QT, QT), :]
                nc.vector.tensor_copy(xr[:, :, 0, :], tiles[:, :, 0:HA])
                for t in range(QT):
                    ins = nc.vector.tensor_copy(xr[:, t, 1, :].rearrange("p (r f) -> p r f", r=REP),
                                                x[:, b * QT + t, None, HA:HID].to_broadcast([P, REP, HB]))
                ins.then_inc(xr_ready, 1)

            def extra(kind, period, key, batch):
                (b, j), (what, _, i) = batch, key
                bank_ = shared[ring.bank(kind, key)]
                if what == "x":
                    dve.wait_ge(x_hi, b + 1)
                    nc.vector.tensor_tensor(x_l[j][:, :], bank_[:, 0:SEQ], x_h[j][:, 0, :], ALU.subtract)
                    for rows in (slice(HB, 2 * HB), slice(3 * HB, P)):
                        ins = nc.vector.tensor_tensor(x_h[j][rows, 1, :], bank_[rows, SEQ:2 * SEQ], x_h[j][rows, 1, :], ALU.subtract)
                    ins.then_inc(emptied, 1)
                elif what == "ctx":
                    dve.wait_ge(ctx_hi, b + 1)
                    nc.vector.tensor_tensor(ctx_l[j][:, :], bank_[0:CDIM, :], ctx_h[j][0:CDIM, :],
                                            ALU.subtract).then_inc(emptied, 1)
                elif what == "v":
                    t = i % 2 * 2
                    dve.wait_ge(v_hi, b * 2 + i % 2 + 1)
                    for c in range(2):
                        ins = nc.vector.tensor_tensor(v_l[j][:, t + c, :, 0:AD], bank_[:, c * SEQ:(c + 1) * SEQ].rearrange(
                            "p (h d) -> p h d", d=APAD)[:, :, 0:AD], v_h[j][:, t + c, :, 0:AD], ALU.subtract)
                    ins.then_inc(emptied, 1)
                elif what == "ot":
                    dve.wait_ge(attn_hi, b + 1)
                    nc.vector.tensor_tensor(attn_tl[:, :], bank_[:, 0:SEQ], attn_th[:, :], ALU.subtract)
                    nc.vector.tensor_tensor(attn_tb[HB:2 * HB, :], bank_[0:HB, SEQ:2 * SEQ], attn_tb[0:HB, :],
                                            ALU.subtract).then_inc(emptied, 1)
                elif what == "out":
                    t = i % 2
                    dve.wait_ge(x_bo_ready, b + 1)
                    dve.wait_ge(filled, ring.number(kind, period, key) + 1)
                    row = x[:, b * QT + t, :]
                    nc.vector.tensor_tensor(row, bank_[:, 0:HID], row, ALU.add).then_inc(part_ready, 1)
                    dve.wait_ge(part_ready, b * QT + t + 1)
                    nc.vector.tensor_tensor(row, bank_[:, HID:2 * HID], row, ALU.add).then_inc(emptied, 1)

            def slot(kind, s, period, cur, prev, nxt):
                if cur is not None:
                    dve.wait_ge(q_hi, cur * SLOTS + s + 1)
                    nc.vector.tensor_tensor(q_l[:, s % 4, :, :],
                                            shared[ring.bank(kind, ("proj", s))][0:CDIM, :].rearrange("p (h q) -> p h q", h=2),
                                            q_h[0:CDIM, s % 4, :, :], ALU.subtract).then_inc(emptied, 1)
                if (work := before(s, 2, cur, prev)) is not None:
                    bank_, rows = shared[ring.bank(kind, ("mt", s))], slice(CDIM, P)
                    dve.wait_ge(filled, ring.number(kind, period, ("mt", s)) + 1)
                    nc.vector.tensor_tensor(q_h[rows, work[1] % 4, :, :], bank_[rows, None, 0:SEQ].to_broadcast([P - CDIM, 2, SEQ]),
                                            const["neg_eye"][rows, 0:2, None].to_broadcast([P - CDIM, 2, SEQ]),
                                            ALU.mult).then_inc(emptied, 1)
                for step in range(U):
                    if (work := before(s, 1, cur, prev)) is not None:
                        r, v = work
                        n = v * U + step
                        at = CDIM + step // 2
                        dve.wait_ge(max_filled, r * UP + n + 1)
                        nc.vector.reduce_max(maxima[:, v % 2, step % 2, at:at + 1], max_bank[n % 2][:, 0:KEYS],
                                             AX.X).then_inc(max_read, 1)
                    for at, key in extras(kind, s):
                        if at == step:
                            extra(kind, period, key, batch_of(key, cur, prev, nxt))
                if s == 1 and cur is not None:
                    lay_out(cur * 2 + 1)
                if s == 4 and nxt is not None:
                    lay_out(nxt * 2)
                if (work := before(s, 4, cur, prev)) is not None:
                    r, v = work
                    dve.wait_ge(pv_done, r * SLOTS + v + 1)
                    groups = pv_bank[:, 0:4 * AV]
                    nc.vector.reciprocal(recip[:, :], groups.rearrange("p (g d) -> p g d", d=AV)[:, :, AD]).then_inc(recip_ready, 1)
                    dve.wait_ge(recip_ready, r * SLOTS + v + 1)
                    head = v % APAIRS * 2
                    out = attn[v // APAIRS][:, :, head * AD:(head + 2) * AD].rearrange("p t (h d) -> p h t d", h=2)
                    nc.vector.tensor_tensor(out, groups.rearrange("p (h t d) -> p h t d", h=2, t=QT)[:, :, :, 0:AD],
                                            recip[:, :].rearrange("p (h t) -> p h t", h=2)[:, :, :, None].to_broadcast([P, 2, QT, AD]),
                                            ALU.mult).then_inc(attn_ready, 1)

            lay_out(0)
            for j in two:
                ins = nc.vector.memset(ctx_h[j][CDIM:P, :].bitcast(F32), 1.0)
            ins.then_inc(consts, 1)
            extra("first", 0, ("ctx", "pre", 0), (0, 0))
            extra("first", 0, ("x", "pre", 0), (0, 0))
            dve.wait_ge(consts, 2)
            run(slot)(dve)

        @block.tensor
        def _(pe):
            ident = const["ident"]
            def claim(kind, period, key):
                after(pe, emptied, ring.free(kind, period, key)[0])
                return shared[ring.bank(kind, key)]

            def extra(kind, period, key, batch):
                (b, j), (what, _, i) = batch, key
                if what == "x":
                    pe.wait_ge(xr_ready, b + 1)
                    bank_ = claim(kind, period, key)
                    for c in range(2):
                        for t in range(QT):
                            mm = nc.tensor.transpose(bank_[:, c * SEQ + t * P:c * SEQ + (t + 1) * P], xr[:, t, c, :], ident)
                elif what == "ctx":
                    pe.wait_ge(rows_in[j], (b - j) * 8 + 16)
                    bank_ = claim(kind, period, key)
                    for t in range(KT):
                        mm = nc.tensor.transpose(bank_[0:CDIM, t * P:(t + 1) * P], ctx_rows[j][:, t, :], ident)
                elif what == "v":
                    pe.wait_ge(emptied, context_number(kind, period, j) + 1)
                    bank_ = claim(kind, period, key)
                    for c in range(2):
                        t = i % 2 * 2 + c
                        tok, out = slice(t * P, (t + 1) * P), bank_[:, c * SEQ:(c + 1) * SEQ]
                        high, low = (w[:, :, :].rearrange("p h d -> p (h d)") for w in (wv_h, wv_l))
                        nc.tensor.matmul(out, ctx_h[j][0:CDIM, tok], high, start=True, stop=False)
                        nc.tensor.matmul(out, ctx_l[j][:, tok], high, start=False, stop=False)
                        mm = nc.tensor.matmul(out, ctx_h[j][0:CDIM, tok], low, start=False, stop=True)
                elif what == "ot":
                    pe.wait_ge(attn_ready, b * APAIRS + APAIRS)
                    bank_ = claim(kind, period, key)
                    for t in range(QT):
                        nc.tensor.transpose(bank_[:, t * P:(t + 1) * P], attn[j][:, t, 0:HA], ident)
                        mm = nc.tensor.transpose(bank_[0:HB, SEQ + t * P:SEQ + (t + 1) * P], attn[j][:, t, HA:HID], ident)
                elif what == "out":
                    bank_ = claim(kind, period, key)
                    pe.wait_ge(emptied, ring.number(kind, period, ("ot", "prev", j)) + 1)
                    cols, out = slice(i % 2 * P, (i % 2 + 1) * P), bank_[:, 0:2 * HID]
                    for n, (lhs, rhs) in enumerate(((attn_th, wo_a), (attn_tl, wo_a), (attn_tb, wo_b))):
                        nc.tensor.matmul(out, lhs[:, cols], rhs[:, :, :].rearrange("p a n -> p (a n)"), start=n == 0, stop=False)
                    mm = nc.tensor.matmul(out, pick[:, cols], branch[:, b, :, :].rearrange("p a n -> p (a n)"), start=False, stop=True)
                mm.then_inc(filled, 1)

            def project(kind, s, period):
                j = s // APAIRS
                if s % APAIRS == 0:
                    if j == 1:
                        number = ring.number(kind, period, ("x", "cur", 1))
                    else:
                        number = ring.number("first", 0, ("x", "pre", 0)) if kind == "first" else earlier(kind, period, ("x", "nxt", 0))
                    pe.wait_ge(emptied, number + 1)
                bank_ = claim(kind, period, ("proj", s))
                for c in range(2):
                    head = s % APAIRS * 2 + c
                    out = bank_[0:CDIM, c * SEQ:(c + 1) * SEQ]
                    nc.tensor.matmul(out, wq_h[:, head, :], x_h[j][:, 0, :], start=True, stop=False)
                    nc.tensor.matmul(out, wq_h[:, head, :], x_l[j][:, :], start=False, stop=False)
                    nc.tensor.matmul(out, wq_l[:, head, :], x_h[j][:, 0, :], start=False, stop=False)
                    mm = nc.tensor.matmul(out, wq_s[:, head, :], x_h[j][:, 1, :], start=False, stop=True)
                mm.then_inc(filled, 1)

            def find_max(kind, s, step, period, work):
                r, v = work
                n, j, t = v * U + step, v // APAIRS, step % 2
                pe.wait_ge(emptied, unit_of(kind, s, period, "proj", 1) + 1)
                after(pe, max_read, r * UP + n - 1)
                nc.tensor.matmul(max_bank[n % 2][:, 0:KEYS], q_h[0:CDIM, v % 4, step // 2, t * P:(t + 1) * P],
                                 ctx_h[j][0:CDIM, 0:KEYS], start=True, stop=True).then_inc(max_filled, 1)

            def score(kind, s, step, period, work):
                r, v = work
                n, j = v * U + step, v // APAIRS
                if step == 0:
                    pe.wait_ge(emptied, unit_of(kind, s, period, "mt", 1) + 1)
                after(pe, exped, r * UP + n - 1)
                out = score_bank[n % 2][0:KEY_ROWS[step], :]
                keys = slice(step * P, step * P + KEY_ROWS[step])
                nc.tensor.matmul(out, ctx_h[j][:, keys], q_h[:, v % 4, :, :], start=True, stop=False)
                nc.tensor.matmul(out, ctx_h[j][0:CDIM, keys], q_l[:, v % 4, :, :], start=False, stop=False)
                nc.tensor.matmul(out, ctx_l[j][:, keys], q_h[0:CDIM, v % 4, :, :], start=False, stop=True).then_inc(scored, 1)

            def weigh(kind, s, group, period, work):
                r, v = work
                j = v // APAIRS
                if group == 0:
                    pe.wait_ge(probs_split, r * UP + (v + 1) * U)
                    after(pe, attn_ready, r * SLOTS + v)
                    if v % APAIRS == 0:
                        number = earlier(kind, period, ("v", "cur", 3)) if j else ring.number(kind, period, ("v", "cur", 1))
                        pe.wait_ge(emptied, number + 1)
                head, col = v % APAIRS * 2 + group // QT, group * P
                out = pv_bank[:, group * AV:(group + 1) * AV]
                n = 0
                for c in range(KT):
                    rows, unit = slice(0, KEY_ROWS[c]), (v * U + c) % PR
                    hi = probs[rows, unit, :].bitcast(BF16)[:, 1::2][:, col:col + P]
                    lo = probs_l[rows, unit, col:col + P]
                    for lhs, rhs in ((hi, v_h), (hi, v_l), (lo, v_h)):
                        mm = nc.tensor.matmul(out, lhs, rhs[j][rows, c, head, :], start=n == 0, stop=n == 3 * KT - 1)
                        n += 1
                if group == 3:
                    mm.then_inc(pv_done, 1)

            def slot(kind, s, period, cur, prev, nxt):
                if cur is not None:
                    project(kind, s, period)
                if (work := before(s, 2, cur, prev)) is not None:
                    r, v = work
                    bank_ = claim(kind, period, ("mt", s))
                    pe.wait_ge(max_read, r * UP + (v + 1) * U)
                    for t in range(QT):
                        mm = nc.tensor.transpose(bank_[:, t * P:(t + 1) * P], maxima[:, v % 2, t, :], ident)
                    mm.then_inc(filled, 1)
                for step in range(U):
                    if (work := before(s, 1, cur, prev)) is not None:
                        find_max(kind, s, step, period, work)
                    if (work := before(s, 3, cur, prev)) is not None:
                        score(kind, s, step, period, work)
                    if (work := before(s, 4, cur, prev)) is not None:
                        weigh(kind, s, step, period, work)
                    for at, key in extras(kind, s):
                        if at == step:
                            extra(kind, period, key, batch_of(key, cur, prev, nxt))

            extra("first", 0, ("ctx", "pre", 0), (0, 0))
            extra("first", 0, ("x", "pre", 0), (0, 0))
            pe.wait_ge(consts, 2)
            run(slot)(pe)


def build(nc, columns, shapes, a, out):
    l0 = {n[len("L0_xattn_"):]: v for n, v in a.items() if n.startswith("L0_xattn_")}
    l1 = {n[len("L1_xattn_"):]: v for n, v in a.items() if n.startswith("L1_xattn_")}
    context = a["ctx_768"]
    stack = ExitStack()
    with stack:
        x = stack.enter_context(nc.sbuf_tensor("x_rows", [P, NT, HID], F32))
        ident = stack.enter_context(nc.sbuf_tensor("ident", [P, P], F32))
        with ExitStack() as self_stack:
            self_weights = SelfWeights(nc, self_stack, {w.rstrip("1"): l1[w] for w in ("g1", "be1", "wq1", "wk1", "wv1", "wo1", "bo1")})
            with ExitStack() as adapter_stack:
                def sb(what, shape, dt=F32):
                    return adapter_stack.enter_context(nc.sbuf_tensor(what, shape, dt))

                consts = sb("shape_consts", list(shapes))
                const = {what: consts[:, at:at + width] for what, (at, width) in columns.items()}
                branch = sb("branch", [CDIM, NB, 2, HID], F32R)
                raw = {"wq": sb("raw_wq", [P, 2, HID]), "wk": sb("raw_wk", [CDIM, HID]), "wv": sb("raw_wv", [CDIM, HID]),
                       "wo": sb("raw_wo", [P, 2, HID]), "bo": sb("raw_bo", [P, HID]),
                       "loaded": adapter_stack.enter_context(nc.semaphore("raw_loaded"))}

                def load_constants(engine, semaphore):
                    at, width = columns["ident"]
                    engine.dma_start(consts[:, :], a["shapes"]).then_inc(semaphore, 16)
                    engine.dma_start(ident[:, :], a["shapes"][:, at:at + width]).then_inc(semaphore, 16)

                def load_raw(engine):
                    for out, w in ((raw["wq"][:, 0, :], l0["Wq"][0:HA, :]), (raw["wq"][0:HB, 1, :], l0["Wq"][HA:HID, :]),
                                   (raw["wk"][:, :], l0["Wk"]), (raw["wv"][:, :], l0["Wv"]), (raw["wo"][:, 0, :], l0["Wout"][0:HA, :]),
                                   (raw["wo"][0:2 * HB, 1, :], l0["Wout"][HA:HID, :][None, :, :].to_broadcast([2, HB, HID])),
                                   (raw["bo"][:, :], l0["b_out"].rearrange("(a n) -> a n", a=1).to_broadcast([P, HID]))):
                        engine.dma_start(out, w).then_inc(raw["loaded"], 16)

                adapter_queries(nc, x, a["x"], const, load_constants, context, l0["Wq_ca"], l0["Wk_ca"], l0["Wv_ca"],
                                raw, load_raw, self_weights, branch)
                adapter(nc, x, const, context, raw, branch)
            far_stack = stack.enter_context(ExitStack())
            cross_raw = CrossRaw(nc, far_stack, [l1[w] for w in ("wq2", "wk2", "wv2", "wo2")])
            attention(nc, "self", False, x, ident, context, self_weights, lambda: cross_raw.load)
        last_stack = stack.enter_context(ExitStack())
        ahead = []

        def feed_forward_loads():
            far_stack.close()
            ahead.append(FeedForwardRaw(nc, last_stack, [l1["w_ff1"], l1["w_ff2"]]))
            return ahead[0].load

        attention(nc, "cross", True, x, ident, context, ([l1[w] for w in ("g2", "be2", "bo2")] + [cross_raw]), feed_forward_loads)
        feed_forward(nc, x, ident, l1["g3"], l1["be3"], l1["b_ff1"], l1["b_ff2"], ahead[0], out)


def kernel(**inputs):
    import concourse.bacc as bacc
    from concourse.bass_utils import run_bass_kernel_spmd

    nc = bacc.Bacc("TRN2", target_bir_lowering=False, num_devices=1)
    arrays = {name: np.ascontiguousarray(v) for name, v in inputs.items()}
    arrays["shapes"], columns = shape_constants()
    drams = {name: nc.dram_tensor(f"in_{name}", v.shape, mybir.dt.from_np(v.dtype), kind="ExternalInput").ap()
             for name, v in arrays.items()}
    out = nc.dram_tensor("out", (NB, SEQ, HID), F32, kind="ExternalOutput").ap()
    build(nc, columns, arrays["shapes"].shape, drams, out)
    result = run_bass_kernel_spmd(nc, [{f"in_{name}": v for name, v in arrays.items()}], core_ids=[0])
    return result.results[0]["out"]
```
